# Optimizing a Trainium2 kernel written in Bass

```python
import numpy as np
import jax
import jax.numpy as jnp

def _softmax(x, axis=-1):
    return jax.nn.softmax(x, axis=axis)

def _gelu(x):
    return jax.nn.gelu(x, approximate=True)

def _silu(x):
    return jax.nn.silu(x)

def _sigmoid(x):
    return jax.nn.sigmoid(x)

def _layernorm(x, axis=-1, eps=1e-05):
    m = jnp.mean(x, axis=axis, keepdims=True)
    v = jnp.var(x, axis=axis, keepdims=True)
    return (x - m) / jnp.sqrt(v + eps)

def _scatter_add(tgt, idx, src, axis=0):
    return tgt.at[idx].add(src)

def _segment_sum(src, seg, n):
    return jax.ops.segment_sum(src, seg, n)
kernel_name = 'mk_adj_resnorm_d4_adj_r2_248b52'

def setup_inputs(seed: int=0):
    np.random.seed(seed)
    _w = jnp.asarray

    def _rec_inputs():
        import jax
        import jax.numpy as jnp
        _gk = jax.random.key(seed)
        x = -0.000125 + 0.9999 * jax.random.normal(jax.random.fold_in(_gk, 1), (64, 128, 128), jnp.float32)
        _a = jax.random.bernoulli(jax.random.fold_in(_gk, 2), 0.03125, (128, 128))
        _a = jnp.logical_or(_a, jnp.swapaxes(_a, -1, -2))
        _a = jnp.logical_or(_a, jnp.eye(128, dtype=bool))
        _af = _a.astype(jnp.float32)
        _af = _af * jax.random.uniform(jax.random.fold_in(_gk, 3), (128, 128), jnp.float32, 0.05, 0.000488281)
        adj = _af
        return (x, adj)
    x, adj = _rec_inputs()

    def _L0_gnn_setup():
        import jax, jax.numpy as jnp
        import numpy as np
        B, T, D, H = (64, 1024, 128, 128)
        MAX_SKIP = 4

        def _lstm_last(Wih, Whh, bih, bhh, xs):
            N, _, Hd = xs.shape
            bias = bih + bhh

            def step(carry, x_t):
                h, c = carry
                g = x_t @ Wih.T + h @ Whh.T + bias
                i, f, gg, o = jnp.split(g, 4, axis=-1)
                c = jax.nn.sigmoid(f) * c + jax.nn.sigmoid(i) * jnp.tanh(gg)
                h = jax.nn.sigmoid(o) * jnp.tanh(c)
                return ((h, c), None)
            init = (jnp.zeros((N, Hd), xs.dtype), jnp.zeros((N, Hd), xs.dtype))
            (h_last, _), _ = jax.lax.scan(step, init, jnp.swapaxes(xs, 0, 1))
            return h_last
        key = jax.random.key(seed)
        ks = jax.random.split(key, 8)
        s = 0.05
        x = jax.random.normal(ks[0], (B, T, D), jnp.float32)
        adj = jax.random.uniform(ks[1], (T, T), jnp.float32) / T
        Wg0 = jax.random.normal(ks[2], (D, H), jnp.float32) * s
        bg0 = jnp.zeros((H,), jnp.float32)
        Wg1 = jax.random.normal(ks[3], (H, H), jnp.float32) * s
        bg1 = jnp.zeros((H,), jnp.float32)
        Wih = jax.random.normal(ks[4], (MAX_SKIP, 4 * H, H), jnp.float32) * s
        Whh = jax.random.normal(ks[5], (MAX_SKIP, 4 * H, H), jnp.float32) * s
        bih = jax.random.normal(ks[6], (MAX_SKIP, 4 * H), jnp.float32) * s
        bhh = jax.random.normal(ks[7], (MAX_SKIP, 4 * H), jnp.float32) * s
        return dict(x=x, adj=adj, Wg0=Wg0, bg0=bg0, Wg1=Wg1, bg1=bg1, Wih=Wih, Whh=Whh, bih=bih, bhh=bhh)
    _L0_gnn_all = _L0_gnn_setup()
    _L0_gnn_in = {k: v for k, v in _L0_gnn_all.items() if k in ('Wg0', 'bg0', 'Wg1', 'bg1', 'Wih', 'Whh', 'bih', 'bhh')}
    del _L0_gnn_all

    def _L1_gnn_setup():
        import jax, jax.numpy as jnp
        import numpy as np
        EPS = 1e-05

        def _batchnorm(x, gamma, beta):
            mu = jnp.mean(x, axis=0)
            var = jnp.var(x, axis=0)
            return (x - mu) * jax.lax.rsqrt(var + EPS) * gamma + beta
        key = jax.random.key(seed)
        ks = jax.random.split(key, 4)
        b, n, d, h, o = (32, 1024, 128, 256, 128)
        features = jax.random.normal(ks[0], (b, n, d), dtype=jnp.float32)
        A = jax.random.uniform(ks[1], (n, n), dtype=jnp.float32)
        lim1 = float(np.sqrt(6.0 / (d + h)))
        W1 = jax.random.uniform(ks[2], (h, d), minval=-lim1, maxval=lim1, dtype=jnp.float32)
        b1 = jnp.zeros((h,), jnp.float32)
        lim2 = float(np.sqrt(6.0 / (h + o)))
        W2 = jax.random.uniform(ks[3], (o, h), minval=-lim2, maxval=lim2, dtype=jnp.float32)
        b2 = jnp.zeros((o,), jnp.float32)
        g1 = jnp.ones((h,), jnp.float32)
        be1 = jnp.zeros((h,), jnp.float32)
        g2 = jnp.ones((o,), jnp.float32)
        be2 = jnp.zeros((o,), jnp.float32)
        return {'features': features, 'A': A, 'W1': W1, 'b1': b1, 'g1': g1, 'be1': be1, 'W2': W2, 'b2': b2, 'g2': g2, 'be2': be2}
    _L1_gnn_all = _L1_gnn_setup()
    _L1_gnn_in = {k: v for k, v in _L1_gnn_all.items() if k in ('W1', 'b1', 'g1', 'be1', 'W2', 'b2', 'g2', 'be2')}
    del _L1_gnn_all

    def _L2_gnn_setup():
        import jax, jax.numpy as jnp
        import numpy as np
        BT, N, D, HEADS, E = (512, 64, 128, 4, 256)
        LRELU_SLOPE = 0.2
        EPS = 1e-08
        key = jax.random.key(seed)
        ks = jax.random.split(key, 8)
        d = D
        return {'H': jax.random.normal(ks[0], (BT, N, d), jnp.float32), 'W_lin': jax.random.normal(ks[1], (d, d), jnp.float32) / np.sqrt(d).astype(np.float32), 'W_val': jax.random.normal(ks[2], (d, d), jnp.float32) / np.sqrt(d).astype(np.float32), 'a': jax.random.normal(ks[3], (HEADS, d // HEADS), jnp.float32), 'W_out': jax.random.normal(ks[4], (d, d), jnp.float32) / np.sqrt(d).astype(np.float32), 'A0': jax.random.uniform(ks[5], (N, N), jnp.float32), 'src': jax.random.randint(ks[6], (E,), 0, N, jnp.int32), 'dst': jax.random.randint(ks[7], (E,), 0, N, jnp.int32)}
    _L2_gnn_all = _L2_gnn_setup()
    _L2_gnn_in = {k: v for k, v in _L2_gnn_all.items() if k in ('W_lin', 'W_val', 'a', 'W_out', 'src', 'dst')}
    del _L2_gnn_all

    def _L3_gnn_setup():
        import jax, jax.numpy as jnp
        import numpy as np
        N = 2048
        NFEAT, NHID, NCLASS = (128, 256, 128)
        B = 4

        def _slconv(x, adj, S, W):
            support = jnp.einsum('bnf,fh->bnh', x, W)
            weighting = adj * S
            return jnp.einsum('nm,bmh->bnh', weighting, support)
        key = jax.random.key(seed)
        ks = jax.random.split(key, 6)
        x = jax.random.normal(ks[0], (B, N, NFEAT), dtype=jnp.float32)
        adj = jax.random.uniform(ks[1], (N, N), dtype=jnp.float32)
        S = jnp.ones((N, N), dtype=jnp.float32)
        W1 = jax.random.normal(ks[2], (NFEAT, NHID), dtype=jnp.float32) / np.sqrt(NFEAT)
        W2 = jax.random.normal(ks[3], (NHID, 2 * NHID), dtype=jnp.float32) / np.sqrt(NHID)
        W3 = jax.random.normal(ks[4], (2 * NHID, NCLASS), dtype=jnp.float32) / np.sqrt(2 * NHID)
        return {'x': x, 'adj': adj, 'S': S, 'W1': W1, 'W2': W2, 'W3': W3}
    _L3_gnn_all = _L3_gnn_setup()
    _L3_gnn_in = {k: v for k, v in _L3_gnn_all.items() if k in ('W1', 'W2', 'W3')}
    del _L3_gnn_all
    return {'x': x, 'adj': adj, 'L0_gnn_Wg0': _L0_gnn_in['Wg0'], 'L0_gnn_bg0': _L0_gnn_in['bg0'], 'L0_gnn_Wg1': _L0_gnn_in['Wg1'], 'L0_gnn_bg1': _L0_gnn_in['bg1'], 'L0_gnn_Wih': _L0_gnn_in['Wih'], 'L0_gnn_Whh': _L0_gnn_in['Whh'], 'L0_gnn_bih': _L0_gnn_in['bih'], 'L0_gnn_bhh': _L0_gnn_in['bhh'], 'L1_gnn_W1': _L1_gnn_in['W1'], 'L1_gnn_b1': _L1_gnn_in['b1'], 'L1_gnn_g1': _L1_gnn_in['g1'], 'L1_gnn_be1': _L1_gnn_in['be1'], 'L1_gnn_W2': _L1_gnn_in['W2'], 'L1_gnn_b2': _L1_gnn_in['b2'], 'L1_gnn_g2': _L1_gnn_in['g2'], 'L1_gnn_be2': _L1_gnn_in['be2'], 'L2_gnn_W_lin': _L2_gnn_in['W_lin'], 'L2_gnn_W_val': _L2_gnn_in['W_val'], 'L2_gnn_a': _L2_gnn_in['a'], 'L2_gnn_W_out': _L2_gnn_in['W_out'], 'L2_gnn_src': _L2_gnn_in['src'], 'L2_gnn_dst': _L2_gnn_in['dst'], 'L3_gnn_W1': _L3_gnn_in['W1'], 'L3_gnn_W2': _L3_gnn_in['W2'], 'L3_gnn_W3': _L3_gnn_in['W3']}

def reference(x, adj, L0_gnn_Wg0, L0_gnn_bg0, L0_gnn_Wg1, L0_gnn_bg1, L0_gnn_Wih, L0_gnn_Whh, L0_gnn_bih, L0_gnn_bhh, L1_gnn_W1, L1_gnn_b1, L1_gnn_g1, L1_gnn_be1, L1_gnn_W2, L1_gnn_b2, L1_gnn_g2, L1_gnn_be2, L2_gnn_W_lin, L2_gnn_W_val, L2_gnn_a, L2_gnn_W_out, L2_gnn_src, L2_gnn_dst, L3_gnn_W1, L3_gnn_W2, L3_gnn_W3):
    import jax
    import jax.numpy as jnp

    def _L0_gnn_ref(x, adj, Wg0, bg0, Wg1, bg1, Wih, Whh, bih, bhh):
        import jax, jax.numpy as jnp
        import numpy as np
        B, T, D, H = (64, 1024, 128, 128)
        MAX_SKIP = 4

        def _lstm_last(Wih, Whh, bih, bhh, xs):
            N, _, Hd = xs.shape
            bias = bih + bhh

            def step(carry, x_t):
                h, c = carry
                g = x_t @ Wih.T + h @ Whh.T + bias
                i, f, gg, o = jnp.split(g, 4, axis=-1)
                c = jax.nn.sigmoid(f) * c + jax.nn.sigmoid(i) * jnp.tanh(gg)
                h = jax.nn.sigmoid(o) * jnp.tanh(c)
                return ((h, c), None)
            init = (jnp.zeros((N, Hd), xs.dtype), jnp.zeros((N, Hd), xs.dtype))
            (h_last, _), _ = jax.lax.scan(step, init, jnp.swapaxes(xs, 0, 1))
            return h_last
        h = jax.nn.relu(jnp.einsum('ts,bsh->bth', adj, x @ Wg0 + bg0))
        h = jax.nn.relu(jnp.einsum('ts,bsh->bth', adj, h @ Wg1 + bg1))
        Bv, Tv, Hd = h.shape
        for p in range(1, MAX_SKIP + 1):
            nw = Tv // p
            wins = h[:, :nw * p, :].reshape(Bv * nw, p, Hd)
            last = _lstm_last(Wih[p - 1], Whh[p - 1], bih[p - 1], bhh[p - 1], wins)
            idx = jnp.arange(nw) * p + (p - 1)
            h = h.at[:, idx, :].set(last.reshape(Bv, nw, Hd))
        return h

    def _L1_gnn_ref(features, A, W1, b1, g1, be1, W2, b2, g2, be2):
        import jax, jax.numpy as jnp
        import numpy as np
        EPS = 1e-05

        def _batchnorm(x, gamma, beta):
            mu = jnp.mean(x, axis=0)
            var = jnp.var(x, axis=0)
            return (x - mu) * jax.lax.rsqrt(var + EPS) * gamma + beta
        b, n, d = features.shape
        A_norm = A + jnp.eye(n, dtype=A.dtype)
        deg = jnp.sum(A_norm, axis=0) + jnp.sum(A_norm, axis=1) - jnp.diagonal(A_norm)
        dinv = jax.lax.rsqrt(deg)
        A_hat = A_norm * dinv[:, None] * dinv[None, :]
        agg = jnp.einsum('nm,bmd->bnd', A_hat, features)
        x = agg.reshape(-1, d)
        h = jax.nn.relu(_batchnorm(x @ W1.T + b1, g1, be1))
        out = h @ W2.T + b2
        out = _batchnorm(out, g2, be2)
        return out.reshape(b, n, -1)

    def _L2_gnn_ref(H, W_lin, W_val, a, W_out, A0, src, dst):
        import jax, jax.numpy as jnp
        import numpy as np
        BT, N, D, HEADS, E = (512, 64, 128, 4, 256)
        LRELU_SLOPE = 0.2
        EPS = 1e-08
        bt, n, d = H.shape
        h, dh = a.shape
        Xq = (H @ W_lin.T).reshape(bt, n, h, dh)
        Xv = (H @ W_val.T).reshape(bt, n, h, dh)
        Qs = Xq[:, src]
        Kt = Xq[:, dst]
        e = jnp.einsum('behd,hd->beh', jax.nn.leaky_relu(Qs + Kt, LRELU_SLOPE), a)
        e = e + jnp.log(A0[src, dst] + EPS)[None, :, None]
        e_t = e.transpose(1, 0, 2)
        m = jax.ops.segment_max(e_t, src, num_segments=n)
        ex = jnp.exp(e_t - m[src])
        denom = jax.ops.segment_sum(ex, src, num_segments=n)
        attn = ex / denom[src]
        Vt = Xv[:, dst].transpose(1, 0, 2, 3)
        Y = jax.ops.segment_sum(attn[..., None] * Vt, src, num_segments=n)
        Y = Y.transpose(1, 0, 2, 3).reshape(bt, n, d)
        return Y @ W_out.T

    def _L3_gnn_ref(x, adj, S, W1, W2, W3):
        import jax, jax.numpy as jnp
        import numpy as np
        N = 2048
        NFEAT, NHID, NCLASS = (128, 256, 128)
        B = 4

        def _slconv(x, adj, S, W):
            support = jnp.einsum('bnf,fh->bnh', x, W)
            weighting = adj * S
            return jnp.einsum('nm,bmh->bnh', weighting, support)
        h = jax.nn.relu(_slconv(x, adj, S, W1))
        h = jax.nn.relu(_slconv(h, adj, S, W2))
        return _slconv(h, adj, S, W3)
    x = _layernorm(x + _L0_gnn_ref(x, adj, L0_gnn_Wg0, L0_gnn_bg0, L0_gnn_Wg1, L0_gnn_bg1, L0_gnn_Wih, L0_gnn_Whh, L0_gnn_bih, L0_gnn_bhh), axis=-1)
    x = _layernorm(x + _L1_gnn_ref(x, adj, L1_gnn_W1, L1_gnn_b1, L1_gnn_g1, L1_gnn_be1, L1_gnn_W2, L1_gnn_b2, L1_gnn_g2, L1_gnn_be2), axis=-1)
    x = _layernorm(x + _L2_gnn_ref(x, L2_gnn_W_lin, L2_gnn_W_val, L2_gnn_a, L2_gnn_W_out, adj, L2_gnn_src, L2_gnn_dst), axis=-1)
    x = _layernorm(x + _L3_gnn_ref(x, adj, adj, L3_gnn_W1, L3_gnn_W2, L3_gnn_W3), axis=-1)
    return x

_drawn_inputs = setup_inputs


def setup_inputs(seed=0):
    import zlib

    import numpy as np

    out = dict(_drawn_inputs(seed))
    spreads = {'L0_gnn_bg0': (0.0, 0.8),
     'L0_gnn_bg1': (0.0, 0.8),
     'L1_gnn_b1': (0.0, 2.0),
     'L1_gnn_g1': (1.0, 0.2),
     'L1_gnn_be1': (0.0, 0.1),
     'L1_gnn_b2': (0.0, 2.0),
     'L1_gnn_g2': (1.0, 0.2),
     'L1_gnn_be2': (0.0, 0.1)}
    factors = {'L0_gnn_Wg0': 8.0,
     'L0_gnn_Wg1': 8.0,
     'L0_gnn_Wih': 8.0,
     'L0_gnn_Whh': 8.0,
     'L3_gnn_W1': 64.0,
     'L3_gnn_W2': 64.0,
     'L3_gnn_W3': 64.0}
    for name, (base, spread) in spreads.items():
        noise = np.random.default_rng([zlib.crc32(name.encode()), seed]).standard_normal(out[name].shape)
        drawn = base * np.exp(spread * noise) if base else spread * noise
        out[name] = jnp.asarray(drawn.astype(out[name].dtype))
    for name, factor in factors.items():
        out[name] = (out[name] * factor).astype(out[name].dtype)
    return out
```

```python
from contextlib import ExitStack

import concourse.bass as bass
from concourse import mybir

F32 = mybir.dt.float32
F32R = mybir.dt.float32r
I32 = mybir.dt.int32
ALU = mybir.AluOpType
ACT = mybir.ActivationFunctionType

B, T, D = 64, 128, 128
GB = 4
GN = GB * T
TURNS = B // GB // 2
SKIPS = 4
E = 256
ET = E // 128
HEADS = 4
HD = D // HEADS
SLOPE = 0.2
EPS_NORM = 1e-5
EPS_LOG = 1e-8
NEG = -3.0e38
HI, LO = 0, 1

GNN = dict(adjT=(0, 128), Wg0=(128, 256), Wg1=(256, 384))
GNN_COLS = 384
LSTM_COLS = SKIPS * 2 * 4 * D
LATE = dict(L1W1=(0, 256), L1W2=(256, 512), QV=(512, 768), WOUT=(768, 896), L3W1=(896, 1152),
            L3W2=(1152, 2176), L3W3=(2176, 2688))
LATE_COLS = 2688
V_BIH, V_BHH, V_B1, V_G1, V_BE1, V_B2, V_G2, V_BE2, V_A = 0, 16, 32, 34, 36, 38, 39, 40, 41
VEC_COLS = 42


def f32(ap):
    return ap.bitcast(F32)


class Chain:

    def __init__(self, eng, sem):
        self.eng, self.sem, self.n = eng, sem, 0

    def __call__(self, ins):
        self.n += 1
        ins.then_inc(self.sem, 1)
        self.eng.wait_ge(self.sem, self.n)


def hold(pool, sem, value, passed):
    pool.wait_ge(sem, value)
    pool.sem_inc(passed, 1)


def mm3(nc, out, wh, wl, xh, xl, start, stop):
    nc.tensor.matmul(out, wh, xh, start=start, stop=False)
    nc.tensor.matmul(out, wh, xl, start=False, stop=False)
    return nc.tensor.matmul(out, wl, xh, start=False, stop=stop)


def take_hi(nc, out, psum, func=ACT.Copy):
    return nc.scalar.activation(out, psum, func)


def take_lo(nc, out, psum, hi, relu=False):
    if relu:
        return nc.vector.scalar_tensor_tensor(out=out, in0=psum, scalar=0.0, in1=f32(hi), op0=ALU.max, op1=ALU.subtract)
    return nc.vector.tensor_tensor(out, psum, f32(hi), ALU.subtract)


class Mem:
    pass


def build(nc, x, adj, gnn_w, lstm_w, late_w, vecs, bg0, bg1, src, dst, out):
    with ExitStack() as ctx:
        m = Mem()

        def sb(name, shape, dt=F32):
            return ctx.enter_context(nc.sbuf_tensor(name, shape, dt))

        m.X = sb("X", [128, B, D])
        m.ident = sb("ident", [128, 128])
        m.gnn = sb("gnn", [128, 2, GNN_COLS], F32R)
        m.ahat = sb("ahat", [128, 2, 128], F32R)
        m.adj2 = sb("adj2", [128, 2, 128], F32R)
        m.late = sb("late", [128, 2, LATE_COLS], F32R)
        m.vec = sb("vec", [128, VEC_COLS])
        m.lbias = sb("lbias", [128, SKIPS * 4])
        m.abd = sb("abd", [128, HEADS])
        m.st = sb("st", [128, E], F32R)
        m.dstn = sb("dstn", [128, E], F32R)
        m.srce = sb("srce", [128, ET, 128], F32R)
        m.loga = sb("loga", [128, ET])
        m.same = sb("same", [128, E + 1])
        m.pen = sb("pen", [128, E + 1])
        m.mean = sb("mean", [128, B])
        m.rstd = sb("rstd", [128, B])
        m.ps = ctx.enter_context(nc.psum_tensor("ps", [128, 8, 512], F32))

        with ExitStack() as hctx:
            m.H = hctx.enter_context(nc.sbuf_tensor("H", [128, 2, B, T], F32R))
            with ExitStack() as lctx:
                m.lstm = lctx.enter_context(nc.sbuf_tensor("lstm", [128, 2, LSTM_COLS], F32R))
                with ExitStack() as actx:
                    m.biasrow = actx.enter_context(nc.sbuf_tensor("biasrow", [128, 2, 128], F32R))
                    m.rowsum = actx.enter_context(nc.sbuf_tensor("rowsum", [128, 128], F32R))
                    m.rowsum4 = actx.enter_context(nc.sbuf_tensor("rowsum4", [128, GN], F32R))
                    m.bias4 = actx.enter_context(nc.sbuf_tensor("bias4", [128, GN], F32R))
                    setup(nc, m, adj, gnn_w, vecs, bg0, bg1, src, dst)
                    l0_gnn(nc, m, x, lstm_w)
                l0_lstm(nc, m, late_w)
            l0_residual(nc, m)
        finish_norm(nc, m, "n1")
        with nc.sbuf_tensor("pre1", [128, 2, B, T], F32) as m.pre1, nc.sbuf_tensor("pre2", [128, B, T], F32) as m.pre2:
            l1(nc, m)
        finish_norm(nc, m, "n2")
        l2(nc, m)
        finish_norm(nc, m, "n3")
        l3(nc, m, out)


def setup(nc, m, adj, gnn_w, vecs, bg0, bg1, src, dst):
    with ExitStack() as ctx:
        def sb(name, shape, dt=F32):
            return ctx.enter_context(nc.sbuf_tensor(name, shape, dt))

        def sem(name):
            return ctx.enter_context(nc.semaphore(name))

        gnn_raw = sb("gnn_raw", [128, GNN_COLS])
        adjn = sb("adjn", [128, 128])
        bgb = sb("bgb", [128, 2, 128])
        row_i = sb("row_i", [128, 2, E], I32)
        col_i = sb("col_i", [128, 2, ET], I32)
        rowf = sb("rowf", [128, 2, E])
        colf = sb("colf", [128, 2, ET])
        ones = sb("ones", [128, 128])
        masks = sb("masks", [128, 4])
        node = sb("node", [128, 1])
        rank_no = sb("rank_no", [128, E])
        edge_no = sb("edge_no", [128, ET])
        keyrow = sb("keyrow", [128, E])
        keycol = sb("keycol", [128, ET])
        below = sb("below", [128, ET, E])
        rank = sb("rank", [128, ET])
        perm = sb("perm", [128, ET, E])
        bcast = sb("bcast", [128, 2, ET, 128])
        sorted_row = sb("sorted_row", [128, 2, E])
        onehot = sb("onehot", [128, 2, E])
        dste = sb("dste", [128, ET, 128])
        picked = sb("picked", [128, ET, 128])
        edge_adj = sb("edge_adj", [128, ET])
        anorm = sb("anorm", [128, 2, 128])
        sums = sb("sums", [128, 4])
        dinv = sb("dinv", [128, 2])
        half = sb("half", [128, 128])
        sq = sb("sq", [128, 128])
        rs = sb("rs", [128, 2, 128], F32R)
        bgs = sb("bgs", [128, 2, 2, 128], F32R)
        mix = sb("mix", [128, 2, 128])
        eps_log = sb("eps_log", [128, 1])
        loaded, made, dv, pe, ac = sem("su_loaded"), sem("su_made"), sem("su_dv"), sem("su_pe"), sem("su_ac")
        ps = m.ps

        with nc.Block() as block:
            @block.sync
            def _(sp):
                sp.dma_start(gnn_raw[:, :], gnn_w).then_inc(loaded, 16)
                sp.dma_start(adjn[:, :], adj).then_inc(loaded, 16)
                sp.dma_start(m.vec[:, :], vecs).then_inc(loaded, 16)
                sp.dma_start(bgb[:, 0, :], bg0.partition_broadcast(128)).then_inc(loaded, 16)
                sp.dma_start(bgb[:, 1, :], bg1.partition_broadcast(128)).then_inc(loaded, 16)
                for k, ids in enumerate((src, dst)):
                    sp.dma_start(row_i[:, k, :], ids.partition_broadcast(128)).then_inc(loaded, 16)
                    sp.dma_start(col_i[:, k, :], ids.rearrange("(n a) -> n a", a=ET)).then_inc(loaded, 16)

            @block.gpsimd
            def _(pool):
                chain = Chain(pool, made)
                chain(nc.gpsimd.memset(m.ident[:, :], 0.0))
                chain(nc.gpsimd.affine_select(out=m.ident[:, :], in_=m.ident[:, :], compare_op=ALU.not_equal, fill=1.0,
                                              base=0, pattern=[[-1, 128]], channel_multiplier=1))
                chain(nc.gpsimd.iota(node[:, :], pattern=[[0, 1]], base=0, channel_multiplier=1,
                                     allow_small_or_imprecise_dtypes=True))
                chain(nc.gpsimd.iota(rank_no[:, :], pattern=[[1, E]], base=0, channel_multiplier=0,
                                     allow_small_or_imprecise_dtypes=True))
                chain(nc.gpsimd.iota(edge_no[:, :], pattern=[[1, ET]], base=0, channel_multiplier=ET,
                                     allow_small_or_imprecise_dtypes=True))
                chain(nc.gpsimd.memset(ones[:, :], 1.0))
                chain(nc.gpsimd.memset(eps_log[:, :], EPS_LOG))
                chain(nc.gpsimd.memset(bcast[:, :, :, :], 0.0))
                chain(nc.gpsimd.memset(m.abd[:, :], 1.0))
                chain(nc.gpsimd.affine_select(out=m.abd[:, :], in_=m.abd[:, :], compare_op=ALU.is_ge, fill=0.0,
                                              base=0, pattern=[[-HD, HEADS]], channel_multiplier=1))
                chain(nc.gpsimd.affine_select(out=m.abd[:, :], in_=m.abd[:, :], compare_op=ALU.is_ge, fill=0.0,
                                              base=HD - 1, pattern=[[HD, HEADS]], channel_multiplier=-1))

            @block.vector
            def _(v):
                chain = Chain(v, dv)
                v.wait_ge(loaded, 9 * 16)
                v.wait_ge(made, 11)
                chain(nc.vector.tensor_copy(m.gnn[:, HI, :], gnn_raw[:, :]))
                chain(nc.vector.tensor_tensor(m.gnn[:, LO, :], gnn_raw[:, :], f32(m.gnn[:, HI, :]), ALU.subtract))
                chain(nc.vector.tensor_tensor(sq[:, :], gnn_raw[:, 0:128], gnn_raw[:, 0:128], ALU.mult))
                chain(nc.vector.tensor_copy(m.adj2[:, HI, :], sq[:, :]))
                chain(nc.vector.tensor_tensor(m.adj2[:, LO, :], sq[:, :], f32(m.adj2[:, HI, :]), ALU.subtract))
                chain(nc.vector.tensor_tensor(m.lbias[:, :], m.vec[:, V_BIH:V_BIH + 16], m.vec[:, V_BHH:V_BHH + 16], ALU.add))
                chain(nc.vector.tensor_scalar(m.abd[:, :], m.abd[:, :], m.vec[:, V_A:V_A + 1], None, ALU.mult))
                chain(nc.vector.tensor_tensor(anorm[:, 0, :], adjn[:, :], m.ident[:, :], ALU.add))
                chain(nc.vector.tensor_tensor(anorm[:, 1, :], gnn_raw[:, 0:128], m.ident[:, :], ALU.add))
                chain(nc.vector.reduce_sum(sums[:, 0:1], anorm[:, 0, :], mybir.AxisListType.X))
                chain(nc.vector.reduce_sum(sums[:, 1:2], anorm[:, 1, :], mybir.AxisListType.X))
                chain(nc.vector.tensor_tensor(half[:, :], anorm[:, 0, :], m.ident[:, :], ALU.mult))
                chain(nc.vector.reduce_sum(sums[:, 2:3], half[:, :], mybir.AxisListType.X))
                chain(nc.vector.tensor_tensor(sums[:, 0:1], sums[:, 0:1], sums[:, 1:2], ALU.add))
                chain(nc.vector.tensor_tensor(sums[:, 3:4], sums[:, 0:1], sums[:, 2:3], ALU.subtract))
                chain(nc.vector.reciprocal(dinv[:, 0:1], sums[:, 3:4]))
                chain(nc.vector.tensor_copy(rowf[:, :, :], row_i[:, :, :]))
                chain(nc.vector.tensor_copy(colf[:, :, :], col_i[:, :, :]))
                chain(nc.vector.scalar_tensor_tensor(out=keyrow[:, :], in0=rowf[:, 0, :], scalar=float(E), in1=rank_no[:, :],
                                                     op0=ALU.mult, op1=ALU.add))
                chain(nc.vector.scalar_tensor_tensor(out=keycol[:, :], in0=colf[:, 0, :], scalar=float(E), in1=edge_no[:, :],
                                                     op0=ALU.mult, op1=ALU.add))
                for t in range(ET):
                    chain(nc.vector.tensor_scalar(below[:, t, :], keyrow[:, :], keycol[:, t:t + 1], None, ALU.is_lt,
                                                  ALU.add, accum_out=rank[:, t:t + 1]))
                for t in range(ET):
                    chain(nc.vector.tensor_scalar(perm[:, t, :], rank_no[:, :], rank[:, t:t + 1], None, ALU.is_equal))
                for k in range(2):
                    for t in range(ET):
                        chain(nc.vector.tensor_scalar(bcast[:, k, t, :], ones[:, :], colf[:, k, t:t + 1], None, ALU.mult))
                v.wait_ge(pe, 1)
                chain(nc.vector.tensor_copy(sorted_row[:, :, :], ps[:, 0, :].rearrange("p (k e) -> p k e", k=2)))
                for k in range(2):
                    chain(nc.vector.tensor_scalar(onehot[:, k, :], sorted_row[:, k, :], node[:, 0:1], None, ALU.is_equal))
                chain(nc.vector.tensor_tensor(m.st[:, :], onehot[:, 0, :], onehot[:, 1, :], ALU.add))
                chain(nc.vector.tensor_copy(m.dstn[:, :], onehot[:, 1, :]))
                chain(nc.vector.memset(m.same[:, :], 0.0))
                chain(nc.vector.tensor_tensor(m.same[:, 1:E], sorted_row[:, 0, 1:E], sorted_row[:, 0, 0:E - 1], ALU.is_equal))
                chain(nc.vector.tensor_scalar(m.pen[:, :], m.same[:, :], -1.0, -NEG, ALU.add, ALU.mult))
                v.wait_ge(pe, 2)
                chain(nc.vector.tensor_copy(m.srce[:, :, :], ps[:, 1, 0:E].rearrange("p (t n) -> p t n", t=ET)))
                chain(nc.vector.tensor_copy(dste[:, :, :], ps[:, 1, E:2 * E].rearrange("p (t n) -> p t n", t=ET)))
                v.wait_ge(pe, 3)
                chain(nc.vector.tensor_tensor(picked[:, :, :], ps[:, 2, 0:E].rearrange("p (t n) -> p t n", t=ET),
                                              dste[:, :, :], ALU.mult))
                chain(nc.vector.reduce_sum(edge_adj[:, :], picked[:, :, :], mybir.AxisListType.X))
                v.wait_ge(ac, 1)
                chain(nc.vector.tensor_scalar(half[:, :], anorm[:, 0, :], dinv[:, 1:2], None, ALU.mult))
                v.wait_ge(pe, 4)
                chain(nc.vector.tensor_scalar(sq[:, :], ps[:, 3, 0:128], dinv[:, 1:2], None, ALU.mult))
                chain(nc.vector.tensor_copy(m.ahat[:, HI, :], sq[:, :]))
                chain(nc.vector.tensor_tensor(m.ahat[:, LO, :], sq[:, :], f32(m.ahat[:, HI, :]), ALU.subtract))
                chain(nc.vector.tensor_copy(masks[:, 0:1], m.ident[:, 0:1]))
                chain(nc.vector.tensor_tensor(masks[:, 0:1], masks[:, 0:1], m.ident[:, 1:2], ALU.add))
                chain(nc.vector.tensor_tensor(masks[:, 2:3], m.ident[:, 0:1], m.ident[:, 2:3], ALU.add))
                v.wait_ge(pe, 5)
                chain(nc.vector.tensor_copy(rs[:, HI, :], ps[:, 4, 0:128]))
                chain(nc.vector.tensor_tensor(rs[:, LO, :], ps[:, 4, 0:128], f32(rs[:, HI, :]), ALU.subtract))
                chain(nc.vector.tensor_scalar(mix[:, 0, :], f32(rs[:, LO, :]), m.ident[:, 2:3], None, ALU.mult))
                chain(nc.vector.scalar_tensor_tensor(out=m.rowsum[:, :], in0=f32(rs[:, HI, :]), scalar=masks[:, 0:1],
                                                     in1=mix[:, 0, :], op0=ALU.mult, op1=ALU.add))
                for b in range(GB):
                    chain(nc.vector.tensor_copy(m.rowsum4[:, b * 128:(b + 1) * 128], f32(m.rowsum[:, :])))
                for k in range(2):
                    chain(nc.vector.tensor_copy(bgs[:, k, HI, :], bgb[:, k, :]))
                    chain(nc.vector.tensor_tensor(bgs[:, k, LO, :], bgb[:, k, :], f32(bgs[:, k, HI, :]), ALU.subtract))
                    chain(nc.vector.tensor_scalar(mix[:, k, :], f32(bgs[:, k, LO, :]), m.ident[:, 1:2], None, ALU.mult))
                    chain(nc.vector.scalar_tensor_tensor(out=m.biasrow[:, k, :], in0=f32(bgs[:, k, HI, :]),
                                                         scalar=masks[:, 2:3], in1=mix[:, k, :], op0=ALU.mult, op1=ALU.add))
                for b in range(GB):
                    chain(nc.vector.tensor_copy(m.bias4[:, b * 128:(b + 1) * 128], f32(m.biasrow[:, 0, :])))

            @block.scalar
            def _(act):
                act.wait_ge(dv, 16)
                nc.scalar.activation(dinv[:, 1:2], dinv[:, 0:1], ACT.Sqrt).then_inc(ac, 1)
                act.wait_ge(dv, 40)
                nc.scalar.activation(m.loga[:, :], edge_adj[:, :], ACT.Ln, bias=eps_log[:, 0:1]).then_inc(ac, 1)

            @block.tensor
            def _(t_):
                t_.wait_ge(dv, 28)
                for k in range(2):
                    for t in range(ET):
                        last = nc.tensor.matmul(ps[:, 0, k * E:(k + 1) * E], bcast[:, k, t, :], perm[:, t, :],
                                                start=(t == 0), stop=(t == ET - 1))
                last.then_inc(pe, 1)
                t_.wait_ge(dv, 33)
                for k in range(2):
                    for t in range(ET):
                        last = nc.tensor.transpose(ps[:, 1, (k * ET + t) * 128:(k * ET + t + 1) * 128],
                                                   onehot[:, k, t * 128:(t + 1) * 128], m.ident[:, :])
                last.then_inc(pe, 1)
                for t in range(ET):
                    last = nc.tensor.matmul(ps[:, 2, t * 128:(t + 1) * 128], onehot[:, 0, t * 128:(t + 1) * 128],
                                            adjn[:, :], start=True, stop=True)
                last.then_inc(pe, 1)
                t_.wait_ge(dv, 41)
                nc.tensor.transpose(ps[:, 3, 0:128], half[:, :], m.ident[:, :]).then_inc(pe, 1)
                nc.tensor.matmul(ps[:, 4, 0:128], ones[:, :], gnn_raw[:, 0:128], start=True, stop=True).then_inc(pe, 1)


def l0_gnn(nc, m, x, lstm_w):
    with ExitStack() as ctx:
        def sb(name, shape, dt=F32):
            return ctx.enter_context(nc.sbuf_tensor(name, shape, dt))

        def sem(name):
            return ctx.enter_context(nc.semaphore(name))

        xs = sb("xs", [128, 2, 2, GN], F32R)
        stage = [sb(f"a_stage{s}", [128, 2, 2, GN], F32R) for s in range(3)]
        CUTS = 4
        LC = LSTM_COLS // CUTS
        lraw = sb("lraw", [128, LC])
        landed = [sem(f"a_landed{u}") for u in range(2)]
        passed = sem("a_passed")
        raw_landed, split, prod, hi, lo, wsplit = (sem("a_raw"), sem("a_split"), sem("a_prod"), sem("a_hi"),
                                                   sem("a_lo"), sem("a_wsplit"))
        X = m.X[:, :, :].rearrange("p (i u b) d -> p i u (b d)", u=2, b=GB)
        xd = x.rearrange("(i u b) n d -> n i u b d", u=2, b=GB)
        Xb = m.X[:, :, :].rearrange("p (i u b) d -> p i u b d", u=2, b=GB)
        H = m.H[:, :, :, :].rearrange("p k (i u b) t -> p k i u (b t)", u=2, b=GB)
        ps = m.ps
        STAGES = 4
        PER = 2 * STAGES

        def at(i, s, u):
            return PER * i + 2 * s + u + 1 + PER

        with nc.Block() as block:
            @block.sync
            def _(sp):
                for u in range(2):
                    sp.sem_inc(landed[u], 16)
                with sp.Fori(0, TURNS) as i:
                    for u in range(2):
                        sp.wait_ge(landed[u], 16 * i + 16)
                        sp.dma_start(Xb[:, i, u, :, :], xd[:, i, u, :, :]).then_inc(landed[u], 16)
                for k in range(CUTS):
                    if k:
                        sp.wait_ge(wsplit, 2 * k)
                    sp.dma_start(lraw[:, :], lstm_w[:, k * LC:(k + 1) * LC]).then_inc(raw_landed, 16)

            @block.gpsimd
            def _(pool):
                with pool.Fori(0, TURNS) as i:
                    for u in range(2):
                        hold(pool, landed[u], 16 * i + 32, passed)
                        pool.wait_ge(prod, at(i, 0, u) - PER)
                        nc.gpsimd.tensor_copy(xs[:, u, HI, :], X[:, i, u, :]).then_inc(split, 1)
                        hold(pool, split, 4 * i + 2 * u + 1, passed)
                        nc.gpsimd.tensor_tensor(xs[:, u, LO, :], X[:, i, u, :], f32(xs[:, u, HI, :]),
                                                ALU.subtract).then_inc(split, 1)
                for k in range(CUTS):
                    c = slice(k * LC, (k + 1) * LC)
                    pool.wait_ge(raw_landed, 16 * (k + 1))
                    nc.gpsimd.tensor_copy(m.lstm[:, HI, c], lraw[:, :]).then_inc(wsplit, 1)
                    pool.wait_ge(wsplit, 2 * k + 1)
                    nc.gpsimd.tensor_tensor(m.lstm[:, LO, c], lraw[:, :], f32(m.lstm[:, HI, c]), ALU.subtract).then_inc(wsplit, 1)

            @block.tensor
            def _(pe):
                pe.sem_inc(prod, PER)
                with pe.Fori(0, TURNS) as i:
                    for s in range(STAGES):
                        for u in range(2):
                            bank = ps[:, 4 * u + s, :]
                            if s == 0:
                                pe.wait_ge(split, 4 * i + 2 * u + 2)
                                src_ = xs
                            else:
                                pe.wait_ge(lo, at(i, s - 1, u) - PER)
                                src_ = stage[s - 1]
                            if s == 3:
                                w0, w1 = GNN["Wg1"]
                                nc.tensor.matmul(bank, m.biasrow[:, 1, :], m.rowsum4[:, :], start=True, stop=False)
                                last = mm3(nc, bank, m.gnn[:, HI, w0:w1], m.gnn[:, LO, w0:w1], src_[:, u, HI, :],
                                           src_[:, u, LO, :], False, True)
                            else:
                                w0, w1 = GNN["Wg0"] if s == 1 else GNN["adjT"]
                                if s == 1:
                                    nc.tensor.matmul(bank, m.rowsum[:, :], m.bias4[:, :], start=True, stop=False)
                                for b in range(GB):
                                    c = slice(b * 128, (b + 1) * 128)
                                    last = mm3(nc, bank[:, c], src_[:, u, HI, c], src_[:, u, LO, c], m.gnn[:, HI, w0:w1],
                                               m.gnn[:, LO, w0:w1], s != 1, s != 1 or b == GB - 1)
                            last.then_inc(prod, 1)

            @block.scalar
            def _(act):
                with act.Fori(0, TURNS) as i:
                    for s in range(STAGES):
                        for u in range(2):
                            act.wait_ge(prod, at(i, s, u))
                            dst_ = H[:, HI, i, u, :] if s == 3 else stage[s][:, u, HI, :]
                            take_hi(nc, dst_, ps[:, 4 * u + s, :], ACT.Relu if s % 2 else ACT.Copy).then_inc(hi, 1)

            @block.vector
            def _(v):
                with v.Fori(0, TURNS) as i:
                    for s in range(STAGES):
                        for u in range(2):
                            v.wait_ge(hi, at(i, s, u) - PER)
                            d = [H[:, k, i, u, :] if s == 3 else stage[s][:, u, k, :] for k in (HI, LO)]
                            take_lo(nc, d[LO], ps[:, 4 * u + s, :], d[HI], relu=bool(s % 2)).then_inc(lo, 1)


def l0_lstm(nc, m, late_w):
    with ExitStack() as ctx:
        def sb(name, shape, dt=F32):
            return ctx.enter_context(nc.sbuf_tensor(name, shape, dt))

        gates = sb("gates", [128, 2, 4, 512])
        ig = sb("ig", [128, 2, 512])
        fc = sb("fc", [128, 2, 512])
        cell = sb("cell", [128, 2, 512])
        tanc = sb("tanc", [128, 2, 512])
        hf = sb("hf", [128, 2, 512])
        hs = sb("hs", [128, 2, 2, 512], F32R)
        CUTS = 4
        LC = LATE_COLS // CUTS
        raw = sb("late_raw", [128, LC])
        raw_landed, wsplit = [ctx.enter_context(nc.semaphore(f"b_{n}")) for n in ("raw", "wsplit")]
        ps = m.ps

        class Loop:

            def __init__(self, p):
                self.p, self.nw = p, T // p
                self.nb = {1: 4, 2: 8, 3: 8, 4: 16}[p]
                self.n = self.nb * self.nw
                self.turns = B // self.nb // 2
                self.steps = 2 * p
                self.order = [(s, q) for s in range(p) for q in range(2)]
                self.gates = [(0, 2, 3) if s == 0 else (0, 2, 1, 3) for s, q in self.order]
                self.before = [sum(len(g) for g in self.gates[:k]) for k in range(self.steps + 1)]
                self.per = self.before[-1]
                self.gate_prod, self.gate_act, self.cell_done, self.tanh_done, self.h_done, self.dve = [
                    ctx.enter_context(nc.semaphore(f"b{p}_{n}"))
                    for n in ("gate_prod", "gate_act", "cell", "tanh", "h", "dve")]
                self.own = sum(2 if s == 0 else 4 for s, q in self.order)
                self.H = m.H[:, :, :, 0:self.nw * p].rearrange("a k (i q b) (w j) -> a k i q b w j", q=2, b=self.nb, j=p)

            def cols(self, ap):
                return ap.rearrange("a (b w) -> a b w", w=self.nw)

        loops = [Loop(p) for p in range(1, SKIPS + 1)]

        with nc.Block() as block:
            @block.sync
            def _(sp):
                for k in range(CUTS):
                    if k:
                        sp.wait_ge(wsplit, 2 * k)
                    sp.dma_start(raw[:, :], late_w[:, k * LC:(k + 1) * LC]).then_inc(raw_landed, 16)

            @block.gpsimd
            def _(pool):
                for k in range(CUTS):
                    c = slice(k * LC, (k + 1) * LC)
                    pool.wait_ge(raw_landed, 16 * (k + 1))
                    nc.gpsimd.tensor_copy(m.late[:, HI, c], raw[:, :]).then_inc(wsplit, 1)
                    pool.wait_ge(wsplit, 2 * k + 1)
                    nc.gpsimd.tensor_tensor(m.late[:, LO, c], raw[:, :], f32(m.late[:, HI, c]), ALU.subtract).then_inc(wsplit, 1)

            @block.tensor
            def _(pe):
                for L in loops:
                    if L.p > 1:
                        P = loops[L.p - 2]
                        pe.wait_ge(P.h_done, P.steps * (P.turns + 1))
                    W = m.lstm[:, :, :].rearrange("a k (p w g c) -> a k p w g c", p=SKIPS, w=2, g=4)
                    with pe.Fori(0, L.turns) as i:
                        for k, (s, q) in enumerate(L.order):
                            free = L.before[k - 1] if k >= 2 else L.before[L.steps - 1 + k] - L.per
                            pe.wait_ge(L.gate_act, L.per * i + free + L.per)
                            xh, xl = [L.H[:, j, i, q, :, :, s] for j in (HI, LO)]
                            for g in L.gates[k]:
                                out_ = L.cols(ps[:, 4 * q + g, 0:L.n])
                                last = mm3(nc, out_, W[:, HI, L.p - 1, 0, g, :], W[:, LO, L.p - 1, 0, g, :], xh, xl,
                                           True, s == 0)
                                if s == 0:
                                    last.then_inc(L.gate_prod, 1)
                            if s:
                                pe.wait_ge(L.h_done, L.steps * i + k - 1 + L.steps)
                                for g in L.gates[k]:
                                    mm3(nc, ps[:, 4 * q + g, 0:L.n], W[:, HI, L.p - 1, 1, g, :],
                                        W[:, LO, L.p - 1, 1, g, :], hs[:, q, HI, 0:L.n], hs[:, q, LO, 0:L.n],
                                        False, True).then_inc(L.gate_prod, 1)

            @block.scalar
            def _(act):
                for L in loops:
                    act.sem_inc(L.gate_act, L.per)
                    with act.Fori(0, L.turns) as i:
                        for k, (s, q) in enumerate(L.order):
                            act.wait_ge(L.h_done, L.steps * i + k - 1 + L.steps)
                            for j, g in enumerate(L.gates[k]):
                                act.wait_ge(L.gate_prod, L.per * i + L.before[k] + j + 1)
                                col = 4 * (L.p - 1) + g
                                nc.scalar.activation(gates[:, q, g, 0:L.n], ps[:, 4 * q + g, 0:L.n],
                                                     ACT.Tanh if g == 2 else ACT.Sigmoid,
                                                     bias=m.lbias[:, col:col + 1]).then_inc(L.gate_act, 1)
                            act.wait_ge(L.cell_done, L.steps * i + k + 1)
                            nc.scalar.activation(tanc[:, q, 0:L.n], cell[:, q, 0:L.n], ACT.Tanh).then_inc(L.tanh_done, 1)

            @block.vector
            def _(v):
                for L in loops:
                    v.sem_inc(L.h_done, L.steps)
                    with v.Fori(0, L.turns) as i:
                        done = 0
                        for k, (s, q) in enumerate(L.order):
                            g_ = [gates[:, q, g, 0:L.n] for g in range(4)]
                            c_ = cell[:, q, 0:L.n]
                            acts = L.per * i + L.before[k] + L.per
                            v.wait_ge(L.gate_act, acts + 2)
                            if s == 0:
                                nc.vector.tensor_tensor(c_, g_[0], g_[2], ALU.mult).then_inc(L.cell_done, 1)
                            else:
                                nc.vector.tensor_tensor(ig[:, q, 0:L.n], g_[0], g_[2], ALU.mult).then_inc(L.dve, 1)
                                v.wait_ge(L.gate_act, acts + 3)
                                nc.vector.tensor_tensor(fc[:, q, 0:L.n], g_[1], c_, ALU.mult).then_inc(L.dve, 1)
                                done += 2
                                v.wait_ge(L.dve, L.own * i + done)
                                nc.vector.tensor_tensor(c_, ig[:, q, 0:L.n], fc[:, q, 0:L.n], ALU.add).then_inc(L.cell_done, 1)
                            v.wait_ge(L.tanh_done, L.steps * i + k + 1)
                            nc.vector.tensor_tensor(hf[:, q, 0:L.n], g_[3], tanc[:, q, 0:L.n], ALU.mult).then_inc(L.dve, 1)
                            done += 1
                            v.wait_ge(L.dve, L.own * i + done)
                            if s == L.p - 1:
                                hi_, lo_ = [L.H[:, j, i, q, :, :, s] for j in (HI, LO)]
                                new = L.cols(hf[:, q, 0:L.n])
                            else:
                                hi_, lo_ = [hs[:, q, j, 0:L.n] for j in (HI, LO)]
                                new = hf[:, q, 0:L.n]
                            nc.vector.tensor_copy(hi_, new).then_inc(L.dve, 1)
                            done += 1
                            v.wait_ge(L.dve, L.own * i + done)
                            nc.vector.tensor_tensor(lo_, new, f32(hi_), ALU.subtract).then_inc(L.h_done, 1)
                        assert done == L.own


def bn_group(nc, stats, y, i, u):
    for b in range(GB):
        last = nc.vector.bn_stats(stats[:, i, u, b, :], y[:, b * 128:(b + 1) * 128])
    return last


def l0_residual(nc, m):
    with ExitStack() as ctx:
        hsum = ctx.enter_context(nc.sbuf_tensor("hsum", [128, 2, GN], F32))
        stats = ctx.enter_context(nc.sbuf_tensor("r_stats", [128, TURNS, 2, GB, 6], F32))
        summed, turned, added, chain_s = [ctx.enter_context(nc.semaphore(f"r_{n}")) for n in ("sum", "turn", "add", "chain")]
        H = m.H[:, :, :, :].rearrange("p k (i u b) t -> p k i u (b t)", u=2, b=GB)
        X = m.X[:, :, :].rearrange("p (i u b) d -> p i u (b d)", u=2, b=GB)
        passed = ctx.enter_context(nc.semaphore("r_passed"))
        ps = m.ps

        with nc.Block() as block:
            @block.gpsimd
            def _(pool):
                with pool.Fori(0, TURNS) as i:
                    for u in range(2):
                        hold(pool, turned, 2 * i + u + 1, passed)
                        nc.gpsimd.tensor_tensor(hsum[:, u, :], f32(H[:, HI, i, u, :]), f32(H[:, LO, i, u, :]),
                                                ALU.add).then_inc(summed, 1)

            @block.tensor
            def _(pe):
                pe.sem_inc(turned, 2)
                with pe.Fori(0, TURNS) as i:
                    for u in range(2):
                        pe.wait_ge(summed, 2 * i + u + 1)
                        pe.wait_ge(added, 2 * i + u + 1)
                        for b in range(GB):
                            c = slice(b * 128, (b + 1) * 128)
                            last = nc.tensor.transpose(ps[:, u, c], hsum[:, u, c], m.ident[:, :])
                        last.then_inc(turned, 1)

            @block.vector
            def _(v):
                v.sem_inc(added, 2)
                with v.Fori(0, TURNS) as i:
                    for u in range(2):
                        v.wait_ge(turned, 2 * i + u + 3)
                        nc.vector.tensor_tensor(X[:, i, u, :], ps[:, u, :], X[:, i, u, :], ALU.add).then_inc(added, 1)
                        v.wait_ge(added, 2 * i + u + 3)
                        last = bn_group(nc, stats, X[:, i, u, :], i, u)
                last.then_inc(chain_s, 1)
                v.wait_ge(chain_s, TURNS)
                gather_norm(nc, v, m, stats, ctx, "r")


def gather_norm(nc, v, m, stats, ctx, tag):
    chain = Chain(v, ctx.enter_context(nc.semaphore(f"{tag}_gather")))
    S = stats[:, :, :, :, :].rearrange("p i u b s -> p (i u b) s")
    t = ctx.enter_context(nc.sbuf_tensor(f"{tag}_t", [128, 2, B], F32))
    chain(nc.vector.tensor_tensor(t[:, 0, :], S[:, :, 1], S[:, :, 4], ALU.subtract))
    chain(nc.vector.tensor_tensor(t[:, 1, :], S[:, :, 2], S[:, :, 5], ALU.add))
    chain(nc.vector.tensor_tensor(m.mean[:, :], S[:, :, 1], S[:, :, 4], ALU.add))
    chain(nc.vector.tensor_scalar(m.mean[:, :], m.mean[:, :], 0.5, None, ALU.mult))
    chain(nc.vector.tensor_tensor(t[:, 0, :], t[:, 0, :], t[:, 0, :], ALU.mult))
    chain(nc.vector.scalar_tensor_tensor(out=t[:, 1, :], in0=t[:, 0, :], scalar=float(D // 4), in1=t[:, 1, :],
                                         op0=ALU.mult, op1=ALU.add))
    chain(nc.vector.tensor_scalar(m.rstd[:, :], t[:, 1, :], 1.0 / D, EPS_NORM, ALU.mult, ALU.add))


def finish_norm(nc, m, tag):
    with nc.semaphore(f"{tag}_rec") as rec, nc.semaphore(f"{tag}_root") as root, nc.Block() as block:
        @block.vector
        def _(v):
            nc.vector.reciprocal(m.rstd[:, :], m.rstd[:, :]).then_inc(rec, 1)

        @block.scalar
        def _(act):
            act.wait_ge(rec, 1)
            nc.scalar.activation(m.rstd[:, :], m.rstd[:, :], ACT.Sqrt).then_inc(root, 1)


def norm_group(nc, m, out, y, i, u):
    mean = m.mean[:, :].rearrange("p (i u b) -> p i u b", u=2, b=GB)
    rstd = m.rstd[:, :].rearrange("p (i u b) -> p i u b", u=2, b=GB)
    for b in range(GB):
        c = slice(b * 128, (b + 1) * 128)
        last = nc.vector.tensor_scalar(out[:, c], y[:, c], mean[:, i, u, b:b + 1], rstd[:, i, u, b:b + 1],
                                       ALU.subtract, ALU.mult)
    return last


def late(m, name, k, a=0, b=None):
    c0, c1 = LATE[name]
    return m.late[:, k, c0 + a:(c1 if b is None else c0 + b)]


def batch_coef(nc, v, act_wait, chain, stats, gamma, beta, scale, shift, tmp, rec_sem, root_sem):
    chain(nc.vector.bn_aggr(tmp[:, 0:2], stats))
    chain(nc.vector.tensor_scalar(tmp[:, 2:3], tmp[:, 1:2], EPS_NORM, None, ALU.add))
    nc.vector.reciprocal(tmp[:, 3:4], tmp[:, 2:3]).then_inc(rec_sem, 1)
    v.wait_ge(root_sem, act_wait)
    chain(nc.vector.tensor_tensor(scale, gamma, tmp[:, 4:5], ALU.mult))
    chain(nc.vector.tensor_tensor(tmp[:, 5:6], tmp[:, 0:1], scale, ALU.mult))
    chain(nc.vector.tensor_tensor(shift, beta, tmp[:, 5:6], ALU.subtract))


def l1(nc, m):
    with ExitStack() as ctx:
        def sb(name, shape, dt=F32):
            return ctx.enter_context(nc.sbuf_tensor(name, shape, dt))

        def sem(name):
            return ctx.enter_context(nc.semaphore(name))

        xs = sb("c_xs", [128, 2, 2, GN], F32R)
        agg = sb("c_agg", [128, 2, 2, GN], F32R)
        st1 = sb("c_st1", [128, 2, TURNS * 2, 6])
        st2 = sb("c_st2", [128, TURNS * 2, 6])
        coef = sb("c_coef", [128, 2, 3])
        tmp = sb("c_tmp", [128, 3, 8])
        stats = sb("c_stats", [128, TURNS, 2, GB, 6])
        X = m.X[:, :, :].rearrange("p (i u b) d -> p i u (b d)", u=2, b=GB)
        pre1 = m.pre1[:, :, :, :].rearrange("p k (i u b) t -> p k i u (b t)", u=2, b=GB)
        pre2 = m.pre2[:, :, :].rearrange("p (i u b) t -> p i u (b t)", u=2, b=GB)
        st1v = st1[:, :, :, :].rearrange("p k (i u) s -> p k i u s", u=2)
        st2v = st2[:, :, :].rearrange("p (i u) s -> p i u s", u=2)
        ps = m.ps

        normed, xhi, xlo, prod, ahi, alo, kept, counted = [sem(f"c1_{n}") for n in (
            "normed", "xhi", "xlo", "prod", "ahi", "alo", "kept", "counted")]
        rec, root, chs = sem("c1_rec"), sem("c1_root"), sem("c1_chain")
        passed = sem("c1_passed")
        PER = 6
        with nc.Block() as block:
            @block.vector
            def _(v):
                with v.Fori(0, TURNS) as i:
                    for u in range(2):
                        norm_group(nc, m, X[:, i, u, :], X[:, i, u, :], i, u).then_inc(normed, 1)
                    for u in range(2):
                        v.wait_ge(ahi, 2 * i + u + 1)
                        take_lo(nc, agg[:, u, LO, :], ps[:, 4 * u, :], agg[:, u, HI, :]).then_inc(alo, 1)
                    for u in range(2):
                        for t in range(2):
                            v.wait_ge(kept, 4 * i + 2 * u + t + 1)
                            nc.vector.bn_stats(st1v[:, t, i, u, :], pre1[:, t, i, u, :]).then_inc(counted, 1)
                v.wait_ge(counted, 4 * TURNS)
                chain = Chain(v, chs)
                for t in range(2):
                    batch_coef(nc, v, t + 1, chain, st1[:, t, :, :].rearrange("p g s -> p (g s)"),
                               m.vec[:, V_G1 + t:V_G1 + t + 1], m.vec[:, V_BE1 + t:V_BE1 + t + 1],
                               coef[:, 0, t:t + 1], coef[:, 1, t:t + 1], tmp[:, t, :], rec, root)

            @block.scalar
            def _(act):
                with act.Fori(0, TURNS) as i:
                    for u in range(2):
                        act.wait_ge(normed, 2 * i + u + 1)
                        act.wait_ge(prod, PER * i + u + 1)
                        take_hi(nc, xs[:, u, HI, :], X[:, i, u, :]).then_inc(xhi, 1)
                    for u in range(2):
                        act.wait_ge(prod, PER * i + u + 1 + PER)
                        take_hi(nc, agg[:, u, HI, :], ps[:, 4 * u, :]).then_inc(ahi, 1)
                    for u in range(2):
                        for t in range(2):
                            act.wait_ge(prod, PER * i + 2 + 2 * u + t + 1 + PER)
                            nc.scalar.activation(pre1[:, t, i, u, :], ps[:, 4 * u + 1 + t, :], ACT.Identity,
                                                 bias=m.vec[:, V_B1 + t:V_B1 + t + 1]).then_inc(kept, 1)
                for t in range(2):
                    act.wait_ge(rec, t + 1)
                    nc.scalar.activation(tmp[:, t, 4:5], tmp[:, t, 3:4], ACT.Sqrt).then_inc(root, 1)

            @block.gpsimd
            def _(pool):
                with pool.Fori(0, TURNS) as i:
                    for u in range(2):
                        hold(pool, xhi, 2 * i + u + 1, passed)
                        nc.gpsimd.tensor_tensor(xs[:, u, LO, :], X[:, i, u, :], f32(xs[:, u, HI, :]),
                                                ALU.subtract).then_inc(xlo, 1)

            @block.tensor
            def _(pe):
                pe.sem_inc(prod, PER)
                with pe.Fori(0, TURNS) as i:
                    for u in range(2):
                        pe.wait_ge(xlo, 2 * i + u + 1)
                        for b in range(GB):
                            c = slice(b * 128, (b + 1) * 128)
                            last = mm3(nc, ps[:, 4 * u, c], xs[:, u, HI, c], xs[:, u, LO, c], m.ahat[:, HI, :],
                                       m.ahat[:, LO, :], True, True)
                        last.then_inc(prod, 1)
                    for u in range(2):
                        pe.wait_ge(alo, 2 * i + u + 1)
                        for t in range(2):
                            w = [late(m, "L1W1", k, 128 * t, 128 * (t + 1)) for k in (HI, LO)]
                            mm3(nc, ps[:, 4 * u + 1 + t, :], w[HI], w[LO], agg[:, u, HI, :], agg[:, u, LO, :],
                                True, True).then_inc(prod, 1)

        rf = sb("c_rf", [128, 2, 2, GN])
        rr = sb("c_rr", [128, 2, 2, 2, GN], F32R)
        relu, rhi, rlo, prod, kept, counted = [sem(f"c2_{n}") for n in ("relu", "rhi", "rlo", "prod", "kept", "counted")]
        rec2, root2, chs2 = sem("c2_rec"), sem("c2_root"), sem("c2_chain")
        with nc.Block() as block:
            @block.scalar
            def _(act):
                with act.Fori(0, TURNS) as i:
                    for u in range(2):
                        act.wait_ge(rlo, 2 * i + u + 1)
                        for t in range(2):
                            last = nc.scalar.activation(rf[:, u, t, :], pre1[:, t, i, u, :], ACT.Relu,
                                                        bias=coef[:, 1, t:t + 1], scale=coef[:, 0, t:t + 1])
                        last.then_inc(relu, 1)
                    for u in range(2):
                        act.wait_ge(prod, 2 * i + u + 3)
                        nc.scalar.activation(pre2[:, i, u, :], ps[:, u, :], ACT.Identity,
                                             bias=m.vec[:, V_B2:V_B2 + 1]).then_inc(kept, 1)
                act.wait_ge(rec2, 1)
                nc.scalar.activation(tmp[:, 2, 4:5], tmp[:, 2, 3:4], ACT.Sqrt).then_inc(root2, 1)

            @block.gpsimd
            def _(pool):
                with pool.Fori(0, TURNS) as i:
                    for u in range(2):
                        hold(pool, relu, 2 * i + u + 1, passed)
                        hold(pool, prod, 2 * i + u + 1, passed)
                        nc.gpsimd.tensor_copy(rr[:, u, HI, :, :], rf[:, u, :, :]).then_inc(rhi, 1)

            @block.vector
            def _(v):
                v.sem_inc(rlo, 2)
                with v.Fori(0, TURNS) as i:
                    for u in range(2):
                        v.wait_ge(rhi, 2 * i + u + 1)
                        nc.vector.tensor_tensor(rr[:, u, LO, :, :], rf[:, u, :, :], f32(rr[:, u, HI, :, :]),
                                                ALU.subtract).then_inc(rlo, 1)
                    for u in range(2):
                        v.wait_ge(kept, 2 * i + u + 1)
                        nc.vector.bn_stats(st2v[:, i, u, :], pre2[:, i, u, :]).then_inc(counted, 1)
                v.wait_ge(counted, 2 * TURNS)
                batch_coef(nc, v, 1, Chain(v, chs2), st2[:, :, :].rearrange("p g s -> p (g s)"),
                           m.vec[:, V_G2:V_G2 + 1], m.vec[:, V_BE2:V_BE2 + 1], coef[:, 0, 2:3], coef[:, 1, 2:3],
                           tmp[:, 2, :], rec2, root2)

            @block.tensor
            def _(pe):
                pe.sem_inc(prod, 2)
                with pe.Fori(0, TURNS) as i:
                    for u in range(2):
                        pe.wait_ge(rlo, 2 * i + u + 3)
                        for t in range(2):
                            w = [late(m, "L1W2", k, 128 * t, 128 * (t + 1)) for k in (HI, LO)]
                            last = mm3(nc, ps[:, u, :], w[HI], w[LO], rr[:, u, HI, t, :], rr[:, u, LO, t, :],
                                       t == 0, t == 1)
                        last.then_inc(prod, 1)

        z = sb("c_z", [128, 2, GN])
        scaled, turned, added, cnt3 = [sem(f"c3_{n}") for n in ("scaled", "turned", "added", "counted")]
        with nc.Block() as block:
            @block.scalar
            def _(act):
                with act.Fori(0, TURNS) as i:
                    for u in range(2):
                        act.wait_ge(turned, 2 * i + u + 1)
                        nc.scalar.activation(z[:, u, :], pre2[:, i, u, :], ACT.Identity, bias=coef[:, 1, 2:3],
                                             scale=coef[:, 0, 2:3]).then_inc(scaled, 1)

            @block.tensor
            def _(pe):
                pe.sem_inc(turned, 2)
                with pe.Fori(0, TURNS) as i:
                    for u in range(2):
                        pe.wait_ge(scaled, 2 * i + u + 1)
                        pe.wait_ge(added, 2 * i + u + 1)
                        for b in range(GB):
                            c = slice(b * 128, (b + 1) * 128)
                            last = nc.tensor.transpose(ps[:, u, c], z[:, u, c], m.ident[:, :])
                        last.then_inc(turned, 1)

            @block.vector
            def _(v):
                v.sem_inc(added, 2)
                with v.Fori(0, TURNS) as i:
                    for u in range(2):
                        v.wait_ge(turned, 2 * i + u + 3)
                        nc.vector.tensor_tensor(X[:, i, u, :], ps[:, u, :], X[:, i, u, :], ALU.add).then_inc(added, 1)
                        v.wait_ge(added, 2 * i + u + 3)
                        last = bn_group(nc, stats, X[:, i, u, :], i, u)
                last.then_inc(cnt3, 1)
                v.wait_ge(cnt3, TURNS)
                gather_norm(nc, v, m, stats, ctx, "c")


def l2(nc, m):
    with ExitStack() as ctx:
        def sb(name, shape, dt=F32, c=ctx):
            return c.enter_context(nc.sbuf_tensor(name, shape, dt))

        def sem(name):
            return ctx.enter_context(nc.semaphore(name))

        V = sb("V", [128, 2, TURNS, 2, GB, D], F32R)
        scores = sb("scores", [128, ET, TURNS, 2, GB * HEADS])
        attn = sb("attn", [128, ET, TURNS, 2, GB * HEADS])
        stats = sb("d_stats", [128, TURNS, 2, GB, 6])
        X = m.X[:, :, :].rearrange("p (i u b) d -> p i u (b d)", u=2, b=GB)
        ps = m.ps

        passed = sem("d_passed")

        with ExitStack() as c1:
            xs = sb("d_xs", [128, 2, GN], F32, c1)
            xt = sb("d_xt", [128, 2, 2, GN], F32R, c1)
            q = sb("d_q", [128, 2, 2, GB, D], F32R, c1)
            z2 = sb("d_z2", [128, 2, GB, E], F32, c1)
            lz = sb("d_lz", [128, 2, GB, E], F32, c1)
            normed, copied, prod, hi, lo, leak, scored = [sem(f"d1_{n}") for n in (
                "normed", "copied", "prod", "hi", "lo", "leak", "scored")]
            PER = 8
            with nc.Block() as block:
                @block.vector
                def _(v):
                    with v.Fori(0, TURNS) as i:
                        for u in range(2):
                            v.wait_ge(prod, PER * i + u + 1)
                            v.wait_ge(copied, 2 * i + u + 1)
                            norm_group(nc, m, xs[:, u, :], X[:, i, u, :], i, u).then_inc(normed, 1)
                        for u in range(2):
                            v.wait_ge(hi, 8 * i + u + 1)
                            take_lo(nc, xt[:, u, LO, :], ps[:, 4 * u, :], xt[:, u, HI, :]).then_inc(lo, 1)
                        for u in range(2):
                            qv = ps[:, 4 * u + 2:4 * u + 4, :].rearrange("p k (b w d) -> p (k b) w d", b=2, w=2)
                            v.wait_ge(hi, 8 * i + 2 + 2 * u + 2)
                            take_lo(nc, q[:, u, LO, :, :], qv[:, :, 0, :], q[:, u, HI, :, :]).then_inc(lo, 1)
                            take_lo(nc, V[:, LO, i, u, :, :], qv[:, :, 1, :], V[:, HI, i, u, :, :]).then_inc(lo, 1)
                        for u in range(2):
                            v.wait_ge(hi, 8 * i + 6 + u + 1)
                            zz = ps[:, 4 * u:4 * u + 2, :].rearrange("p k (b e) -> p (k b) e", b=2)
                            nc.vector.tensor_tensor(lz[:, u, :, :], zz, z2[:, u, :, :], ALU.max).then_inc(leak, 1)
                        for u in range(2):
                            v.wait_ge(prod, PER * i + 6 + u + 1 + PER)
                            nc.vector.tensor_copy(scores[:, :, i, u, :],
                                                  ps[:, 4 * u + 2, 0:ET * GB * HEADS].rearrange("p (t s) -> p t s", t=ET)
                                                  ).then_inc(scored, 1)

                @block.gpsimd
                def _(pool):
                    pool.sem_inc(copied, 2)
                    with pool.Fori(0, TURNS) as i:
                        for u in range(2):
                            hold(pool, normed, 2 * i + u + 1, passed)
                            nc.gpsimd.tensor_copy(X[:, i, u, :], xs[:, u, :]).then_inc(copied, 1)

                @block.scalar
                def _(act):
                    with act.Fori(0, TURNS) as i:
                        for u in range(2):
                            act.wait_ge(prod, PER * i + u + 1 + PER)
                            take_hi(nc, xt[:, u, HI, :], ps[:, 4 * u, :]).then_inc(hi, 1)
                        for u in range(2):
                            qv = ps[:, 4 * u + 2:4 * u + 4, :].rearrange("p k (b w d) -> p (k b) w d", b=2, w=2)
                            act.wait_ge(prod, PER * i + 2 + u + 1 + PER)
                            take_hi(nc, q[:, u, HI, :, :], qv[:, :, 0, :]).then_inc(hi, 1)
                            take_hi(nc, V[:, HI, i, u, :, :], qv[:, :, 1, :]).then_inc(hi, 1)
                        for u in range(2):
                            act.wait_ge(prod, PER * i + 4 + u + 1 + PER)
                            zz = ps[:, 4 * u:4 * u + 2, :].rearrange("p k (b e) -> p (k b) e", b=2)
                            nc.scalar.activation(z2[:, u, :, :], zz, ACT.Copy, scale=SLOPE).then_inc(hi, 1)

                @block.tensor
                def _(pe):
                    pe.sem_inc(prod, PER)
                    with pe.Fori(0, TURNS) as i:
                        for u in range(2):
                            pe.wait_ge(normed, 2 * i + u + 1)
                            for b in range(GB):
                                c = slice(b * 128, (b + 1) * 128)
                                last = nc.tensor.transpose(ps[:, 4 * u, c], xs[:, u, c], m.ident[:, :])
                            last.then_inc(prod, 1)
                        for u in range(2):
                            pe.wait_ge(lo, 6 * i + u + 1)
                            pe.wait_ge(scored, 2 * i + u + 1)
                            for b in range(GB):
                                c = slice(b * 128, (b + 1) * 128)
                                o = ps[:, 4 * u + 2 + b // 2, (b % 2) * 256:(b % 2) * 256 + 256]
                                last = mm3(nc, o, xt[:, u, HI, c], xt[:, u, LO, c], late(m, "QV", HI), late(m, "QV", LO),
                                           True, True)
                            last.then_inc(prod, 1)
                        for u in range(2):
                            pe.wait_ge(lo, 6 * i + 2 + 2 * u + 1)
                            for b in range(GB):
                                o = ps[:, 4 * u + b // 2, (b % 2) * 256:(b % 2) * 256 + 256]
                                nc.tensor.matmul(o, q[:, u, HI, b, :], m.st[:, :], start=True, stop=False)
                                last = nc.tensor.matmul(o, q[:, u, LO, b, :], m.st[:, :], start=False, stop=True)
                            last.then_inc(prod, 1)
                        for u in range(2):
                            pe.wait_ge(leak, 2 * i + u + 1)
                            pe.wait_ge(lo, 6 * i + 2 + 2 * u + 2)
                            for t in range(ET):
                                for b in range(GB):
                                    c = (t * GB + b) * HEADS
                                    last = nc.tensor.matmul(ps[:, 4 * u + 2, c:c + HEADS], lz[:, u, b, t * 128:(t + 1) * 128],
                                                            m.abd[:, :], start=True, stop=True)
                            last.then_inc(prod, 1)

                @block.sync
                def _(sp):
                    sp.sem_inc(scored, 2)

        with ExitStack() as c2:
            se = sb("s_e", [128, 2, E], F32, c2)
            pre = sb("s_pre", [128, 2, E], F32, c2)
            top = sb("s_top", [128, 2, E], F32, c2)
            ex = sb("s_ex", [128, 2, E], F32, c2)
            dv, pe_s, ac = sem("d2_dv"), sem("d2_pe"), sem("d2_ac")
            sc = scores[:, :, :, :, :].rearrange("p t i u s -> p t (i u s)")
            at_ = attn[:, :, :, :, :].rearrange("p t i u s -> p t (i u s)")
            with nc.Block() as block:
                @block.vector
                def _(v):
                    chain = Chain(v, dv)
                    for t in range(ET):
                        chain(nc.vector.tensor_scalar(sc[:, t, :], sc[:, t, :], m.loga[:, t:t + 1], None, ALU.add))
                    v.wait_ge(pe_s, 1)
                    chain(nc.vector.tensor_copy(se[:, :, :], ps[:, 0, :].rearrange("p (k e) -> p k e", k=2)))
                    for k in range(2):
                        chain(nc.vector.tensor_tensor_scan(pre[:, k, :], m.pen[:, 0:E], se[:, k, :], NEG, ALU.add, ALU.max))
                    for k in range(2):
                        chain(nc.vector.tensor_tensor_scan(top[:, k, ::-1], m.pen[:, E:0:-1], pre[:, k, ::-1], NEG,
                                                           ALU.add, ALU.max))
                    chain(nc.vector.tensor_tensor(se[:, :, :], se[:, :, :], top[:, :, :], ALU.subtract))
                    v.wait_ge(ac, 1)
                    for k in range(2):
                        chain(nc.vector.tensor_tensor_scan(pre[:, k, :], m.same[:, 0:E], ex[:, k, :], 0.0, ALU.mult, ALU.add))
                    for k in range(2):
                        chain(nc.vector.tensor_tensor_scan(top[:, k, ::-1], m.same[:, E:0:-1], pre[:, k, ::-1], 0.0,
                                                           ALU.mult, ALU.max))
                    chain(nc.vector.reciprocal(top[:, :, :], top[:, :, :]))
                    chain(nc.vector.tensor_tensor(ex[:, :, :], ex[:, :, :], top[:, :, :], ALU.mult))
                    v.wait_ge(pe_s, 2)
                    chain(nc.vector.tensor_copy(at_[:, :, :], ps[:, 1, :].rearrange("p (t s) -> p t s", t=ET)))

                @block.tensor
                def _(pe):
                    pe.wait_ge(dv, 2)
                    for k in range(2):
                        for t in range(ET):
                            last = nc.tensor.transpose(ps[:, 0, k * E + t * 128:k * E + (t + 1) * 128],
                                                       sc[:, t, k * 128:(k + 1) * 128], m.ident[:, :])
                    last.then_inc(pe_s, 1)
                    pe.wait_ge(dv, 14)
                    for t in range(ET):
                        for k in range(2):
                            last = nc.tensor.transpose(ps[:, 1, (t * 2 + k) * 128:(t * 2 + k + 1) * 128],
                                                       ex[:, k, t * 128:(t + 1) * 128], m.ident[:, :])
                    last.then_inc(pe_s, 1)

                @block.scalar
                def _(act):
                    act.wait_ge(dv, 8)
                    nc.scalar.activation(ex[:, :, :], se[:, :, :], ACT.Exp).then_inc(ac, 1)

        with ExitStack() as c3:
            avf = sb("e_avf", [128, 2, ET, GN], F32, c3)
            av = sb("e_av", [128, 2, 2, ET, GN], F32R, c3)
            y = sb("e_y", [128, 2, 2, GN], F32R, c3)
            prod, weighed, avhi, avlo, yhi, ylo, added, cnt = [sem(f"d3_{n}") for n in (
                "prod", "weighed", "avhi", "avlo", "yhi", "ylo", "added", "cnt")]
            PER = 6
            with nc.Block() as block:
                @block.tensor
                def _(pe):
                    pe.sem_inc(prod, PER)
                    with pe.Fori(0, TURNS) as i:
                        for u in range(2):
                            pe.wait_ge(weighed, 2 * i + u + 1)
                            for t in range(ET):
                                w = m.dstn[:, t * 128:(t + 1) * 128]
                                o = ps[:, 4 * u + t, :]
                                nc.tensor.matmul(o, w, V[:, HI, i, u, :, :].rearrange("p b d -> p (b d)"), start=True, stop=False)
                                last = nc.tensor.matmul(o, w, V[:, LO, i, u, :, :].rearrange("p b d -> p (b d)"),
                                                        start=False, stop=True)
                            last.then_inc(prod, 1)
                        for u in range(2):
                            pe.wait_ge(avlo, 2 * i + u + 1)
                            for b in range(GB):
                                c = slice(b * 128, (b + 1) * 128)
                                for t in range(ET):
                                    for k in (HI, LO):
                                        last = nc.tensor.matmul(ps[:, 4 * u + 2, c], av[:, u, k, t, c], m.srce[:, t, :],
                                                                start=(t == 0 and k == HI), stop=(t == ET - 1 and k == LO))
                            last.then_inc(prod, 1)
                        for u in range(2):
                            pe.wait_ge(ylo, 2 * i + u + 1)
                            pe.wait_ge(added, 2 * i + u + 1)
                            for b in range(GB):
                                c = slice(b * 128, (b + 1) * 128)
                                last = mm3(nc, ps[:, 4 * u + 3, c], y[:, u, HI, c], y[:, u, LO, c], late(m, "WOUT", HI),
                                           late(m, "WOUT", LO), True, True)
                            last.then_inc(prod, 1)

                @block.vector
                def _(v):
                    v.sem_inc(weighed, 2)
                    v.sem_inc(added, 2)
                    with v.Fori(0, TURNS) as i:
                        for u in range(2):
                            v.wait_ge(prod, PER * i + u + 1 + PER)
                            for t in range(ET):
                                last = nc.vector.tensor_tensor(
                                    avf[:, u, t, :].rearrange("p (s d) -> p s d", d=HD),
                                    ps[:, 4 * u + t, :].rearrange("p (s d) -> p s d", d=HD),
                                    attn[:, t, i, u, :].unsqueeze(2).broadcast_to([128, GB * HEADS, HD]), ALU.mult)
                            last.then_inc(weighed, 1)
                        for u in range(2):
                            v.wait_ge(yhi, 2 * i + u + 1)
                            take_lo(nc, y[:, u, LO, :], ps[:, 4 * u + 2, :], y[:, u, HI, :]).then_inc(ylo, 1)
                        for u in range(2):
                            v.wait_ge(prod, PER * i + 4 + u + 1 + PER)
                            nc.vector.tensor_tensor(X[:, i, u, :], ps[:, 4 * u + 3, :], X[:, i, u, :], ALU.add).then_inc(added, 1)
                            v.wait_ge(added, 2 * i + u + 3)
                            last = bn_group(nc, stats, X[:, i, u, :], i, u)
                    last.then_inc(cnt, 1)
                    v.wait_ge(cnt, TURNS)
                    gather_norm(nc, v, m, stats, c3, "e")

                @block.scalar
                def _(act):
                    with act.Fori(0, TURNS) as i:
                        for u in range(2):
                            act.wait_ge(weighed, 2 * i + u + 3)
                            act.wait_ge(prod, PER * i + 2 + u + 1)
                            take_hi(nc, av[:, u, HI, :, :], avf[:, u, :, :]).then_inc(avhi, 1)
                        for u in range(2):
                            act.wait_ge(prod, PER * i + 2 + u + 1 + PER)
                            take_hi(nc, y[:, u, HI, :], ps[:, 4 * u + 2, :]).then_inc(yhi, 1)

                @block.gpsimd
                def _(pool):
                    with pool.Fori(0, TURNS) as i:
                        for u in range(2):
                            hold(pool, avhi, 2 * i + u + 1, passed)
                            nc.gpsimd.tensor_tensor(av[:, u, LO, :, :], avf[:, u, :, :], f32(av[:, u, HI, :, :]),
                                                    ALU.subtract).then_inc(avlo, 1)


def l3(nc, m, out):
    with ExitStack() as ctx:
        def sb(name, shape, dt=F32):
            return ctx.enter_context(nc.sbuf_tensor(name, shape, dt))

        def sem(name):
            return ctx.enter_context(nc.semaphore(name))

        xs = sb("f_xs", [128, 2, 2, GN], F32R)
        ax = sb("f_ax", [128, 2, 2, GN], F32R)
        h1 = sb("f_h1", [128, 2, 2, 2, GN], F32R)
        a1 = sb("f_a1", [128, 2, 2, 2, GN], F32R)
        h2 = sb("f_h2", [128, 2, 2, 4, GN], F32R)
        s3 = sb("f_s3", [128, 2, 2, GN], F32R)
        stats = sb("f_stats", [128, TURNS, 2, GB, 6])
        ln = sb("f_ln", [128, 2, 4, GB])
        power = sb("f_power", [128, GB])
        res = sb("f_res", [128, 2, GN])
        X = m.X[:, :, :].rearrange("p (i u b) d -> p i u (b d)", u=2, b=GB)
        outd = out.rearrange("(i u b) n d -> n i u b d", u=2, b=GB)
        ps = m.ps
        normed, xhi, xlo, prod, hi, lo, fin, added, counted, ready, written, gp, xused = [sem(f"f_{n}") for n in (
            "normed", "xhi", "xlo", "prod", "hi", "lo", "fin", "added", "counted", "ready", "written", "gp", "xused")]
        stored = [sem(f"f_stored{u}") for u in range(2)]
        passed = sem("f_passed")

        PARTS = ([(0, 0, 0, ax, False)] + [(1, k, 1 + k, h1, True) for k in range(2)] +
                 [(2, t, (3 + t) % 4, a1, False) for t in range(2)] + [(3, t, (1 + t) % 4, h2, True) for t in range(4)] +
                 [(4, 0, 1, s3, False)])
        ORDER = [(u, part) for s in range(5) for u in range(2) for part in PARTS if part[0] == s]
        PER = len(ORDER)
        LAST_BANK = 2

        def done(i, s, u):
            return PER * i + max(n for n, (w, part) in enumerate(ORDER) if w == u and part[0] == s) + 1

        def pair(buf, u, k, part):
            return buf[:, u, k, :] if buf in (ax, s3) else buf[:, u, k, part, :]

        def product(u, s, k, bank):
            o = ps[:, 4 * u + bank, :]
            if s == 0:
                for b in range(GB):
                    c = slice(b * 128, (b + 1) * 128)
                    last = mm3(nc, o[:, c], xs[:, u, HI, c], xs[:, u, LO, c], m.adj2[:, HI, :], m.adj2[:, LO, :], True, True)
            elif s == 1:
                for b in range(2):
                    g = 2 * k + b
                    last = mm3(nc, o[:, b * 256:(b + 1) * 256], ax[:, u, HI, g * 128:(g + 1) * 128],
                               ax[:, u, LO, g * 128:(g + 1) * 128], late(m, "L3W1", HI), late(m, "L3W1", LO), True, True)
            elif s == 2:
                for b in range(GB):
                    c = slice((b % 2) * 256 + k * 128, (b % 2) * 256 + (k + 1) * 128)
                    last = mm3(nc, o[:, b * 128:(b + 1) * 128], h1[:, u, HI, b // 2, c], h1[:, u, LO, b // 2, c],
                               m.adj2[:, HI, :], m.adj2[:, LO, :], True, True)
            elif s == 3:
                for t in range(2):
                    c = 512 * t + 128 * k
                    last = mm3(nc, o, late(m, "L3W2", HI, c, c + 128), late(m, "L3W2", LO, c, c + 128),
                               a1[:, u, HI, t, :], a1[:, u, LO, t, :], t == 0, t == 1)
            else:
                for b in range(GB):
                    for t in range(4):
                        c = slice(b * 128, (b + 1) * 128)
                        last = mm3(nc, o[:, c], h2[:, u, HI, t, c], h2[:, u, LO, t, c],
                                   late(m, "L3W3", HI, 128 * t, 128 * t + 128), late(m, "L3W3", LO, 128 * t, 128 * t + 128),
                                   t == 0, t == 3)
            return last

        with nc.Block() as block:
            @block.tensor
            def _(pe):
                pe.sem_inc(xused, 2)
                with pe.Fori(0, TURNS) as i:
                    for u, (s, k, bank, _, _) in ORDER:
                        if s == 0:
                            pe.wait_ge(xlo, 2 * i + u + 1)
                        elif k == 0:
                            pe.wait_ge(lo, done(i, s - 1, u))
                        if s == 3 and k == 1:
                            pe.wait_ge(added, 2 * i + u + 1)
                        product(u, s, k, bank).then_inc(prod, 1)
                    for u in range(2):
                        pe.wait_ge(lo, done(i, 4, u))
                        mm3(nc, ps[:, 4 * u + LAST_BANK, :], m.adj2[:, HI, :], m.adj2[:, LO, :], s3[:, u, HI, :],
                            s3[:, u, LO, :], True, True).then_inc(fin, 1)

            @block.scalar
            def _(act):
                with act.Fori(0, TURNS) as i:
                    for u in range(2):
                        act.wait_ge(normed, 2 * i + u + 1)
                        act.wait_ge(fin, 2 * i + u + 1)
                        take_hi(nc, xs[:, u, HI, :], X[:, i, u, :]).then_inc(xhi, 1)
                    for n, (u, (s, k, bank, buf, relu)) in enumerate(ORDER):
                        act.wait_ge(prod, PER * i + n + 1)
                        take_hi(nc, pair(buf, u, HI, k), ps[:, 4 * u + bank, :], ACT.Relu if relu else ACT.Copy).then_inc(hi, 1)

            @block.vector
            def _(v):
                v.sem_inc(added, 2)
                with v.Fori(0, TURNS) as i:
                    for u in range(2):
                        norm_group(nc, m, X[:, i, u, :], X[:, i, u, :], i, u).then_inc(normed, 1)
                    for n, (u, (s, k, bank, buf, relu)) in enumerate(ORDER):
                        v.wait_ge(hi, PER * i + n + 1)
                        take_lo(nc, pair(buf, u, LO, k), ps[:, 4 * u + bank, :], pair(buf, u, HI, k), relu).then_inc(lo, 1)
                    for u in range(2):
                        v.wait_ge(fin, 2 * i + u + 3)
                        nc.vector.tensor_tensor(X[:, i, u, :], ps[:, 4 * u + LAST_BANK, :], X[:, i, u, :],
                                                ALU.add).then_inc(added, 1)
                        v.wait_ge(added, 2 * i + u + 3)
                        bn_group(nc, stats, X[:, i, u, :], i, u).then_inc(counted, 1)
                    for u in range(2):
                        v.wait_ge(ready, 2 * i + u + 2)
                        v.wait_ge(stored[u], 16 * i + 16)
                        for b in range(GB):
                            c = slice(b * 128, (b + 1) * 128)
                            last = nc.vector.tensor_scalar(res[:, u, c], X[:, i, u, c], ln[:, u, 0, b:b + 1],
                                                           ln[:, u, 3, b:b + 1], ALU.subtract, ALU.mult)
                        last.then_inc(written, 1)

            @block.gpsimd
            def _(pool):
                nc.gpsimd.memset(power[:, :], -0.5).then_inc(ready, 1)
                with pool.Fori(0, TURNS) as i:
                    for u in range(2):
                        hold(pool, xhi, 2 * i + u + 1, passed)
                        nc.gpsimd.tensor_tensor(xs[:, u, LO, :], X[:, i, u, :], f32(xs[:, u, HI, :]),
                                                ALU.subtract).then_inc(xlo, 1)
                    for u in range(2):
                        S = stats[:, i, u, :, :]
                        hold(pool, counted, 2 * i + u + 1, passed)
                        n0 = 12 * i + 6 * u
                        nc.gpsimd.tensor_tensor(ln[:, u, 0, :], S[:, :, 1], S[:, :, 4], ALU.add).then_inc(gp, 1)
                        nc.gpsimd.tensor_tensor(ln[:, u, 1, :], S[:, :, 1], S[:, :, 4], ALU.subtract).then_inc(gp, 1)
                        nc.gpsimd.tensor_tensor(ln[:, u, 2, :], S[:, :, 2], S[:, :, 5], ALU.add).then_inc(gp, 1)
                        hold(pool, gp, n0 + 3, passed)
                        nc.gpsimd.tensor_scalar(ln[:, u, 0, :], ln[:, u, 0, :], 0.5, None, ALU.mult).then_inc(gp, 1)
                        nc.gpsimd.tensor_tensor(ln[:, u, 1, :], ln[:, u, 1, :], ln[:, u, 1, :], ALU.mult).then_inc(gp, 1)
                        hold(pool, gp, n0 + 5, passed)
                        nc.gpsimd.tensor_scalar(ln[:, u, 1, :], ln[:, u, 1, :], float(D // 4), None, ALU.mult).then_inc(gp, 1)
                        hold(pool, gp, n0 + 6, passed)
                        nc.gpsimd.tensor_tensor(ln[:, u, 2, :], ln[:, u, 2, :], ln[:, u, 1, :], ALU.add).then_inc(xused, 1)
                        hold(pool, xused, 4 * i + 2 * u + 3, passed)
                        nc.gpsimd.tensor_scalar(ln[:, u, 2, :], ln[:, u, 2, :], 1.0 / D, EPS_NORM, ALU.mult,
                                                ALU.add).then_inc(xused, 1)
                        hold(pool, xused, 4 * i + 2 * u + 4, passed)
                        nc.gpsimd.tensor_tensor(ln[:, u, 3, :], ln[:, u, 2, :], power[:, :], ALU.pow).then_inc(ready, 1)

            @block.sync
            def _(sp):
                sp.sem_inc(fin, 2)
                for u in range(2):
                    sp.sem_inc(stored[u], 16)
                with sp.Fori(0, TURNS) as i:
                    for u in range(2):
                        sp.wait_ge(written, 2 * i + u + 1)
                        sp.dma_start(outd[:, i, u, :, :], res[:, u, :].rearrange("p (b d) -> p b d", b=GB)).then_inc(stored[u], 16)
                for u in range(2):
                    sp.wait_ge(stored[u], 16 * (TURNS + 1))


def kernel(**inputs):
    import numpy as np
    import concourse.bacc as bacc
    from concourse import mybir as mb
    from concourse.bass_utils import run_bass_kernel_spmd

    a = {k: np.asarray(v) for k, v in inputs.items()}

    def tiles(w):
        return w.reshape(-1, 128, w.shape[1]).transpose(1, 0, 2).reshape(128, -1)

    wih, whh = a["L0_gnn_Wih"].transpose(0, 2, 1), a["L0_gnn_Whh"].transpose(0, 2, 1)
    lstm = np.stack([wih, whh], 1).transpose(2, 0, 1, 3).reshape(128, -1)
    cols = lambda v: v.reshape(-1, 128).T
    arrays = dict(
        x=a["x"], adj=a["adj"],
        gnn_w=np.concatenate([a["adj"].T, a["L0_gnn_Wg0"], a["L0_gnn_Wg1"]], 1),
        lstm_w=lstm,
        late_w=np.concatenate([a["L1_gnn_W1"].T, tiles(a["L1_gnn_W2"].T), a["L2_gnn_W_lin"].T, a["L2_gnn_W_val"].T,
                               a["L2_gnn_W_out"].T, a["L3_gnn_W1"], tiles(a["L3_gnn_W2"]), tiles(a["L3_gnn_W3"])], 1),
        vecs=np.concatenate([cols(a[k]) for k in ("L0_gnn_bih", "L0_gnn_bhh", "L1_gnn_b1", "L1_gnn_g1", "L1_gnn_be1",
                                                  "L1_gnn_b2", "L1_gnn_g2", "L1_gnn_be2", "L2_gnn_a")], 1),
        bg0=a["L0_gnn_bg0"], bg1=a["L0_gnn_bg1"], src=a["L2_gnn_src"], dst=a["L2_gnn_dst"])
    nc = bacc.Bacc("TRN2", target_bir_lowering=False, num_devices=1)
    args, feed = [], {}
    for name, arr in arrays.items():
        arr = np.ascontiguousarray(arr)
        feed[f"in_{name}"] = arr
        args.append(nc.dram_tensor(f"in_{name}", arr.shape, mb.dt.from_np(arr.dtype), kind="ExternalInput").ap())
    args.append(nc.dram_tensor("out", (64, 128, 128), mb.dt.float32, kind="ExternalOutput").ap())
    build(nc, *args)
    r = run_bass_kernel_spmd(nc, [feed], core_ids=[0])
    return r.results[0]["out"]
```

```python
from contextlib import ExitStack

import concourse.bass as bass
from concourse import mybir

F32 = mybir.dt.float32
F32R = mybir.dt.float32r
I32 = mybir.dt.int32
ALU = mybir.AluOpType
ACT = mybir.ActivationFunctionType

B, T, D = 64, 128, 128
GB = 4
GN = GB * T
NG = B // GB
SKIPS = 4
E = 256
ET = E // 128
HEADS = 4
HD = D // HEADS
SLOPE = 0.2
EPS_NORM = 1e-5
EPS_LOG = 1e-8
NEG = -3.0e38
HI, LO = 0, 1

GNN = dict(Wg0=(0, 128), adjT=(128, 256), Wg1=(256, 384))
GNN_COLS = 384
LSTM_COLS = SKIPS * 2 * 4 * D
WHOLE = dict(L1W1=(0, 256), L1W2=(256, 512), WOUT=(512, 640), L3W3=(640, 1152))
WHOLE_COLS = 1152
LATE = dict(QV=(0, 256), L3W1=(256, 512), L3W2=(512, 1536))
LATE_COLS = 1536
V_BIH, V_BHH, V_B1, V_G1, V_BE1, V_B2, V_G2, V_BE2, V_A = 0, 16, 32, 34, 36, 38, 39, 40, 41
VEC_COLS = 42


def f32(ap):
    return ap.bitcast(F32)


class Chain:

    def __init__(self, eng, sem):
        self.eng, self.sem, self.n = eng, sem, 0

    def __call__(self, ins):
        self.n += 1
        ins.then_inc(self.sem, 1)
        self.eng.wait_ge(self.sem, self.n)


def hold(pool, sem, value, passed):
    if not isinstance(value, int) or value > 0:
        pool.wait_ge(sem, value)
        pool.sem_inc(passed, 1)


def slots(eng, depth, body):
    lead = (depth + 3) // 2 * 2
    for i in range(lead):
        body(i, i % 2)
    with eng.Fori(lead // 2, NG // 2) as turn:
        body(2 * turn, 0)
        body(2 * turn + 1, 1)
    for i in range(NG, NG + depth):
        body(i, i % 2)


def live(i, behind):
    return not isinstance(i, int) or 0 <= i - behind < NG


def wait(eng, sem, value):
    if not isinstance(value, int) or value > 0:
        eng.wait_ge(sem, value)


def group4(ap):
    return [ap[:, b * 128:(b + 1) * 128] for b in range(GB)]


def mm3(nc, out, wh, wl, xh, xl, start, stop):
    nc.tensor.matmul(out, wh, xh, start=start, stop=False)
    nc.tensor.matmul(out, wh, xl, start=False, stop=False)
    return nc.tensor.matmul(out, wl, xh, start=False, stop=stop)


def mm_each(nc, out, data, w):
    for o, x in zip(group4(out), group4(data)):
        last = nc.tensor.matmul(o, x, w, start=True, stop=True)
    return last


def take_hi(nc, out, psum, func=ACT.Copy):
    return nc.scalar.activation(out, psum, func)


def take_lo(nc, out, psum, hi, relu=False):
    if relu:
        return nc.vector.scalar_tensor_tensor(out=out, in0=psum, scalar=0.0, in1=f32(hi), op0=ALU.max, op1=ALU.subtract)
    return nc.vector.tensor_tensor(out, psum, f32(hi), ALU.subtract)


class Mem:
    pass


def build(nc, x, xt, adj, gnn_w, lstm_w, whole_w, late_w, vecs, bg0, bg1, src, dst, out):
    with ExitStack() as ctx:
        m = Mem()

        def sb(name, shape, dt=F32):
            return ctx.enter_context(nc.sbuf_tensor(name, shape, dt))

        m.X = sb("X", [128, B, D])
        m.ident = sb("ident", [128, 128])
        m.gnn = sb("gnn", [128, GNN_COLS])
        m.wg1 = sb("wg1", [128, 2, 128], F32R)
        m.ahat = sb("ahat", [128, 128])
        m.adj2 = sb("adj2", [128, 128])
        m.adj2s = sb("adj2s", [128, 2, 128], F32R)
        m.whole = sb("whole", [128, WHOLE_COLS])
        m.late = sb("late", [128, 2, LATE_COLS], F32R)
        m.vec = sb("vec", [128, VEC_COLS])
        m.lbias = sb("lbias", [128, SKIPS * 4])
        m.abd = sb("abd", [128, HEADS])
        m.st = sb("st", [128, E], F32R)
        m.dstn = sb("dstn", [128, E], F32R)
        m.srce = sb("srce", [128, ET, 128])
        m.loga = sb("loga", [128, ET])
        m.same = sb("same", [128, E + 1])
        m.pen = sb("pen", [128, E + 1])
        m.mean = sb("mean", [128, B])
        m.rstd = sb("rstd", [128, B])
        m.ps = ctx.enter_context(nc.psum_tensor("ps", [128, 8, 512], F32))

        with ExitStack() as hctx:
            m.lstm = hctx.enter_context(nc.sbuf_tensor("lstm", [128, 2, LSTM_COLS], F32R))
            m.H = hctx.enter_context(nc.sbuf_tensor("H", [128, 2, B, T], F32R))
            with ExitStack() as actx:
                m.lraw = actx.enter_context(nc.sbuf_tensor("lraw", [128, LSTM_COLS], F32))
                m.bg0 = actx.enter_context(nc.sbuf_tensor("bg0b", [128, 128], F32))
                m.biasrow = actx.enter_context(nc.sbuf_tensor("biasrow", [128, 128], F32R))
                m.rowsum4 = actx.enter_context(nc.sbuf_tensor("rowsum4", [128, GN], F32R))
                m.xt = actx.enter_context(nc.sbuf_tensor("xt", [128, 2, GN], F32))
                setup(nc, m, xt, adj, gnn_w, lstm_w, vecs, bg0, bg1, src, dst)
                l0_gnn(nc, m, xt)
            l0_lstm(nc, m, x, whole_w, late_w)
            l0_residual(nc, m)
        with nc.sbuf_tensor("pre1", [128, 2, B, T], F32) as m.pre1, nc.sbuf_tensor("pre2", [128, B, T], F32) as m.pre2:
            l1(nc, m)
        l2(nc, m)
        l3(nc, m, out)


def setup(nc, m, xt, adj, gnn_w, lstm_w, vecs, bg0, bg1, src, dst):
    with ExitStack() as ctx:
        def sb(name, shape, dt=F32):
            return ctx.enter_context(nc.sbuf_tensor(name, shape, dt))

        def sem(name):
            return ctx.enter_context(nc.semaphore(name))

        adjn = sb("adjn", [128, 128])
        bg1b = sb("bg1b", [128, 128])
        rowsum = sb("rowsum", [128, 128], F32R)
        row_i = sb("row_i", [128, 2, E], I32)
        col_i = sb("col_i", [128, 2, ET], I32)
        rowf = sb("rowf", [128, 2, E])
        colf = sb("colf", [128, 2, ET])
        ones = sb("ones", [128, 128])
        masks = sb("masks", [128, 4])
        node = sb("node", [128, 1])
        rank_no = sb("rank_no", [128, E])
        edge_no = sb("edge_no", [128, ET])
        keyrow = sb("keyrow", [128, E])
        keycol = sb("keycol", [128, ET])
        rank = sb("rank", [128, ET])
        perm = sb("perm", [128, ET, E])
        bcast = sb("bcast", [128, 2, ET, 128])
        sorted_row = sb("sorted_row", [128, 2, E])
        onehot = sb("onehot", [128, 2, E])
        dste = sb("dste", [128, ET, 128])
        edge_adj = sb("edge_adj", [128, ET])
        anorm = sb("anorm", [128, 2, 128])
        sums = sb("sums", [128, 4])
        dinv = sb("dinv", [128, 2])
        half = sb("half", [128, 128])
        rs = sb("rs", [128, 2, 128], F32R)
        bgs = sb("bgs", [128, 2, 128], F32R)
        mix = sb("mix", [128, 2, 128])
        eps_log = sb("eps_log", [128, 1])
        loaded, made, dv, pe, ac = sem("su_loaded"), sem("su_made"), sem("su_dv"), sem("su_pe"), sem("su_ac")
        x_landed, l_landed = sem("su_x"), sem("su_lstm")
        ps = m.ps

        with nc.Block() as block:
            @block.sync
            def _(sp):
                sp.dma_start(m.gnn[:, :], gnn_w).then_inc(loaded, 16)
                sp.dma_start(adjn[:, :], adj).then_inc(loaded, 16)
                sp.dma_start(m.vec[:, :], vecs).then_inc(loaded, 16)
                sp.dma_start(m.bg0[:, :], bg0.partition_broadcast(128)).then_inc(loaded, 16)
                sp.dma_start(bg1b[:, :], bg1.partition_broadcast(128)).then_inc(loaded, 16)
                for k, ids in enumerate((src, dst)):
                    sp.dma_start(row_i[:, k, :], ids.partition_broadcast(128)).then_inc(loaded, 16)
                    sp.dma_start(col_i[:, k, :], ids.rearrange("(n a) -> n a", a=ET)).then_inc(loaded, 16)
                for g in range(2):
                    sp.dma_start(m.xt[:, g, :], xt[:, g * GN:(g + 1) * GN]).then_inc(x_landed, 16)
                sp.dma_start(m.lraw[:, :], lstm_w).then_inc(l_landed, 16)
                sp.wait_ge(x_landed, 32)
                sp.wait_ge(l_landed, 16)

            @block.gpsimd
            def _(pool):
                chain = Chain(pool, made)
                chain(nc.gpsimd.memset(m.ident[:, :], 0.0))
                chain(nc.gpsimd.affine_select(out=m.ident[:, :], in_=m.ident[:, :], compare_op=ALU.not_equal, fill=1.0,
                                              base=0, pattern=[[-1, 128]], channel_multiplier=1))
                chain(nc.gpsimd.iota(node[:, :], pattern=[[0, 1]], base=0, channel_multiplier=1,
                                     allow_small_or_imprecise_dtypes=True))
                chain(nc.gpsimd.iota(rank_no[:, :], pattern=[[1, E]], base=0, channel_multiplier=0,
                                     allow_small_or_imprecise_dtypes=True))
                chain(nc.gpsimd.iota(edge_no[:, :], pattern=[[1, ET]], base=0, channel_multiplier=ET,
                                     allow_small_or_imprecise_dtypes=True))
                chain(nc.gpsimd.memset(ones[:, :], 1.0))
                chain(nc.gpsimd.memset(eps_log[:, :], EPS_LOG))
                chain(nc.gpsimd.memset(bcast[:, :, :, :], 0.0))
                chain(nc.gpsimd.memset(m.abd[:, :], 1.0))
                chain(nc.gpsimd.affine_select(out=m.abd[:, :], in_=m.abd[:, :], compare_op=ALU.is_ge, fill=0.0,
                                              base=0, pattern=[[-HD, HEADS]], channel_multiplier=1))
                chain(nc.gpsimd.affine_select(out=m.abd[:, :], in_=m.abd[:, :], compare_op=ALU.is_ge, fill=0.0,
                                              base=HD - 1, pattern=[[HD, HEADS]], channel_multiplier=-1))

            @block.vector
            def _(v):
                chain = Chain(v, dv)
                v.wait_ge(loaded, 9 * 16)
                v.wait_ge(made, 11)
                w1 = m.gnn[:, GNN["Wg1"][0]:GNN["Wg1"][1]]
                adj_t = m.gnn[:, GNN["adjT"][0]:GNN["adjT"][1]]
                chain(nc.vector.tensor_copy(m.wg1[:, HI, :], w1))
                chain(nc.vector.tensor_tensor(m.wg1[:, LO, :], w1, f32(m.wg1[:, HI, :]), ALU.subtract))
                chain(nc.vector.tensor_tensor(m.adj2[:, :], adj_t, adj_t, ALU.mult))
                chain(nc.vector.tensor_copy(m.adj2s[:, HI, :], m.adj2[:, :]))
                chain(nc.vector.tensor_tensor(m.adj2s[:, LO, :], m.adj2[:, :], f32(m.adj2s[:, HI, :]), ALU.subtract))
                chain(nc.vector.tensor_tensor(m.lbias[:, :], m.vec[:, V_BIH:V_BIH + 16], m.vec[:, V_BHH:V_BHH + 16], ALU.add))
                chain(nc.vector.tensor_scalar(m.abd[:, :], m.abd[:, :], m.vec[:, V_A:V_A + 1], None, ALU.mult))
                chain(nc.vector.tensor_tensor(anorm[:, 0, :], adjn[:, :], m.ident[:, :], ALU.add))
                chain(nc.vector.tensor_tensor(anorm[:, 1, :], adj_t, m.ident[:, :], ALU.add))
                chain(nc.vector.reduce_sum(sums[:, 0:1], anorm[:, 0, :], mybir.AxisListType.X))
                chain(nc.vector.reduce_sum(sums[:, 1:2], anorm[:, 1, :], mybir.AxisListType.X))
                chain(nc.vector.tensor_tensor(half[:, :], anorm[:, 0, :], m.ident[:, :], ALU.mult))
                chain(nc.vector.reduce_sum(sums[:, 2:3], half[:, :], mybir.AxisListType.X))
                chain(nc.vector.tensor_tensor(sums[:, 0:1], sums[:, 0:1], sums[:, 1:2], ALU.add))
                chain(nc.vector.tensor_tensor(sums[:, 3:4], sums[:, 0:1], sums[:, 2:3], ALU.subtract))
                chain(nc.vector.reciprocal(dinv[:, 0:1], sums[:, 3:4]))
                chain(nc.vector.tensor_copy(rowf[:, :, :], row_i[:, :, :]))
                chain(nc.vector.tensor_copy(colf[:, :, :], col_i[:, :, :]))
                chain(nc.vector.scalar_tensor_tensor(out=keyrow[:, :], in0=rowf[:, 0, :], scalar=float(E), in1=rank_no[:, :],
                                                     op0=ALU.mult, op1=ALU.add))
                chain(nc.vector.scalar_tensor_tensor(out=keycol[:, :], in0=colf[:, 0, :], scalar=float(E), in1=edge_no[:, :],
                                                     op0=ALU.mult, op1=ALU.add))
                for t in range(ET):
                    chain(nc.vector.tensor_scalar(perm[:, t, :], keyrow[:, :], keycol[:, t:t + 1], None, ALU.is_lt,
                                                  ALU.add, accum_out=rank[:, t:t + 1]))
                for t in range(ET):
                    chain(nc.vector.tensor_scalar(perm[:, t, :], rank_no[:, :], rank[:, t:t + 1], None, ALU.is_equal))
                for k in range(2):
                    for t in range(ET):
                        chain(nc.vector.tensor_scalar(bcast[:, k, t, :], ones[:, :], colf[:, k, t:t + 1], None, ALU.mult))
                v.wait_ge(pe, 1)
                chain(nc.vector.tensor_copy(sorted_row[:, :, :], ps[:, 0, :].rearrange("p (k e) -> p k e", k=2)))
                for k in range(2):
                    chain(nc.vector.tensor_scalar(onehot[:, k, :], sorted_row[:, k, :], node[:, 0:1], None, ALU.is_equal))
                chain(nc.vector.tensor_tensor(m.st[:, :], onehot[:, 0, :], onehot[:, 1, :], ALU.add))
                chain(nc.vector.tensor_copy(m.dstn[:, :], onehot[:, 1, :]))
                chain(nc.vector.memset(m.same[:, :], 0.0))
                chain(nc.vector.tensor_tensor(m.same[:, 1:E], sorted_row[:, 0, 1:E], sorted_row[:, 0, 0:E - 1], ALU.is_equal))
                chain(nc.vector.tensor_scalar(m.pen[:, :], m.same[:, :], -1.0, -NEG, ALU.add, ALU.mult))
                v.wait_ge(pe, 2)
                chain(nc.vector.tensor_copy(m.srce[:, :, :], ps[:, 1, 0:E].rearrange("p (t n) -> p t n", t=ET)))
                chain(nc.vector.tensor_copy(dste[:, :, :], ps[:, 1, E:2 * E].rearrange("p (t n) -> p t n", t=ET)))
                v.wait_ge(pe, 3)
                chain(nc.vector.tensor_tensor(perm[:, :, 0:128], ps[:, 2, 0:E].rearrange("p (t n) -> p t n", t=ET),
                                              dste[:, :, :], ALU.mult))
                chain(nc.vector.reduce_sum(edge_adj[:, :], perm[:, :, 0:128], mybir.AxisListType.X))
                v.wait_ge(ac, 1)
                chain(nc.vector.tensor_scalar(half[:, :], anorm[:, 0, :], dinv[:, 1:2], None, ALU.mult))
                v.wait_ge(pe, 4)
                chain(nc.vector.tensor_scalar(m.ahat[:, :], ps[:, 3, 0:128], dinv[:, 1:2], None, ALU.mult))
                chain(nc.vector.tensor_copy(masks[:, 0:1], m.ident[:, 0:1]))
                chain(nc.vector.tensor_tensor(masks[:, 0:1], masks[:, 0:1], m.ident[:, 1:2], ALU.add))
                chain(nc.vector.tensor_tensor(masks[:, 2:3], m.ident[:, 0:1], m.ident[:, 2:3], ALU.add))
                v.wait_ge(pe, 5)
                chain(nc.vector.tensor_copy(rs[:, HI, :], ps[:, 4, 0:128]))
                chain(nc.vector.tensor_tensor(rs[:, LO, :], ps[:, 4, 0:128], f32(rs[:, HI, :]), ALU.subtract))
                chain(nc.vector.tensor_scalar(mix[:, 0, :], f32(rs[:, LO, :]), m.ident[:, 2:3], None, ALU.mult))
                chain(nc.vector.scalar_tensor_tensor(out=rowsum[:, :], in0=f32(rs[:, HI, :]), scalar=masks[:, 0:1],
                                                     in1=mix[:, 0, :], op0=ALU.mult, op1=ALU.add))
                for b in range(GB):
                    chain(nc.vector.tensor_copy(m.rowsum4[:, b * 128:(b + 1) * 128], f32(rowsum[:, :])))
                chain(nc.vector.tensor_copy(bgs[:, HI, :], bg1b[:, :]))
                chain(nc.vector.tensor_tensor(bgs[:, LO, :], bg1b[:, :], f32(bgs[:, HI, :]), ALU.subtract))
                chain(nc.vector.tensor_scalar(mix[:, 1, :], f32(bgs[:, LO, :]), m.ident[:, 1:2], None, ALU.mult))
                chain(nc.vector.scalar_tensor_tensor(out=m.biasrow[:, :], in0=f32(bgs[:, HI, :]),
                                                     scalar=masks[:, 2:3], in1=mix[:, 1, :], op0=ALU.mult, op1=ALU.add))

            @block.scalar
            def _(act):
                act.wait_ge(dv, 16)
                nc.scalar.activation(dinv[:, 1:2], dinv[:, 0:1], ACT.Sqrt).then_inc(ac, 1)
                act.wait_ge(dv, 40)
                nc.scalar.activation(m.loga[:, :], edge_adj[:, :], ACT.Ln, bias=eps_log[:, 0:1]).then_inc(ac, 1)

            @block.tensor
            def _(t_):
                t_.wait_ge(dv, 28)
                for k in range(2):
                    for t in range(ET):
                        last = nc.tensor.matmul(ps[:, 0, k * E:(k + 1) * E], bcast[:, k, t, :], perm[:, t, :],
                                                start=(t == 0), stop=(t == ET - 1))
                last.then_inc(pe, 1)
                t_.wait_ge(dv, 33)
                for k in range(2):
                    for t in range(ET):
                        last = nc.tensor.transpose(ps[:, 1, (k * ET + t) * 128:(k * ET + t + 1) * 128],
                                                   onehot[:, k, t * 128:(t + 1) * 128], m.ident[:, :])
                last.then_inc(pe, 1)
                for t in range(ET):
                    last = nc.tensor.matmul(ps[:, 2, t * 128:(t + 1) * 128], onehot[:, 0, t * 128:(t + 1) * 128],
                                            adjn[:, :], start=True, stop=True)
                last.then_inc(pe, 1)
                t_.wait_ge(dv, 41)
                nc.tensor.transpose(ps[:, 3, 0:128], half[:, :], m.ident[:, :]).then_inc(pe, 1)
                nc.tensor.matmul(ps[:, 4, 0:128], ones[:, :], m.gnn[:, GNN["adjT"][0]:GNN["adjT"][1]], start=True,
                                 stop=True).then_inc(pe, 1)


def l0_gnn(nc, m, xt):
    with ExitStack() as ctx:
        def sb(name, shape, dt=F32):
            return ctx.enter_context(nc.sbuf_tensor(name, shape, dt))

        def sem(name):
            return ctx.enter_context(nc.semaphore(name))

        xw = sb("a_xw", [128, GN])
        h = sb("a_h", [128, GN])
        ah = sb("a_ah", [128, 2, GN], F32R)
        prod = [sem(f"a_prod{s}") for s in range(4)]
        xw_ready, h_ready, ah_hi, ah_lo, H_hi, H_lo, w_hi, w_lo, passed = [sem(f"a_{n}") for n in (
            "xw", "h", "ah_hi", "ah_lo", "H_hi", "H_lo", "w_hi", "w_lo", "passed")]
        landed = [sem(f"a_landed{u}") for u in range(2)]
        H = m.H[:, :, :, :].rearrange("p k (g b) t -> p k g (b t)", b=GB)
        lstm = m.lstm[:, :, :].rearrange("p k (g c) -> p k g c", g=NG)
        lraw = m.lraw[:, :].rearrange("p (g c) -> p g c", g=NG)
        xtd = xt.rearrange("p (g c) -> p g c", c=GN)
        ps = m.ps
        w0, adj_t = [m.gnn[:, GNN[n][0]:GNN[n][1]] for n in ("Wg0", "adjT")]
        DEPTH = 3

        with nc.Block() as block:
            @block.sync
            def _(sp):
                def slot(i, parity):
                    if not isinstance(i, int) or 2 <= i < NG:
                        sp.wait_ge(prod[0], i - 1)
                        sp.dma_start(m.xt[:, parity, :], xtd[:, i, :]).then_inc(landed[parity], 16)
                slots(sp, DEPTH, slot)
                for u in range(2):
                    sp.wait_ge(landed[u], 16 * (NG // 2 - 1))

            @block.tensor
            def _(pe):
                def slot(i, parity):
                    if live(i, 3):
                        pe.wait_ge(ah_lo, i - 2)
                        wait(pe, H_lo, i - 3)
                        nc.tensor.matmul(ps[:, 3, :], m.biasrow[:, :], m.rowsum4[:, :], start=True, stop=False)
                        mm3(nc, ps[:, 3, :], m.wg1[:, HI, :], m.wg1[:, LO, :], ah[:, HI, :], ah[:, LO, :], False,
                            True).then_inc(prod[3], 1)
                    if live(i, 2):
                        pe.wait_ge(h_ready, i - 1)
                        mm_each(nc, ps[:, 2, :], h, adj_t).then_inc(prod[2], 1)
                    if live(i, 1):
                        pe.wait_ge(xw_ready, i)
                        nc.tensor.matmul(ps[:, 1, :], adj_t, xw[:, :], start=True, stop=True).then_inc(prod[1], 1)
                    if live(i, 0):
                        wait(pe, landed[parity], 8 * (i - parity))
                        mm_each(nc, ps[:, 0, :], m.xt[:, parity, :], w0).then_inc(prod[0], 1)
                slots(pe, DEPTH, slot)

            @block.scalar
            def _(act):
                def slot(i, parity):
                    if live(i, 3):
                        act.wait_ge(prod[3], i - 2)
                        take_hi(nc, H[:, HI, i - 3, :], ps[:, 3, :], ACT.Relu).then_inc(H_hi, 1)
                    if live(i, 2):
                        act.wait_ge(prod[2], i - 1)
                        take_hi(nc, ah[:, HI, :], ps[:, 2, :]).then_inc(ah_hi, 1)
                    if live(i, 1):
                        act.wait_ge(prod[1], i)
                        nc.scalar.activation(h[:, :], ps[:, 1, :], ACT.Relu).then_inc(h_ready, 1)
                slots(act, DEPTH, slot)

            @block.vector
            def _(v):
                def slot(i, parity):
                    if live(i, 3):
                        v.wait_ge(H_hi, i - 2)
                        take_lo(nc, H[:, LO, i - 3, :], ps[:, 3, :], H[:, HI, i - 3, :], relu=True).then_inc(H_lo, 1)
                    if live(i, 2):
                        v.wait_ge(ah_hi, i - 1)
                        take_lo(nc, ah[:, LO, :], ps[:, 2, :], ah[:, HI, :]).then_inc(ah_lo, 1)
                    if live(i, 0):
                        nc.vector.tensor_copy(lstm[:, HI, i, :], lraw[:, i, :]).then_inc(w_hi, 1)
                        wait(v, prod[1], i)
                        v.wait_ge(prod[0], i + 1)
                        nc.vector.tensor_tensor(xw[:, :].rearrange("p (b d) -> p b d", b=GB),
                                                ps[:, 0, :].rearrange("p (b d) -> p b d", b=GB),
                                                m.bg0[:, :].unsqueeze(1).broadcast_to([128, GB, 128]),
                                                ALU.add).then_inc(xw_ready, 1)
                slots(v, DEPTH, slot)

            @block.gpsimd
            def _(pool):
                def slot(i, parity):
                    if live(i, 0):
                        hold(pool, w_hi, i + 1, passed)
                        nc.gpsimd.tensor_tensor(lstm[:, LO, i, :], lraw[:, i, :], f32(lstm[:, HI, i, :]),
                                                ALU.subtract).then_inc(w_lo, 1)
                slots(pool, DEPTH, slot)


def l0_lstm(nc, m, x, whole_w, late_w):
    with ExitStack() as ctx:
        def sb(name, shape, dt=F32):
            return ctx.enter_context(nc.sbuf_tensor(name, shape, dt))

        gates = sb("gates", [128, 2, 4, 512])
        ig = sb("ig", [128, 2, 512])
        fc = sb("fc", [128, 2, 512])
        cell = sb("cell", [128, 2, 512])
        tanc = sb("tanc", [128, 2, 512])
        hf = sb("hf", [128, 2, 512])
        hs = sb("hs", [128, 2, 2, 512], F32R)
        CUTS = 4
        LC = LATE_COLS // CUTS
        raw = sb("late_raw", [128, LC])
        raw_landed, wsplit = [ctx.enter_context(nc.semaphore(f"b_{n}")) for n in ("raw", "wsplit")]
        x_landed = ctx.enter_context(nc.semaphore("b_x"))
        ps = m.ps

        class Loop:

            def __init__(self, p):
                self.p, self.nw = p, T // p
                self.nb = {1: 4, 2: 8, 3: 8, 4: 16}[p]
                self.n = self.nb * self.nw
                self.turns = B // self.nb // 2
                self.steps = 2 * p
                self.order = [(s, q) for s in range(p) for q in range(2)]
                self.gates = [(0, 2, 3) if s == 0 else (0, 2, 1, 3) for s, q in self.order]
                self.before = [sum(len(g) for g in self.gates[:k]) for k in range(self.steps + 1)]
                self.per = self.before[-1]
                self.gate_prod, self.gate_act, self.cell_done, self.tanh_done, self.h_done, self.dve = [
                    ctx.enter_context(nc.semaphore(f"b{p}_{n}"))
                    for n in ("gate_prod", "gate_act", "cell", "tanh", "h", "dve")]
                self.own = sum(2 if s == 0 else 4 for s, q in self.order)
                self.H = m.H[:, :, :, 0:self.nw * p].rearrange("a k (i q b) (w j) -> a k i q b w j", q=2, b=self.nb, j=p)

            def cols(self, ap):
                return ap.rearrange("a (b w) -> a b w", w=self.nw)

        loops = [Loop(p) for p in range(1, SKIPS + 1)]

        with nc.Block() as block:
            @block.sync
            def _(sp):
                for k in range(CUTS):
                    if k:
                        sp.wait_ge(wsplit, 2 * k)
                    sp.dma_start(raw[:, :], late_w[:, k * LC:(k + 1) * LC]).then_inc(raw_landed, 16)
                sp.dma_start(m.whole[:, :], whole_w).then_inc(x_landed, 16)
                for k in range(4):
                    c = slice(k * B // 4, (k + 1) * B // 4)
                    sp.dma_start(m.X[:, c, :], x[c].rearrange("b n d -> n b d")).then_inc(x_landed, 16)
                sp.wait_ge(x_landed, 16 * 5)

            @block.gpsimd
            def _(pool):
                for k in range(CUTS):
                    c = slice(k * LC, (k + 1) * LC)
                    pool.wait_ge(raw_landed, 16 * (k + 1))
                    nc.gpsimd.tensor_copy(m.late[:, HI, c], raw[:, :]).then_inc(wsplit, 1)
                    pool.wait_ge(wsplit, 2 * k + 1)
                    nc.gpsimd.tensor_tensor(m.late[:, LO, c], raw[:, :], f32(m.late[:, HI, c]), ALU.subtract).then_inc(wsplit, 1)

            @block.tensor
            def _(pe):
                for L in loops:
                    if L.p > 1:
                        P = loops[L.p - 2]
                        pe.wait_ge(P.h_done, P.steps * (P.turns + 1))
                    W = m.lstm[:, :, :].rearrange("a k (p w g c) -> a k p w g c", p=SKIPS, w=2, g=4)
                    with pe.Fori(0, L.turns) as i:
                        for k, (s, q) in enumerate(L.order):
                            free = L.before[k - 1] if k >= 2 else L.before[L.steps - 1 + k] - L.per
                            pe.wait_ge(L.gate_act, L.per * i + free + L.per)
                            xh, xl = [L.H[:, j, i, q, :, :, s] for j in (HI, LO)]
                            for g in L.gates[k]:
                                out_ = L.cols(ps[:, 4 * q + g, 0:L.n])
                                last = mm3(nc, out_, W[:, HI, L.p - 1, 0, g, :], W[:, LO, L.p - 1, 0, g, :], xh, xl,
                                           True, s == 0)
                                if s == 0:
                                    last.then_inc(L.gate_prod, 1)
                            if s:
                                pe.wait_ge(L.h_done, L.steps * i + k - 1 + L.steps)
                                for g in L.gates[k]:
                                    mm3(nc, ps[:, 4 * q + g, 0:L.n], W[:, HI, L.p - 1, 1, g, :],
                                        W[:, LO, L.p - 1, 1, g, :], hs[:, q, HI, 0:L.n], hs[:, q, LO, 0:L.n],
                                        False, True).then_inc(L.gate_prod, 1)

            @block.scalar
            def _(act):
                for L in loops:
                    act.sem_inc(L.gate_act, L.per)
                    with act.Fori(0, L.turns) as i:
                        for k, (s, q) in enumerate(L.order):
                            act.wait_ge(L.h_done, L.steps * i + k - 1 + L.steps)
                            for j, g in enumerate(L.gates[k]):
                                act.wait_ge(L.gate_prod, L.per * i + L.before[k] + j + 1)
                                col = 4 * (L.p - 1) + g
                                nc.scalar.activation(gates[:, q, g, 0:L.n], ps[:, 4 * q + g, 0:L.n],
                                                     ACT.Tanh if g == 2 else ACT.Sigmoid,
                                                     bias=m.lbias[:, col:col + 1]).then_inc(L.gate_act, 1)
                            act.wait_ge(L.cell_done, L.steps * i + k + 1)
                            nc.scalar.activation(tanc[:, q, 0:L.n], cell[:, q, 0:L.n], ACT.Tanh).then_inc(L.tanh_done, 1)

            @block.vector
            def _(v):
                for L in loops:
                    v.sem_inc(L.h_done, L.steps)
                    with v.Fori(0, L.turns) as i:
                        done = 0
                        for k, (s, q) in enumerate(L.order):
                            g_ = [gates[:, q, g, 0:L.n] for g in range(4)]
                            c_ = cell[:, q, 0:L.n]
                            acts = L.per * i + L.before[k] + L.per
                            v.wait_ge(L.gate_act, acts + 2)
                            if s == 0:
                                nc.vector.tensor_tensor(c_, g_[0], g_[2], ALU.mult).then_inc(L.cell_done, 1)
                            else:
                                nc.vector.tensor_tensor(ig[:, q, 0:L.n], g_[0], g_[2], ALU.mult).then_inc(L.dve, 1)
                                v.wait_ge(L.gate_act, acts + 3)
                                nc.vector.tensor_tensor(fc[:, q, 0:L.n], g_[1], c_, ALU.mult).then_inc(L.dve, 1)
                                done += 2
                                v.wait_ge(L.dve, L.own * i + done)
                                nc.vector.tensor_tensor(c_, ig[:, q, 0:L.n], fc[:, q, 0:L.n], ALU.add).then_inc(L.cell_done, 1)
                            v.wait_ge(L.tanh_done, L.steps * i + k + 1)
                            nc.vector.tensor_tensor(hf[:, q, 0:L.n], g_[3], tanc[:, q, 0:L.n], ALU.mult).then_inc(L.dve, 1)
                            done += 1
                            v.wait_ge(L.dve, L.own * i + done)
                            if s == L.p - 1:
                                hi_, lo_ = [L.H[:, j, i, q, :, :, s] for j in (HI, LO)]
                                new = L.cols(hf[:, q, 0:L.n])
                            else:
                                hi_, lo_ = [hs[:, q, j, 0:L.n] for j in (HI, LO)]
                                new = hf[:, q, 0:L.n]
                            nc.vector.tensor_copy(hi_, new).then_inc(L.dve, 1)
                            done += 1
                            v.wait_ge(L.dve, L.own * i + done)
                            nc.vector.tensor_tensor(lo_, new, f32(hi_), ALU.subtract).then_inc(L.h_done, 1)
                        assert done == L.own


def finish_norm(nc, v, m, stats, ctx, tag, rec):
    chain = Chain(v, ctx.enter_context(nc.semaphore(f"{tag}_gather")))
    S = stats[:, :, :]
    t = ctx.enter_context(nc.sbuf_tensor(f"{tag}_t", [128, 2, B], F32))
    chain(nc.vector.tensor_tensor(t[:, 0, :], S[:, :, 1], S[:, :, 4], ALU.subtract))
    chain(nc.vector.tensor_tensor(t[:, 1, :], S[:, :, 2], S[:, :, 5], ALU.add))
    chain(nc.vector.tensor_tensor(m.mean[:, :], S[:, :, 1], S[:, :, 4], ALU.add))
    chain(nc.vector.tensor_scalar(m.mean[:, :], m.mean[:, :], 0.5, None, ALU.mult))
    chain(nc.vector.tensor_tensor(t[:, 0, :], t[:, 0, :], t[:, 0, :], ALU.mult))
    chain(nc.vector.scalar_tensor_tensor(out=t[:, 1, :], in0=t[:, 0, :], scalar=float(D // 4), in1=t[:, 1, :],
                                         op0=ALU.mult, op1=ALU.add))
    chain(nc.vector.tensor_scalar(m.rstd[:, :], t[:, 1, :], 1.0 / D, EPS_NORM, ALU.mult, ALU.add))
    nc.vector.reciprocal(m.rstd[:, :], m.rstd[:, :]).then_inc(rec, 1)


def root_norm(nc, act, m, rec, root):
    act.wait_ge(rec, 1)
    nc.scalar.activation(m.rstd[:, :], m.rstd[:, :], ACT.Sqrt).then_inc(root, 1)


def norm_group(nc, m, out, y, g):
    mean = m.mean[:, :].rearrange("p (g b) -> p g b", b=GB)
    rstd = m.rstd[:, :].rearrange("p (g b) -> p g b", b=GB)
    for b, (o, x) in enumerate(zip(group4(out), group4(y))):
        last = nc.vector.tensor_scalar(o, x, mean[:, g, b:b + 1], rstd[:, g, b:b + 1], ALU.subtract, ALU.mult)
    return last


def add_and_count(nc, v, X, ps, stats, g, added, counted):
    nc.vector.tensor_tensor(X[:, g, :], ps, X[:, g, :], ALU.add).then_inc(added, 1)
    v.wait_ge(added, g + 1)
    S = stats[:, :, :].rearrange("p (g b) s -> p g b s", b=GB)
    for b, x in enumerate(group4(X[:, g, :])):
        last = nc.vector.bn_stats(S[:, g, b, :], x)
    last.then_inc(counted, 1)


def l0_residual(nc, m):
    with ExitStack() as ctx:
        hsum = ctx.enter_context(nc.sbuf_tensor("hsum", [128, 2, GN], F32))
        stats = ctx.enter_context(nc.sbuf_tensor("r_stats", [128, B, 6], F32))
        summed, turned, added, counted, rec, root, passed = [
            ctx.enter_context(nc.semaphore(f"r_{n}")) for n in ("sum", "turn", "add", "count", "rec", "root", "passed")]
        H = m.H[:, :, :, :].rearrange("p k (g b) t -> p k g (b t)", b=GB)
        X = m.X[:, :, :].rearrange("p (g b) d -> p g (b d)", b=GB)
        ps = m.ps
        DEPTH = 2

        with nc.Block() as block:
            @block.gpsimd
            def _(pool):
                def slot(i, parity):
                    if live(i, 0):
                        hold(pool, turned, i - 1, passed)
                        nc.gpsimd.tensor_tensor(hsum[:, parity, :], f32(H[:, HI, i, :]), f32(H[:, LO, i, :]),
                                                ALU.add).then_inc(summed, 1)
                slots(pool, DEPTH, slot)

            @block.tensor
            def _(pe):
                def slot(i, parity):
                    if live(i, 1):
                        g, q = i - 1, (parity + 1) % 2
                        wait(pe, added, g - 1)
                        pe.wait_ge(summed, g + 1)
                        for o, h in zip(group4(ps[:, q, :]), group4(hsum[:, q, :])):
                            last = nc.tensor.transpose(o, h, m.ident[:, :])
                        last.then_inc(turned, 1)
                slots(pe, DEPTH, slot)

            @block.vector
            def _(v):
                def slot(i, parity):
                    if live(i, 2):
                        v.wait_ge(turned, i - 1)
                        add_and_count(nc, v, X, ps[:, parity, :], stats, i - 2, added, counted)
                slots(v, DEPTH, slot)
                v.wait_ge(counted, NG)
                finish_norm(nc, v, m, stats, ctx, "r", rec)

            @block.scalar
            def _(act):
                root_norm(nc, act, m, rec, root)


def late(m, name, k, a=0, b=None):
    c0, c1 = LATE[name]
    return m.late[:, k, c0 + a:(c1 if b is None else c0 + b)]


def whole(m, name, tile=0, width=128):
    return m.whole[:, WHOLE[name][0] + tile * width:WHOLE[name][0] + (tile + 1) * width]


def batch_coef(nc, v, act_wait, chain, stats, gamma, beta, scale, shift, tmp, rec_sem, root_sem):
    chain(nc.vector.bn_aggr(tmp[:, 0:2], stats))
    chain(nc.vector.tensor_scalar(tmp[:, 2:3], tmp[:, 1:2], EPS_NORM, None, ALU.add))
    nc.vector.reciprocal(tmp[:, 3:4], tmp[:, 2:3]).then_inc(rec_sem, 1)
    v.wait_ge(root_sem, act_wait)
    chain(nc.vector.tensor_tensor(scale, gamma, tmp[:, 4:5], ALU.mult))
    chain(nc.vector.tensor_tensor(tmp[:, 5:6], tmp[:, 0:1], scale, ALU.mult))
    chain(nc.vector.tensor_tensor(shift, beta, tmp[:, 5:6], ALU.subtract))


def l1(nc, m):
    with ExitStack() as ctx:
        def sb(name, shape, dt=F32):
            return ctx.enter_context(nc.sbuf_tensor(name, shape, dt))

        def sem(name):
            return ctx.enter_context(nc.semaphore(name))

        xs = sb("c_xs", [128, 2, GN])
        agg = sb("c_agg", [128, GN])
        st1 = sb("c_st1", [128, 2, NG, 6])
        st2 = sb("c_st2", [128, NG, 6])
        coef = sb("c_coef", [128, 2, 3])
        tmp = sb("c_tmp", [128, 3, 8])
        stats = sb("c_stats", [128, B, 6])
        X = m.X[:, :, :].rearrange("p (g b) d -> p g (b d)", b=GB)
        pre1 = m.pre1[:, :, :, :].rearrange("p k (g b) t -> p k g (b t)", b=GB)
        pre2 = m.pre2[:, :, :].rearrange("p (g b) t -> p g (b t)", b=GB)
        ps = m.ps

        normed, stored, agged, copied, wide, kept, counted = [sem(f"c1_{n}") for n in (
            "normed", "stored", "agged", "copied", "wide", "kept", "counted")]
        rec, root, chs = sem("c1_rec"), sem("c1_root"), sem("c1_chain")
        with nc.Block() as block:
            @block.vector
            def _(v):
                def slot(i, parity):
                    if live(i, 0):
                        wait(v, agged, i - 1)
                        wait(v, stored, i - 1)
                        norm_group(nc, m, xs[:, parity, :], X[:, i, :], i).then_inc(normed, 1)
                    if live(i, 2):
                        for t in range(2):
                            v.wait_ge(kept, 2 * (i - 2) + t + 1)
                            nc.vector.bn_stats(st1[:, t, i - 2, :], pre1[:, t, i - 2, :]).then_inc(counted, 1)
                slots(v, 2, slot)
                v.wait_ge(counted, 2 * NG)
                chain = Chain(v, chs)
                for t in range(2):
                    batch_coef(nc, v, t + 1, chain, st1[:, t, :, :].rearrange("p g s -> p (g s)"),
                               m.vec[:, V_G1 + t:V_G1 + t + 1], m.vec[:, V_BE1 + t:V_BE1 + t + 1],
                               coef[:, 0, t:t + 1], coef[:, 1, t:t + 1], tmp[:, t, :], rec, root)

            @block.scalar
            def _(act):
                def slot(i, parity):
                    if live(i, 2):
                        for t in range(2):
                            act.wait_ge(wide, 2 * (i - 2) + t + 1)
                            nc.scalar.activation(pre1[:, t, i - 2, :], ps[:, 2 * parity + 2 + t, :], ACT.Identity,
                                                 bias=m.vec[:, V_B1 + t:V_B1 + t + 1]).then_inc(kept, 1)
                    if live(i, 1):
                        act.wait_ge(agged, i)
                        nc.scalar.activation(agg[:, :], ps[:, 0, :], ACT.Copy).then_inc(copied, 1)
                    if live(i, 0):
                        act.wait_ge(normed, i + 1)
                        nc.scalar.activation(X[:, i, :], xs[:, parity, :], ACT.Copy).then_inc(stored, 1)
                slots(act, 2, slot)
                for t in range(2):
                    act.wait_ge(rec, t + 1)
                    nc.scalar.activation(tmp[:, t, 4:5], tmp[:, t, 3:4], ACT.Sqrt).then_inc(root, 1)

            @block.tensor
            def _(pe):
                def slot(i, parity):
                    if live(i, 2):
                        g = i - 2
                        pe.wait_ge(copied, g + 1)
                        wait(pe, kept, 2 * (g - 1))
                        for t in range(2):
                            nc.tensor.matmul(ps[:, 2 * parity + 2 + t, :], whole(m, "L1W1", t), agg[:, :],
                                             start=True, stop=True).then_inc(wide, 1)
                    if live(i, 1):
                        pe.wait_ge(normed, i)
                        mm_each(nc, ps[:, 0, :], xs[:, (parity + 1) % 2, :], m.ahat[:, :]).then_inc(agged, 1)
                slots(pe, 2, slot)

        hid = sb("c_hid", [128, 2, 2, GN])
        relu, prod, kept2, counted2, rec2, root2, chs2 = [sem(f"c2_{n}") for n in (
            "relu", "prod", "kept", "counted", "rec", "root", "chain")]
        with nc.Block() as block:
            @block.scalar
            def _(act):
                def slot(i, parity):
                    if live(i, 0):
                        wait(act, prod, i - 1)
                        for t in range(2):
                            nc.scalar.activation(hid[:, parity, t, :], pre1[:, t, i, :], ACT.Relu, bias=coef[:, 1, t:t + 1],
                                                 scale=coef[:, 0, t:t + 1]).then_inc(relu, 1)
                slots(act, 1, slot)
                act.wait_ge(rec2, 1)
                nc.scalar.activation(tmp[:, 2, 4:5], tmp[:, 2, 3:4], ACT.Sqrt).then_inc(root2, 1)

            @block.vector
            def _(v):
                def slot(i, parity):
                    if live(i, 1):
                        v.wait_ge(prod, i)
                        nc.vector.tensor_scalar(pre2[:, i - 1, :], ps[:, (parity + 1) % 2, :], m.vec[:, V_B2:V_B2 + 1],
                                                None, ALU.add).then_inc(kept2, 1)
                        v.wait_ge(kept2, i)
                        nc.vector.bn_stats(st2[:, i - 1, :], pre2[:, i - 1, :]).then_inc(counted2, 1)
                slots(v, 1, slot)
                v.wait_ge(counted2, NG)
                batch_coef(nc, v, 1, Chain(v, chs2), st2[:, :, :].rearrange("p g s -> p (g s)"),
                           m.vec[:, V_G2:V_G2 + 1], m.vec[:, V_BE2:V_BE2 + 1], coef[:, 0, 2:3], coef[:, 1, 2:3],
                           tmp[:, 2, :], rec2, root2)

            @block.tensor
            def _(pe):
                def slot(i, parity):
                    if live(i, 1):
                        q = (parity + 1) % 2
                        pe.wait_ge(relu, 2 * i)
                        wait(pe, kept2, i - 2)
                        for t in range(2):
                            last = nc.tensor.matmul(ps[:, q, :], whole(m, "L1W2", t), hid[:, q, t, :], start=t == 0,
                                                    stop=t == 1)
                        last.then_inc(prod, 1)
                slots(pe, 1, slot)

        z = sb("c_z", [128, 2, GN])
        scaled, turned, added, counted3, rec3, root3 = [sem(f"c3_{n}") for n in (
            "scaled", "turned", "added", "counted", "rec", "root")]
        with nc.Block() as block:
            @block.scalar
            def _(act):
                def slot(i, parity):
                    if live(i, 0):
                        wait(act, turned, i - 1)
                        nc.scalar.activation(z[:, parity, :], pre2[:, i, :], ACT.Identity, bias=coef[:, 1, 2:3],
                                             scale=coef[:, 0, 2:3]).then_inc(scaled, 1)
                slots(act, 1, slot)
                root_norm(nc, act, m, rec3, root3)

            @block.tensor
            def _(pe):
                def slot(i, parity):
                    if live(i, 0):
                        wait(pe, added, i - 1)
                        pe.wait_ge(scaled, i + 1)
                        for o, c in zip(group4(ps[:, parity, :]), group4(z[:, parity, :])):
                            last = nc.tensor.transpose(o, c, m.ident[:, :])
                        last.then_inc(turned, 1)
                slots(pe, 1, slot)

            @block.vector
            def _(v):
                def slot(i, parity):
                    if live(i, 1):
                        v.wait_ge(turned, i)
                        add_and_count(nc, v, X, ps[:, (parity + 1) % 2, :], stats, i - 1, added, counted3)
                slots(v, 1, slot)
                v.wait_ge(counted3, NG)
                finish_norm(nc, v, m, stats, ctx, "c", rec3)


def l2(nc, m):
    with ExitStack() as ctx:
        def sb(name, shape, dt=F32, c=ctx):
            return c.enter_context(nc.sbuf_tensor(name, shape, dt))

        def sem(name):
            return ctx.enter_context(nc.semaphore(name))

        V = sb("V", [128, 2, NG, GB, D], F32R)
        scores = sb("scores", [128, ET, NG, GB * HEADS])
        attn = sb("attn", [128, ET, NG, GB * HEADS])
        stats = sb("d_stats", [128, B, 6])
        X = m.X[:, :, :].rearrange("p (g b) d -> p g (b d)", b=GB)
        mean = m.mean[:, :].rearrange("p (g b) -> p g b", b=GB)
        rstd = m.rstd[:, :].rearrange("p (g b) -> p g b", b=GB)
        ps = m.ps
        passed = sem("d_passed")

        with ExitStack() as c1:
            xc = sb("d_xc", [128, GN], F32, c1)
            xs = sb("d_xs", [128, 2, GN], F32, c1)
            xt = sb("d_xt", [128, 2, GN], F32R, c1)
            q = sb("d_q", [128, 2, GB, D], F32R, c1)
            z2 = sb("d_z2", [128, GB, E], F32, c1)
            lz = sb("d_lz", [128, GB, E], F32, c1)
            centred, normed, copied, turned, thi, tlo, qv, qvhi, qvlo, summed, sloped, leaked, scored, saved = [
                sem(f"d1_{n}") for n in ("centred", "normed", "copied", "turned", "thi", "tlo", "qv", "qvhi", "qvlo",
                                         "summed", "sloped", "leaked", "scored", "saved")]
            qvp = ps[:, 2:4, :].rearrange("p k (b w d) -> p (k b) w d", b=2, w=2)
            sums = ps[:, 4:6, :].rearrange("p k (b e) -> p (k b) e", b=2)
            Q_, V_ = 0, 1
            with nc.Block() as block:
                @block.gpsimd
                def _(pool):
                    def slot(i, parity):
                        if live(i, 0):
                            hold(pool, turned, i - 1, passed)
                            hold(pool, copied, i - 1, passed)
                            hold(pool, normed, i, passed)
                            nc.gpsimd.tensor_tensor(xc[:, :].rearrange("p (b d) -> p b d", b=GB),
                                                    X[:, i, :].rearrange("p (b d) -> p b d", b=GB),
                                                    mean[:, i, :].unsqueeze(2).broadcast_to([128, GB, D]),
                                                    ALU.subtract).then_inc(centred, 1)
                            hold(pool, centred, i + 1, passed)
                            nc.gpsimd.tensor_tensor(xs[:, parity, :].rearrange("p (b d) -> p b d", b=GB),
                                                    xc[:, :].rearrange("p (b d) -> p b d", b=GB),
                                                    rstd[:, i, :].unsqueeze(2).broadcast_to([128, GB, D]),
                                                    ALU.mult).then_inc(normed, 1)
                    slots(pool, 4, slot)

                @block.tensor
                def _(pe):
                    def slot(i, parity):
                        if live(i, 4):
                            g = i - 4
                            pe.wait_ge(leaked, g + 1)
                            wait(pe, saved, g - 1)
                            for t in range(ET):
                                for b in range(GB):
                                    c = (t * GB + b) * HEADS
                                    last = nc.tensor.matmul(ps[:, 6 + parity, c:c + HEADS], lz[:, b, t * 128:(t + 1) * 128],
                                                            m.abd[:, :], start=True, stop=True)
                            last.then_inc(scored, 1)
                        if live(i, 3):
                            pe.wait_ge(qvlo, 2 * (i - 3) + 2)
                            for b in range(GB):
                                nc.tensor.matmul(sums[:, b, :], q[:, HI, b, :], m.st[:, :], start=True, stop=False)
                                last = nc.tensor.matmul(sums[:, b, :], q[:, LO, b, :], m.st[:, :], start=False, stop=True)
                            last.then_inc(summed, 1)
                        if live(i, 2):
                            pe.wait_ge(tlo, i - 1)
                            for b, (h_, l_) in enumerate(zip(group4(xt[:, HI, :]), group4(xt[:, LO, :]))):
                                last = mm3(nc, ps[:, 2 + b // 2, (b % 2) * 256:(b % 2) * 256 + 256], h_, l_,
                                           late(m, "QV", HI), late(m, "QV", LO), True, True)
                            last.then_inc(qv, 1)
                        if live(i, 1):
                            q_ = (parity + 1) % 2
                            pe.wait_ge(normed, i)
                            for o, c in zip(group4(ps[:, q_, :]), group4(xs[:, q_, :])):
                                last = nc.tensor.transpose(o, c, m.ident[:, :])
                            last.then_inc(turned, 1)
                    slots(pe, 4, slot)

                @block.scalar
                def _(act):
                    def slot(i, parity):
                        if live(i, 3):
                            act.wait_ge(summed, i - 2)
                            nc.scalar.activation(z2[:, :, :], sums, ACT.Copy, scale=SLOPE).then_inc(sloped, 1)
                        if live(i, 2):
                            act.wait_ge(qv, i - 1)
                            take_hi(nc, V[:, HI, i - 2, :, :], qvp[:, :, V_, :]).then_inc(qvhi, 1)
                            take_hi(nc, q[:, HI, :, :], qvp[:, :, Q_, :]).then_inc(qvhi, 1)
                        if live(i, 1):
                            q_ = (parity + 1) % 2
                            act.wait_ge(turned, i)
                            take_hi(nc, xt[:, HI, :], ps[:, q_, :]).then_inc(thi, 1)
                            nc.scalar.activation(X[:, i - 1, :], xs[:, q_, :], ACT.Copy).then_inc(copied, 1)
                    slots(act, 4, slot)

                @block.vector
                def _(v):
                    def slot(i, parity):
                        if live(i, 3):
                            v.wait_ge(sloped, i - 2)
                            wait(v, scored, i - 3)
                            nc.vector.tensor_tensor(lz[:, :, :], sums, z2[:, :, :], ALU.max).then_inc(leaked, 1)
                        if live(i, 4):
                            v.wait_ge(scored, i - 3)
                            nc.vector.tensor_copy(scores[:, :, i - 4, :],
                                                  ps[:, 6 + parity, 0:ET * GB * HEADS].rearrange("p (t s) -> p t s", t=ET)
                                                  ).then_inc(saved, 1)
                        if live(i, 2):
                            v.wait_ge(qvhi, 2 * (i - 2) + 2)
                            take_lo(nc, V[:, LO, i - 2, :, :], qvp[:, :, V_, :], V[:, HI, i - 2, :, :]).then_inc(qvlo, 1)
                            take_lo(nc, q[:, LO, :, :], qvp[:, :, Q_, :], q[:, HI, :, :]).then_inc(qvlo, 1)
                        if live(i, 1):
                            v.wait_ge(thi, i)
                            take_lo(nc, xt[:, LO, :], ps[:, (parity + 1) % 2, :], xt[:, HI, :]).then_inc(tlo, 1)
                    slots(v, 4, slot)

        with ExitStack() as c2:
            se = sb("s_e", [128, 2, E], F32, c2)
            pre = sb("s_pre", [128, 2, E], F32, c2)
            top = sb("s_top", [128, 2, E], F32, c2)
            ex = sb("s_ex", [128, 2, E], F32, c2)
            dv, pe_s, ac = sem("d2_dv"), sem("d2_pe"), sem("d2_ac")
            sc = scores[:, :, :, :].rearrange("p t g s -> p t (g s)")
            at_ = attn[:, :, :, :].rearrange("p t g s -> p t (g s)")
            with nc.Block() as block:
                @block.vector
                def _(v):
                    chain = Chain(v, dv)
                    for t in range(ET):
                        chain(nc.vector.tensor_scalar(sc[:, t, :], sc[:, t, :], m.loga[:, t:t + 1], None, ALU.add))
                    v.wait_ge(pe_s, 1)
                    chain(nc.vector.tensor_copy(se[:, :, :], ps[:, 0, :].rearrange("p (k e) -> p k e", k=2)))
                    for k in range(2):
                        chain(nc.vector.tensor_tensor_scan(pre[:, k, :], m.pen[:, 0:E], se[:, k, :], NEG, ALU.add, ALU.max))
                    for k in range(2):
                        chain(nc.vector.tensor_tensor_scan(top[:, k, ::-1], m.pen[:, E:0:-1], pre[:, k, ::-1], NEG,
                                                           ALU.add, ALU.max))
                    chain(nc.vector.tensor_tensor(se[:, :, :], se[:, :, :], top[:, :, :], ALU.subtract))
                    v.wait_ge(ac, 1)
                    for k in range(2):
                        chain(nc.vector.tensor_tensor_scan(pre[:, k, :], m.same[:, 0:E], ex[:, k, :], 0.0, ALU.mult, ALU.add))
                    for k in range(2):
                        chain(nc.vector.tensor_tensor_scan(top[:, k, ::-1], m.same[:, E:0:-1], pre[:, k, ::-1], 0.0,
                                                           ALU.mult, ALU.max))
                    chain(nc.vector.reciprocal(top[:, :, :], top[:, :, :]))
                    chain(nc.vector.tensor_tensor(ex[:, :, :], ex[:, :, :], top[:, :, :], ALU.mult))
                    v.wait_ge(pe_s, 2)
                    chain(nc.vector.tensor_copy(at_[:, :, :], ps[:, 1, :].rearrange("p (t s) -> p t s", t=ET)))

                @block.tensor
                def _(pe):
                    pe.wait_ge(dv, 2)
                    for k in range(2):
                        for t in range(ET):
                            last = nc.tensor.transpose(ps[:, 0, k * E + t * 128:k * E + (t + 1) * 128],
                                                       sc[:, t, k * 128:(k + 1) * 128], m.ident[:, :])
                    last.then_inc(pe_s, 1)
                    pe.wait_ge(dv, 14)
                    for t in range(ET):
                        for k in range(2):
                            last = nc.tensor.transpose(ps[:, 1, (t * 2 + k) * 128:(t * 2 + k + 1) * 128],
                                                       ex[:, k, t * 128:(t + 1) * 128], m.ident[:, :])
                    last.then_inc(pe_s, 1)

                @block.scalar
                def _(act):
                    act.wait_ge(dv, 8)
                    nc.scalar.activation(ex[:, :, :], se[:, :, :], ACT.Exp).then_inc(ac, 1)

        with ExitStack() as c3:
            av = sb("e_av", [128, 2, ET, GN], F32, c3)
            y = sb("e_y", [128, GN], F32, c3)
            taken, weighed, summed, copied, out_, added, counted, rec, root = [sem(f"d3_{n}") for n in (
                "taken", "weighed", "summed", "copied", "out", "added", "counted", "rec", "root")]
            with nc.Block() as block:
                @block.tensor
                def _(pe):
                    def slot(i, parity):
                        if live(i, 2):
                            pe.wait_ge(copied, i - 1)
                            wait(pe, added, i - 2)
                            mm_each(nc, ps[:, 5, :], y, whole(m, "WOUT")).then_inc(out_, 1)
                        if live(i, 0):
                            wait(pe, weighed, i - 1)
                            for t in range(ET):
                                w = m.dstn[:, t * 128:(t + 1) * 128]
                                o = ps[:, 2 * parity + t, :]
                                nc.tensor.matmul(o, w, V[:, HI, i, :, :].rearrange("p b d -> p (b d)"), start=True, stop=False)
                                last = nc.tensor.matmul(o, w, V[:, LO, i, :, :].rearrange("p b d -> p (b d)"),
                                                        start=False, stop=True)
                            last.then_inc(taken, 1)
                        if live(i, 1):
                            pe.wait_ge(weighed, i)
                            for b, o in enumerate(group4(ps[:, 4, :])):
                                for t in range(ET):
                                    last = nc.tensor.matmul(o, av[:, (parity + 1) % 2, t, b * 128:(b + 1) * 128],
                                                            m.srce[:, t, :], start=t == 0, stop=t == ET - 1)
                            last.then_inc(summed, 1)
                    slots(pe, 2, slot)

                @block.vector
                def _(v):
                    def slot(i, parity):
                        if live(i, 2):
                            v.wait_ge(out_, i - 1)
                            add_and_count(nc, v, X, ps[:, 5, :], stats, i - 2, added, counted)
                        if live(i, 0):
                            v.wait_ge(taken, i + 1)
                            wait(v, summed, i - 1)
                            for t in range(ET):
                                last = nc.vector.tensor_tensor(
                                    av[:, parity, t, :].rearrange("p (s d) -> p s d", d=HD),
                                    ps[:, 2 * parity + t, :].rearrange("p (s d) -> p s d", d=HD),
                                    attn[:, t, i, :].unsqueeze(2).broadcast_to([128, GB * HEADS, HD]), ALU.mult)
                            last.then_inc(weighed, 1)
                    slots(v, 2, slot)
                    v.wait_ge(counted, NG)
                    finish_norm(nc, v, m, stats, c3, "e", rec)

                @block.scalar
                def _(act):
                    def slot(i, parity):
                        if live(i, 1):
                            act.wait_ge(summed, i)
                            nc.scalar.activation(y[:, :], ps[:, 4, :], ACT.Copy).then_inc(copied, 1)
                    slots(act, 2, slot)
                    root_norm(nc, act, m, rec, root)


def l3(nc, m, out):
    with ExitStack() as ctx:
        def sb(name, shape, dt=F32):
            return ctx.enter_context(nc.sbuf_tensor(name, shape, dt))

        def sem(name):
            return ctx.enter_context(nc.semaphore(name))

        xs = sb("f_xs", [128, GN])
        ax = sb("f_ax", [128, 2, GN], F32R)
        h1 = sb("f_h1", [128, 2, GN])
        a1 = sb("f_a1", [128, 2, 2, GN], F32R)
        h2 = sb("f_h2", [128, 4, GN])
        s3 = sb("f_s3", [128, 2, GN], F32R)
        stats = sb("f_stats", [128, B, 6])
        ln = sb("f_ln", [128, 2, 4, GB])
        power = sb("f_power", [128, GB])
        res = sb("f_res", [128, 2, GN])
        X = m.X[:, :, :].rearrange("p (g b) d -> p g (b d)", b=GB)
        S = stats[:, :, :].rearrange("p (g b) s -> p g b s", b=GB)
        outd = out.rearrange("(g b) n d -> n g b d", b=GB)
        ps = m.ps
        normed, copied, last_prod, added, counted, ready, written, passed = [sem(f"f_{n}") for n in (
            "normed", "copied", "last", "added", "counted", "ready", "written", "passed")]
        halves = [sem(f"f_ln{n}") for n in range(6)]
        prod, hi, lo = [[sem(f"f_{n}{s}") for s in range(5)] for n in ("prod", "hi", "lo")]
        stored = [sem(f"f_stored{u}") for u in range(2)]

        BEHIND = (1, 1, 1, 2, 2)
        PARTS = (1, 2, 2, 4, 1)
        RELU = (False, True, False, True, False)
        BANK = ((0,), (1, 2), (3, 1), (4, 5, 6, 7), (5,))
        LAST_BANK = 3
        LAST, NEXT = "last", "next"
        ORDER = [(0, 0), (3, 0), LAST, (3, 1), (1, 0), (1, 1), (3, 2), (3, 3), (2, 0), (2, 1), NEXT, (4, 0)]
        DEPTH = 4
        BUF = (ax, h1, a1, h2, s3)

        def pair(s, part):
            return [BUF[s][:, k, :] if PARTS[s] == 1 else BUF[s][:, k, part, :] for k in (HI, LO)]

        def count(s, k, g):
            return PARTS[s] * g + k + 1

        def product(s, k):
            o = ps[:, BANK[s][k], :]
            if s == 0:
                last = mm_each(nc, o, xs, m.adj2[:, :])
            elif s == 1:
                for b in range(2):
                    c = slice((2 * k + b) * 128, (2 * k + b + 1) * 128)
                    last = mm3(nc, o[:, b * 256:(b + 1) * 256], ax[:, HI, c], ax[:, LO, c], late(m, "L3W1", HI),
                               late(m, "L3W1", LO), True, True)
            elif s == 2:
                for b, ob in enumerate(group4(o)):
                    c = slice((b % 2) * 256 + k * 128, (b % 2) * 256 + (k + 1) * 128)
                    last = nc.tensor.matmul(ob, h1[:, b // 2, c], m.adj2[:, :], start=True, stop=True)
            elif s == 3:
                for t in range(2):
                    c = 512 * t + 128 * k
                    last = mm3(nc, o, late(m, "L3W2", HI, c, c + 128), late(m, "L3W2", LO, c, c + 128),
                               a1[:, HI, t, :], a1[:, LO, t, :], t == 0, t == 1)
            else:
                for b, ob in enumerate(group4(o)):
                    c = slice(b * 128, (b + 1) * 128)
                    for t in range(4):
                        last = nc.tensor.matmul(ob, h2[:, t, c], whole(m, "L3W3", t), start=t == 0, stop=t == 3)
            return last

        def stores(g, parity):
            return 8 * (g + 2 - parity)

        with nc.Block() as block:
            @block.tensor
            def _(pe):
                def slot(i, parity):
                    for what in ORDER:
                        if what == NEXT:
                            continue
                        if what == LAST:
                            if live(i, 3):
                                pe.wait_ge(lo[4], i - 2)
                                mm3(nc, ps[:, LAST_BANK, :], m.adj2s[:, HI, :], m.adj2s[:, LO, :], s3[:, HI, :], s3[:, LO, :],
                                    True, True).then_inc(last_prod, 1)
                            continue
                        s, k = what
                        g = i - BEHIND[s]
                        if not live(i, BEHIND[s]):
                            continue
                        if s == 0:
                            pe.wait_ge(normed, g + 1)
                        elif k == 0:
                            pe.wait_ge((hi if RELU[s - 1] else lo)[s - 1], count(s - 1, PARTS[s - 1] - 1, g))
                        if (s, k) == (2, 0):
                            wait(pe, added, i - 2)
                        product(s, k).then_inc(prod[s], 1)
                slots(pe, DEPTH, slot)

            @block.scalar
            def _(act):
                def slot(i, parity):
                    for what in ORDER:
                        if what == NEXT and live(i, 0):
                            act.wait_ge(normed, i + 1)
                            nc.scalar.activation(X[:, i, :], xs[:, :], ACT.Copy).then_inc(copied, 1)
                        if what in (NEXT, LAST) or not live(i, BEHIND[what[0]]):
                            continue
                        s, k = what
                        act.wait_ge(prod[s], count(s, k, i - BEHIND[s]))
                        if RELU[s]:
                            nc.scalar.activation(BUF[s][:, k, :], ps[:, BANK[s][k], :], ACT.Relu).then_inc(hi[s], 1)
                        else:
                            take_hi(nc, pair(s, k)[HI], ps[:, BANK[s][k], :]).then_inc(hi[s], 1)
                slots(act, DEPTH, slot)

            @block.vector
            def _(v):
                def slot(i, parity):
                    for what in ORDER:
                        if what == NEXT:
                            if live(i, 4):
                                v.wait_ge(ready, i - 3 + 1)
                                wait(v, stored[parity], stores(i - 6, parity))
                                for b, (o, y) in enumerate(zip(group4(res[:, parity, :]), group4(X[:, i - 4, :]))):
                                    last = nc.vector.tensor_scalar(o, y, ln[:, parity, 0, b:b + 1], ln[:, parity, 3, b:b + 1],
                                                                   ALU.subtract, ALU.mult)
                                last.then_inc(written, 1)
                            if live(i, 0):
                                wait(v, prod[0], i)
                                wait(v, copied, i)
                                norm_group(nc, m, xs[:, :], X[:, i, :], i).then_inc(normed, 1)
                        elif what == LAST:
                            if live(i, 3):
                                v.wait_ge(last_prod, i - 2)
                                add_and_count(nc, v, X, ps[:, LAST_BANK, :], stats, i - 3, added, counted)
                        elif live(i, BEHIND[what[0]]) and not RELU[what[0]]:
                            s, k = what
                            v.wait_ge(hi[s], count(s, k, i - BEHIND[s]))
                            h_, l_ = pair(s, k)
                            take_lo(nc, l_, ps[:, BANK[s][k], :], h_).then_inc(lo[s], 1)
                slots(v, DEPTH, slot)

            @block.gpsimd
            def _(pool):
                nc.gpsimd.memset(power[:, :], -0.5).then_inc(ready, 1)

                def slot(i, parity):
                    if live(i, 3):
                        g, q = i - 3, (parity + 1) % 2
                        mean_, diff, var, rstd_ = [ln[:, q, k, :] for k in range(4)]
                        hold(pool, counted, g + 1, passed)
                        hold(pool, written, g - 1, passed)
                        nc.gpsimd.tensor_tensor(mean_, S[:, g, :, 1], S[:, g, :, 4], ALU.add)
                        nc.gpsimd.tensor_tensor(diff, S[:, g, :, 1], S[:, g, :, 4], ALU.subtract)
                        nc.gpsimd.tensor_tensor(var, S[:, g, :, 2], S[:, g, :, 5], ALU.add).then_inc(halves[0], 1)
                        hold(pool, halves[0], g + 1, passed)
                        nc.gpsimd.tensor_scalar(mean_, mean_, 0.5, None, ALU.mult)
                        nc.gpsimd.tensor_tensor(diff, diff, diff, ALU.mult).then_inc(halves[1], 1)
                        hold(pool, halves[1], g + 1, passed)
                        nc.gpsimd.tensor_scalar(diff, diff, float(D // 4), None, ALU.mult).then_inc(halves[2], 1)
                        hold(pool, halves[2], g + 1, passed)
                        nc.gpsimd.tensor_tensor(var, var, diff, ALU.add).then_inc(halves[3], 1)
                        hold(pool, halves[3], g + 1, passed)
                        nc.gpsimd.tensor_scalar(var, var, 1.0 / D, EPS_NORM, ALU.mult, ALU.add).then_inc(halves[4], 1)
                        hold(pool, halves[4], g + 1, passed)
                        nc.gpsimd.tensor_tensor(rstd_, var, power[:, :], ALU.pow).then_inc(ready, 1)
                slots(pool, DEPTH, slot)

            @block.sync
            def _(sp):
                def slot(i, parity):
                    if live(i, 4):
                        sp.wait_ge(written, i - 3)
                        sp.dma_start(outd[:, i - 4, :, :], res[:, parity, :].rearrange("p (b d) -> p b d", b=GB)
                                     ).then_inc(stored[parity], 16)
                slots(sp, DEPTH, slot)
                for u in range(2):
                    sp.wait_ge(stored[u], 16 * NG // 2)


def kernel(**inputs):
    import numpy as np
    import concourse.bacc as bacc
    from concourse import mybir as mb
    from concourse.bass_utils import run_bass_kernel_spmd

    a = {k: np.asarray(v) for k, v in inputs.items()}

    def tiles(w):
        return w.reshape(-1, 128, w.shape[1]).transpose(1, 0, 2).reshape(128, -1)

    wih, whh = a["L0_gnn_Wih"].transpose(0, 2, 1), a["L0_gnn_Whh"].transpose(0, 2, 1)
    lstm = np.stack([wih, whh], 1).transpose(2, 0, 1, 3).reshape(128, -1)
    cols = lambda v: v.reshape(-1, 128).T
    arrays = dict(
        x=a["x"], xt=a["x"].transpose(2, 0, 1).reshape(128, -1), adj=a["adj"],
        gnn_w=np.concatenate([a["L0_gnn_Wg0"], a["adj"].T, a["L0_gnn_Wg1"]], 1),
        lstm_w=lstm,
        whole_w=np.concatenate([a["L1_gnn_W1"].T, tiles(a["L1_gnn_W2"].T), a["L2_gnn_W_out"].T, tiles(a["L3_gnn_W3"])], 1),
        late_w=np.concatenate([a["L2_gnn_W_lin"].T, a["L2_gnn_W_val"].T, a["L3_gnn_W1"], tiles(a["L3_gnn_W2"])], 1),
        vecs=np.concatenate([cols(a[k]) for k in ("L0_gnn_bih", "L0_gnn_bhh", "L1_gnn_b1", "L1_gnn_g1", "L1_gnn_be1",
                                                  "L1_gnn_b2", "L1_gnn_g2", "L1_gnn_be2", "L2_gnn_a")], 1),
        bg0=a["L0_gnn_bg0"], bg1=a["L0_gnn_bg1"], src=a["L2_gnn_src"], dst=a["L2_gnn_dst"])
    nc = bacc.Bacc("TRN2", target_bir_lowering=False, num_devices=1)
    args, feed = [], {}
    for name, arr in arrays.items():
        arr = np.ascontiguousarray(arr)
        feed[f"in_{name}"] = arr
        args.append(nc.dram_tensor(f"in_{name}", arr.shape, mb.dt.from_np(arr.dtype), kind="ExternalInput").ap())
    args.append(nc.dram_tensor("out", (64, 128, 128), mb.dt.float32, kind="ExternalOutput").ap())
    build(nc, *args)
    r = run_bass_kernel_spmd(nc, [feed], core_ids=[0])
    return r.results[0]["out"]
```

```python
from contextlib import ExitStack

import concourse.bass as bass
from concourse import mybir

F32 = mybir.dt.float32
F32R = mybir.dt.float32r
I32 = mybir.dt.int32
ALU = mybir.AluOpType
ACT = mybir.ActivationFunctionType

B, T, D = 64, 128, 128
GB = 4
GN = GB * T
NG = B // GB
SKIPS = 4
E = 256
ET = E // 128
HEADS = 4
HD = D // HEADS
SLOPE = 0.2
EPS_NORM = 1e-5
EPS_LOG = 1e-8
NEG = -3.0e38
HI, LO = 0, 1

GNN = dict(Wg0=(0, 128), adjT=(128, 256), Wg1=(256, 384))
GNN_COLS = 384
LSTM_COLS = SKIPS * 2 * 4 * D
WHOLE = dict(L1W1=(0, 256), L1W2=(256, 512), WOUT=(512, 640), L3W3=(640, 1152))
WHOLE_COLS = 1152
LATE = dict(QV=(0, 256), L3W1=(256, 512), L3W2=(512, 1536))
LATE_COLS = 1536
V_BIH, V_BHH, V_B1, V_G1, V_BE1, V_B2, V_G2, V_BE2, V_A = 0, 16, 32, 34, 36, 38, 39, 40, 41
VEC_COLS = 42


def f32(ap):
    return ap.bitcast(F32)


class Chain:

    def __init__(self, eng, sem):
        self.eng, self.sem, self.n = eng, sem, 0

    def __call__(self, ins, wait=True):
        self.n += 1
        ins.then_inc(self.sem, 1)
        if wait:
            self.eng.wait_ge(self.sem, self.n)
        return self.n


def hold(pool, sem, value, passed):
    if not isinstance(value, int) or value > 0:
        pool.wait_ge(sem, value)
        pool.sem_inc(passed, 1)


def slots(eng, depth, body, unroll=2):
    lead = -(-(depth + 2) // unroll) * unroll
    for i in range(lead):
        body(i, i % 2)
    with eng.Fori(lead // unroll, NG // unroll) as turn:
        for k in range(unroll):
            body(unroll * turn + k, k % 2)
    for i in range(NG, NG + depth):
        body(i, i % 2)


def live(i, behind):
    return not isinstance(i, int) or 0 <= i - behind < NG


def wait(eng, sem, value):
    if not isinstance(value, int) or value > 0:
        eng.wait_ge(sem, value)


def group4(ap):
    return [ap[:, b * 128:(b + 1) * 128] for b in range(GB)]


def mm3(nc, out, wh, wl, xh, xl, start, stop):
    nc.tensor.matmul(out, wh, xh, start=start, stop=False)
    nc.tensor.matmul(out, wh, xl, start=False, stop=False)
    return nc.tensor.matmul(out, wl, xh, start=False, stop=stop)


def mm_each(nc, out, data, w):
    for o, x in zip(group4(out), group4(data)):
        last = nc.tensor.matmul(o, x, w, start=True, stop=True)
    return last


def take_hi(nc, out, psum, func=ACT.Copy):
    return nc.scalar.activation(out, psum, func)


def take_lo(nc, out, psum, hi, relu=False):
    if relu:
        return nc.vector.scalar_tensor_tensor(out=out, in0=psum, scalar=0.0, in1=f32(hi), op0=ALU.max, op1=ALU.subtract)
    return nc.vector.tensor_tensor(out, psum, f32(hi), ALU.subtract)


class Mem:
    pass


def build(nc, x, xt, adj, gnn_w, lstm_w, whole_w, late_w, vecs, bg0, bg1, src, dst, out):
    with ExitStack() as ctx:
        m = Mem()

        def sb(name, shape, dt=F32):
            return ctx.enter_context(nc.sbuf_tensor(name, shape, dt))

        m.X = sb("X", [128, B, D])
        m.ident = sb("ident", [128, 128])
        m.gnn = sb("gnn", [128, GNN_COLS])
        m.wg1 = sb("wg1", [128, 2, 128], F32R)
        m.ahat = sb("ahat", [128, 128])
        m.adj2 = sb("adj2", [128, 128])
        m.adj2s = sb("adj2s", [128, 2, 128], F32R)
        m.whole = sb("whole", [128, WHOLE_COLS])
        m.late = sb("late", [128, 2, LATE_COLS], F32R)
        m.vec = sb("vec", [128, VEC_COLS])
        m.lbias = sb("lbias", [128, SKIPS * 4])
        m.abd = sb("abd", [128, HEADS])
        m.score = sb("score", [128, GB, GB * HEADS])
        m.st = sb("st", [128, E], F32R)
        m.dstn = sb("dstn", [128, E], F32R)
        m.srce = sb("srce", [128, ET, 128])
        m.loga = sb("loga", [128, E])
        m.same = sb("same", [128, E + 1])
        m.pen = sb("pen", [128, E + 1])
        m.bn2 = sb("bn2", [128, 2])
        m.bn1 = sb("bn1", [128, 2, 2])
        m.mean = sb("mean", [128, B])
        m.rstd = sb("rstd", [128, B])
        m.ps = ctx.enter_context(nc.psum_tensor("ps", [128, 8, 512], F32))

        pre1 = ExitStack()
        with nc.sbuf_tensor("H", [128, 2, B, T], F32R, side="right") as m.H:
            with nc.sbuf_tensor("lstm", [128, 2, LSTM_COLS], F32R) as m.lstm:
                with ExitStack() as actx:
                    m.lraw = actx.enter_context(nc.sbuf_tensor("lraw", [128, LSTM_COLS], F32))
                    m.w_landed = actx.enter_context(nc.semaphore("w_landed"))
                    m.bg0 = actx.enter_context(nc.sbuf_tensor("bg0b", [128, 128], F32))
                    m.biasrow = actx.enter_context(nc.sbuf_tensor("biasrow", [128, 128], F32R))
                    m.rowsum4 = actx.enter_context(nc.sbuf_tensor("rowsum4", [128, GN], F32R))
                    m.xt = actx.enter_context(nc.sbuf_tensor("xt", [128, 2, GN], F32))
                    setup(nc, m, xt, adj, gnn_w, lstm_w, vecs, bg0, bg1, src, dst)
                    l0_gnn(nc, m, xt, late_w)
                l0_lstm(nc, m, x, whole_w)
            m.pre1 = pre1.enter_context(nc.sbuf_tensor("pre1", [128, 2, B, T], F32))
            l1_first(nc, m)
        with nc.sbuf_tensor("pre2", [128, B, T], F32, side="right") as m.pre2:
            with pre1:
                l1_second(nc, m)
            l2(nc, m)
        l3(nc, m, out)


def setup(nc, m, xt, adj, gnn_w, lstm_w, vecs, bg0, bg1, src, dst):
    with ExitStack() as ctx:
        def sb(name, shape, dt=F32):
            return ctx.enter_context(nc.sbuf_tensor(name, shape, dt))

        def sem(name):
            return ctx.enter_context(nc.semaphore(name))

        adjn = sb("adjn", [128, 128])
        bg1b = sb("bg1b", [128, 128])
        rowsum = sb("rowsum", [128, 128], F32R)
        row_i = sb("row_i", [128, 2, E], I32)
        col_i = sb("col_i", [128, 2, ET], I32)
        rowf = sb("rowf", [128, 2, E])
        colf = sb("colf", [128, 2, ET])
        ones = sb("ones", [128, 128])
        masks = sb("masks", [128, 4])
        node = sb("node", [128, 1])
        rank_no = sb("rank_no", [128, E])
        edge_no = sb("edge_no", [128, ET])
        keyrow = sb("keyrow", [128, E])
        keycol = sb("keycol", [128, ET])
        rank = sb("rank", [128, ET])
        perm = sb("perm", [128, ET, E])
        bcast = sb("bcast", [128, 2, ET, 128])
        sorted_row = sb("sorted_row", [128, 2, E])
        onehot = sb("onehot", [128, 2, E])
        dste = sb("dste", [128, ET, 128])
        edge_adj = sb("edge_adj", [128, ET])
        anorm = sb("anorm", [128, 2, 128])
        sums = sb("sums", [128, 4])
        dinv = sb("dinv", [128, 2])
        half = sb("half", [128, 128])
        rs = sb("rs", [128, 2, 128], F32R)
        bgs = sb("bgs", [128, 2, 128], F32R)
        mix = sb("mix", [128, 2, 128])
        eps_log = sb("eps_log", [128, 1])
        loaded, made, dv, pe, ac = sem("su_loaded"), sem("su_made"), sem("su_dv"), sem("su_pe"), sem("su_ac")
        x_landed = sem("su_x")
        ps = m.ps
        at = {}

        with nc.Block() as block:
            @block.sync
            def _(sp):
                sp.dma_start(m.gnn[:, :], gnn_w).then_inc(loaded, 16)
                sp.dma_start(adjn[:, :], adj).then_inc(loaded, 16)
                sp.dma_start(m.vec[:, :], vecs).then_inc(loaded, 16)
                sp.dma_start(m.bg0[:, :], bg0.partition_broadcast(128)).then_inc(loaded, 16)
                sp.dma_start(bg1b[:, :], bg1.partition_broadcast(128)).then_inc(loaded, 16)
                for k, ids in enumerate((src, dst)):
                    sp.dma_start(row_i[:, k, :], ids.partition_broadcast(128)).then_inc(loaded, 16)
                    sp.dma_start(col_i[:, k, :], ids.rearrange("(n a) -> n a", a=ET)).then_inc(loaded, 16)
                for g in range(2):
                    sp.dma_start(m.xt[:, g, :], xt[:, g * GN:(g + 1) * GN]).then_inc(x_landed, 16)
                sp.dma_start(m.lraw[:, :], lstm_w).then_inc(m.w_landed, 16)
                sp.wait_ge(x_landed, 32)

            @block.gpsimd
            def _(pool):
                chain = Chain(pool, made)
                chain(nc.gpsimd.memset(m.ident[:, :], 0.0))
                chain(nc.gpsimd.affine_select(out=m.ident[:, :], in_=m.ident[:, :], compare_op=ALU.not_equal, fill=1.0,
                                              base=0, pattern=[[-1, 128]], channel_multiplier=1))
                chain(nc.gpsimd.iota(node[:, :], pattern=[[0, 1]], base=0, channel_multiplier=1,
                                     allow_small_or_imprecise_dtypes=True))
                chain(nc.gpsimd.iota(rank_no[:, :], pattern=[[1, E]], base=0, channel_multiplier=0,
                                     allow_small_or_imprecise_dtypes=True))
                chain(nc.gpsimd.iota(edge_no[:, :], pattern=[[1, ET]], base=0, channel_multiplier=ET,
                                     allow_small_or_imprecise_dtypes=True))
                chain(nc.gpsimd.memset(ones[:, :], 1.0))
                chain(nc.gpsimd.memset(eps_log[:, :], EPS_LOG))
                chain(nc.gpsimd.memset(m.score[:, :, :], 0.0))
                chain(nc.gpsimd.memset(bcast[:, :, :, :], 0.0))
                chain(nc.gpsimd.memset(m.abd[:, :], 1.0))
                chain(nc.gpsimd.affine_select(out=m.abd[:, :], in_=m.abd[:, :], compare_op=ALU.is_ge, fill=0.0,
                                              base=0, pattern=[[-HD, HEADS]], channel_multiplier=1))
                chain(nc.gpsimd.affine_select(out=m.abd[:, :], in_=m.abd[:, :], compare_op=ALU.is_ge, fill=0.0,
                                              base=HD - 1, pattern=[[HD, HEADS]], channel_multiplier=-1))

            @block.vector
            def _(v):
                chain = Chain(v, dv)
                v.wait_ge(loaded, 9 * 16)
                v.wait_ge(made, 12)
                vec = nc.vector
                X_ = mybir.AxisListType.X
                w1 = m.gnn[:, GNN["Wg1"][0]:GNN["Wg1"][1]]
                adj_t = m.gnn[:, GNN["adjT"][0]:GNN["adjT"][1]]
                chain(vec.tensor_copy(rowf[:, :, :], row_i[:, :, :]), wait=False)
                chain(vec.tensor_copy(colf[:, :, :], col_i[:, :, :]))
                chain(vec.scalar_tensor_tensor(out=keyrow[:, :], in0=rowf[:, 0, :], scalar=float(E), in1=rank_no[:, :],
                                               op0=ALU.mult, op1=ALU.add), wait=False)
                chain(vec.scalar_tensor_tensor(out=keycol[:, :], in0=colf[:, 0, :], scalar=float(E), in1=edge_no[:, :],
                                               op0=ALU.mult, op1=ALU.add), wait=False)
                for k in range(2):
                    for t in range(ET):
                        chain(vec.tensor_scalar(bcast[:, k, t, :], ones[:, :], colf[:, k, t:t + 1], None, ALU.mult),
                              wait=k == 1 and t == ET - 1)
                for t in range(ET):
                    chain(vec.tensor_scalar(perm[:, t, :], keyrow[:, :], keycol[:, t:t + 1], None, ALU.is_lt,
                                            ALU.add, accum_out=rank[:, t:t + 1]), wait=t == ET - 1)
                for t in range(ET):
                    at["sort"] = chain(vec.tensor_scalar(perm[:, t, :], rank_no[:, :], rank[:, t:t + 1], None,
                                                         ALU.is_equal), wait=False)
                chain(vec.tensor_tensor(anorm[:, 0, :], adjn[:, :], m.ident[:, :], ALU.add), wait=False)
                chain(vec.tensor_tensor(anorm[:, 1, :], adj_t, m.ident[:, :], ALU.add))
                chain(vec.reduce_sum(sums[:, 0:1], anorm[:, 0, :], X_), wait=False)
                chain(vec.reduce_sum(sums[:, 1:2], anorm[:, 1, :], X_), wait=False)
                chain(vec.tensor_tensor(half[:, :], anorm[:, 0, :], m.ident[:, :], ALU.mult))
                chain(vec.reduce_sum(sums[:, 2:3], half[:, :], X_), wait=False)
                chain(vec.tensor_tensor(dinv[:, 0:1], sums[:, 0:1], sums[:, 1:2], ALU.add))
                chain(vec.tensor_tensor(sums[:, 3:4], dinv[:, 0:1], sums[:, 2:3], ALU.subtract))
                at["degree"] = chain(vec.reciprocal(dinv[:, 0:1], sums[:, 3:4]), wait=False)
                v.wait_ge(pe, 1)
                chain(vec.tensor_copy(sorted_row[:, :, :], ps[:, 0, :].rearrange("p (k e) -> p k e", k=2)))
                for k in range(2):
                    at["onehot"] = chain(vec.tensor_scalar(onehot[:, k, :], sorted_row[:, k, :], node[:, 0:1], None,
                                                           ALU.is_equal), wait=k == 1)
                chain(vec.tensor_tensor(m.st[:, :], onehot[:, 0, :], onehot[:, 1, :], ALU.add), wait=False)
                chain(vec.tensor_copy(m.dstn[:, :], onehot[:, 1, :]), wait=False)
                chain(vec.memset(m.same[:, :], 0.0))
                chain(vec.tensor_tensor(m.same[:, 1:E], sorted_row[:, 0, 1:E], sorted_row[:, 0, 0:E - 1], ALU.is_equal))
                chain(vec.tensor_scalar(m.pen[:, :], m.same[:, :], -1.0, -NEG, ALU.add, ALU.mult), wait=False)
                v.wait_ge(pe, 2)
                chain(vec.tensor_copy(m.srce[:, :, :], ps[:, 1, 0:E].rearrange("p (t n) -> p t n", t=ET)), wait=False)
                chain(vec.tensor_copy(dste[:, :, :], ps[:, 1, E:2 * E].rearrange("p (t n) -> p t n", t=ET)))
                v.wait_ge(pe, 3)
                chain(vec.tensor_tensor(perm[:, :, 0:128], ps[:, 2, 0:E].rearrange("p (t n) -> p t n", t=ET),
                                        dste[:, :, :], ALU.mult))
                chain(vec.reduce_sum(edge_adj[:, :], perm[:, :, 0:128], X_))
                for t in range(ET):
                    at["spread"] = chain(vec.tensor_scalar(bcast[:, 0, t, :], ones[:, :], edge_adj[:, t:t + 1], None,
                                                           ALU.mult), wait=False)
                v.wait_ge(ac, 1)
                at["half"] = chain(vec.tensor_scalar(half[:, :], anorm[:, 0, :], dinv[:, 1:2], None, ALU.mult), wait=False)
                chain(vec.tensor_copy(m.wg1[:, HI, :], w1), wait=False)
                chain(vec.tensor_tensor(m.adj2[:, :], adj_t, adj_t, ALU.mult), wait=False)
                chain(vec.tensor_tensor(m.lbias[:, :], m.vec[:, V_BIH:V_BIH + 16], m.vec[:, V_BHH:V_BHH + 16], ALU.add),
                      wait=False)
                chain(vec.tensor_scalar(m.abd[:, :], m.abd[:, :], m.vec[:, V_A:V_A + 1], None, ALU.mult), wait=False)
                chain(vec.tensor_copy(bgs[:, HI, :], bg1b[:, :]), wait=False)
                chain(vec.tensor_tensor(masks[:, 0:1], m.ident[:, 0:1], m.ident[:, 1:2], ALU.add), wait=False)
                chain(vec.tensor_tensor(masks[:, 2:3], m.ident[:, 0:1], m.ident[:, 2:3], ALU.add))
                chain(vec.tensor_tensor(m.wg1[:, LO, :], w1, f32(m.wg1[:, HI, :]), ALU.subtract), wait=False)
                chain(vec.tensor_copy(m.adj2s[:, HI, :], m.adj2[:, :]), wait=False)
                chain(vec.tensor_tensor(bgs[:, LO, :], bg1b[:, :], f32(bgs[:, HI, :]), ALU.subtract))
                chain(vec.tensor_tensor(m.adj2s[:, LO, :], m.adj2[:, :], f32(m.adj2s[:, HI, :]), ALU.subtract), wait=False)
                for b in range(GB):
                    chain(vec.tensor_copy(m.score[:, b, b * HEADS:(b + 1) * HEADS], m.abd[:, :]), wait=False)
                v.wait_ge(pe, 4)
                chain(vec.tensor_copy(rs[:, HI, :], ps[:, 4, 0:128]), wait=False)
                chain(vec.tensor_scalar(mix[:, 1, :], f32(bgs[:, LO, :]), m.ident[:, 1:2], None, ALU.mult))
                chain(vec.tensor_tensor(rs[:, LO, :], ps[:, 4, 0:128], f32(rs[:, HI, :]), ALU.subtract), wait=False)
                chain(vec.scalar_tensor_tensor(out=m.biasrow[:, :], in0=f32(bgs[:, HI, :]),
                                               scalar=masks[:, 2:3], in1=mix[:, 1, :], op0=ALU.mult, op1=ALU.add))
                chain(vec.tensor_scalar(mix[:, 0, :], f32(rs[:, LO, :]), m.ident[:, 2:3], None, ALU.mult))
                chain(vec.scalar_tensor_tensor(out=rowsum[:, :], in0=f32(rs[:, HI, :]), scalar=masks[:, 0:1],
                                               in1=mix[:, 0, :], op0=ALU.mult, op1=ALU.add))
                for b in range(GB):
                    chain(vec.tensor_copy(m.rowsum4[:, b * 128:(b + 1) * 128], f32(rowsum[:, :])), wait=False)
                v.wait_ge(pe, 5)
                chain(vec.tensor_scalar(m.ahat[:, :], ps[:, 3, 0:128], dinv[:, 1:2], None, ALU.mult))

            @block.scalar
            def _(act):
                act.wait_ge(dv, at["degree"])
                nc.scalar.activation(dinv[:, 1:2], dinv[:, 0:1], ACT.Sqrt).then_inc(ac, 1)
                act.wait_ge(pe, 6)
                nc.scalar.activation(m.loga[:, :], ps[:, 5, 0:E], ACT.Ln, bias=eps_log[:, 0:1]).then_inc(ac, 1)

            @block.tensor
            def _(t_):
                t_.wait_ge(dv, at["sort"])
                for k in range(2):
                    for t in range(ET):
                        last = nc.tensor.matmul(ps[:, 0, k * E:(k + 1) * E], bcast[:, k, t, :], perm[:, t, :],
                                                start=(t == 0), stop=(t == ET - 1))
                last.then_inc(pe, 1)
                t_.wait_ge(dv, at["onehot"])
                for k in range(2):
                    for t in range(ET):
                        last = nc.tensor.transpose(ps[:, 1, (k * ET + t) * 128:(k * ET + t + 1) * 128],
                                                   onehot[:, k, t * 128:(t + 1) * 128], m.ident[:, :])
                last.then_inc(pe, 1)
                for t in range(ET):
                    last = nc.tensor.matmul(ps[:, 2, t * 128:(t + 1) * 128], onehot[:, 0, t * 128:(t + 1) * 128],
                                            adjn[:, :], start=True, stop=True)
                last.then_inc(pe, 1)
                nc.tensor.matmul(ps[:, 4, 0:128], ones[:, :], m.gnn[:, GNN["adjT"][0]:GNN["adjT"][1]], start=True,
                                 stop=True).then_inc(pe, 1)
                t_.wait_ge(dv, at["half"])
                nc.tensor.transpose(ps[:, 3, 0:128], half[:, :], m.ident[:, :]).then_inc(pe, 1)
                for t in range(ET):
                    last = nc.tensor.matmul(ps[:, 5, t * 128:(t + 1) * 128], bcast[:, 0, t, :], m.ident[:, :], start=True,
                                            stop=True)
                last.then_inc(pe, 1)


def l0_gnn(nc, m, xt, late_w):
    with ExitStack() as ctx:
        def sb(name, shape, dt=F32):
            return ctx.enter_context(nc.sbuf_tensor(name, shape, dt))

        def sem(name):
            return ctx.enter_context(nc.semaphore(name))

        xw = sb("a_xw", [128, GN])
        h = sb("a_h", [128, GN])
        ah = sb("a_ah", [128, 2, GN], F32R)
        prod = [sem(f"a_prod{s}") for s in range(4)]
        xw_ready, h_ready, ah_hi, ah_lo, H_hi, H_lo, w_hi, w_lo, passed = [sem(f"a_{n}") for n in (
            "xw", "h", "ah_hi", "ah_lo", "H_hi", "H_lo", "w_hi", "w_lo", "passed")]
        landed = [sem(f"a_landed{u}") for u in range(2)]
        H = m.H[:, :, :, :].rearrange("p k (g b) t -> p k g (b t)", b=GB)
        lstm = m.lstm[:, :, :].rearrange("p k (g c) -> p k g c", g=NG)
        lraw = m.lraw[:, :].rearrange("p (g c) -> p g c", g=NG)
        late_raw = sb("late_raw", [128, NG, LATE_COLS // NG])
        later = m.late[:, :, :].rearrange("p k (g c) -> p k g c", g=NG)
        xtd = xt.rearrange("p (g c) -> p g c", c=GN)
        ps = m.ps
        w0, adj_t = [m.gnn[:, GNN[n][0]:GNN[n][1]] for n in ("Wg0", "adjT")]
        DEPTH = 3

        with nc.Block() as block:
            @block.sync
            def _(sp):
                sp.dma_start(late_raw[:, :, :].rearrange("p g c -> p (g c)"), late_w).then_inc(m.w_landed, 16)

                def slot(i, parity):
                    if not isinstance(i, int) or 2 <= i < NG:
                        sp.wait_ge(prod[0], i - 1)
                        sp.dma_start(m.xt[:, parity, :], xtd[:, i, :]).then_inc(landed[parity], 16)
                slots(sp, DEPTH, slot)
                for u in range(2):
                    sp.wait_ge(landed[u], 16 * (NG // 2 - 1))

            @block.tensor
            def _(pe):
                def slot(i, parity):
                    if live(i, 3):
                        pe.wait_ge(ah_lo, i - 2)
                        wait(pe, H_lo, i - 3)
                        nc.tensor.matmul(ps[:, 3, :], m.biasrow[:, :], m.rowsum4[:, :], start=True, stop=False)
                        mm3(nc, ps[:, 3, :], m.wg1[:, HI, :], m.wg1[:, LO, :], ah[:, HI, :], ah[:, LO, :], False,
                            True).then_inc(prod[3], 1)
                    if live(i, 2):
                        pe.wait_ge(h_ready, i - 1)
                        mm_each(nc, ps[:, 2, :], h, adj_t).then_inc(prod[2], 1)
                    if live(i, 1):
                        pe.wait_ge(xw_ready, i)
                        nc.tensor.matmul(ps[:, 1, :], adj_t, xw[:, :], start=True, stop=True).then_inc(prod[1], 1)
                    if live(i, 0):
                        wait(pe, landed[parity], 8 * (i - parity))
                        mm_each(nc, ps[:, 0, :], m.xt[:, parity, :], w0).then_inc(prod[0], 1)
                slots(pe, DEPTH, slot)

            @block.scalar
            def _(act):
                def slot(i, parity):
                    if live(i, 3):
                        act.wait_ge(prod[3], i - 2)
                        take_hi(nc, H[:, HI, i - 3, :], ps[:, 3, :], ACT.Relu).then_inc(H_hi, 1)
                    if live(i, 2):
                        act.wait_ge(prod[2], i - 1)
                        take_hi(nc, ah[:, HI, :], ps[:, 2, :]).then_inc(ah_hi, 1)
                    if live(i, 1):
                        act.wait_ge(prod[1], i)
                        nc.scalar.activation(h[:, :], ps[:, 1, :], ACT.Relu).then_inc(h_ready, 1)
                slots(act, DEPTH, slot)

            @block.vector
            def _(v):
                def slot(i, parity):
                    if live(i, 3):
                        v.wait_ge(H_hi, i - 2)
                        take_lo(nc, H[:, LO, i - 3, :], ps[:, 3, :], H[:, HI, i - 3, :], relu=True).then_inc(H_lo, 1)
                    if live(i, 2):
                        v.wait_ge(ah_hi, i - 1)
                        take_lo(nc, ah[:, LO, :], ps[:, 2, :], ah[:, HI, :]).then_inc(ah_lo, 1)
                    if live(i, 3):
                        if isinstance(i, int) and i == 3:
                            v.wait_ge(m.w_landed, 32)
                        nc.vector.tensor_copy(lstm[:, HI, i - 3, :], lraw[:, i - 3, :])
                        nc.vector.tensor_copy(later[:, HI, i - 3, :], late_raw[:, i - 3, :]).then_inc(w_hi, 1)
                    if live(i, 0):
                        wait(v, prod[1], i)
                        v.wait_ge(prod[0], i + 1)
                        nc.vector.tensor_tensor(xw[:, :].rearrange("p (b d) -> p b d", b=GB),
                                                ps[:, 0, :].rearrange("p (b d) -> p b d", b=GB),
                                                m.bg0[:, :].unsqueeze(1).broadcast_to([128, GB, 128]),
                                                ALU.add).then_inc(xw_ready, 1)
                slots(v, DEPTH, slot)

            @block.gpsimd
            def _(pool):
                def slot(i, parity):
                    if live(i, 3):
                        hold(pool, w_hi, i - 2, passed)
                        for w, raw in ((lstm, lraw), (later, late_raw)):
                            last = nc.gpsimd.tensor_tensor(w[:, LO, i - 3, :], raw[:, i - 3, :],
                                                           f32(w[:, HI, i - 3, :]), ALU.subtract)
                        last.then_inc(w_lo, 1)
                slots(pool, DEPTH, slot)


def l0_lstm(nc, m, x, whole_w):
    with ExitStack() as ctx:
        def sb(name, shape, dt=F32):
            return ctx.enter_context(nc.sbuf_tensor(name, shape, dt))

        gates = sb("gates", [128, 2, 4, 512])
        ig = sb("ig", [128, 2, 512])
        fc = sb("fc", [128, 2, 512])
        cell = sb("cell", [128, 2, 512])
        tanc = sb("tanc", [128, 2, 512])
        hf = sb("hf", [128, 2, 512])
        hs = sb("hs", [128, 2, 2, 512], F32R)
        x_landed = ctx.enter_context(nc.semaphore("b_x"))
        ps = m.ps

        gate_prod, gate_act, cell_done, tanh_done, h_raw, h_hi, h_done, H_done, own, passed = [
            ctx.enter_context(nc.semaphore(f"b_{n}")) for n in (
                "gate_prod", "gate_act", "cell", "tanh", "h_raw", "h_hi", "h", "H", "own", "passed")]

        class Loop:

            def __init__(self, p, before):
                self.p, self.nw = p, T // p
                self.nb = {1: 4, 2: 8, 3: 8, 4: 16}[p]
                self.n = self.nb * self.nw
                self.turns = B // self.nb // 2
                self.steps = 2 * p
                self.order = [(s, q) for s in range(p) for q in range(2)]
                self.gates = [(0, 2, 3) if s == 0 else (0, 2, 1, 3) for s, q in self.order]
                self.ahead = [sum(len(g) for g in self.gates[:k]) for k in range(self.steps + 1)]
                self.per = self.ahead[-1]
                self.own_at = [sum(2 for s, q in self.order[:k] if s) for k in range(self.steps + 1)]
                self.before = before
                self.kept, self.ends = self.steps - 2, 2
                self.step0 = before.step0 + before.steps * before.turns if before else 0
                self.gate0 = before.gate0 + before.per * before.turns if before else 0
                self.kept0 = before.kept0 + before.kept * before.turns if before else 0
                self.end0 = before.end0 + before.ends * before.turns if before else 0
                self.own0 = before.own0 + before.own_at[-1] * before.turns if before else 0
                self.H = m.H[:, :, :, 0:self.nw * p].rearrange("a k (i q b) (w j) -> a k i q b w j", q=2, b=self.nb, j=p)

            def cols(self, ap):
                return ap.rearrange("a (b w) -> a b w", w=self.nw)

            def step(self, i, k):
                return self.steps * i + (self.step0 + k)

            def gate(self, i, k):
                return self.per * i + (self.gate0 + self.ahead[k])

            def own(self, i, k):
                return self.own_at[-1] * i + (self.own0 + self.own_at[k + 1])

            def last(self, i, k):
                if k:
                    return self, i, k - 1
                if isinstance(i, int) and i == 0:
                    return self.before and (self.before, self.before.turns - 1, self.before.steps - 1)
                return self, i - 1, self.steps - 1

        loops = []
        for p in range(1, SKIPS + 1):
            loops.append(Loop(p, loops[-1] if loops else None))

        def all_steps(eng, body):
            for L in loops:
                for k in range(L.steps):
                    body(L, 0, k)
                with eng.Fori(1, L.turns) as i:
                    for k in range(L.steps):
                        body(L, i, k)

        with nc.Block() as block:
            @block.sync
            def _(sp):
                sp.dma_start(m.whole[:, :], whole_w).then_inc(x_landed, 16)
                for k in range(4):
                    c = slice(k * B // 4, (k + 1) * B // 4)
                    sp.dma_start(m.X[:, c, :], x[c].rearrange("b n d -> n b d")).then_inc(x_landed, 16)
                sp.wait_ge(x_landed, 16 * 5)

            @block.gpsimd
            def _(pool):
                def cut(L, i, k):
                    s, q = L.order[k]
                    if s == L.p - 1:
                        hi_, lo_ = [L.H[:, j, i, q, :, :, s] for j in (HI, LO)]
                        hold(pool, h_hi, L.step(i, k) + 1, passed)
                        nc.gpsimd.tensor_tensor(lo_, L.cols(hf[:, q, 0:L.n]), f32(hi_), ALU.subtract).then_inc(H_done, 1)
                all_steps(pool, cut)

            @block.tensor
            def _(pe):
                def step(L, i, k):
                    s, q = L.order[k]
                    first = isinstance(i, int) and k < 2
                    if L.before and first:
                        P = L.before
                        pe.wait_ge(H_done, P.end0 + (q + 1) * L.nb // P.nb)
                    if L.before or not first:
                        M, j, k1 = L.last(i, k)
                        pe.wait_ge(gate_act, M.gate(j, k1))
                    W = m.lstm[:, :, :].rearrange("a k (p w g c) -> a k p w g c", p=SKIPS, w=2, g=4)
                    xh, xl = [L.H[:, j, i, q, :, :, s] for j in (HI, LO)]
                    for g in L.gates[k]:
                        out_ = L.cols(ps[:, 4 * q + g, 0:L.n])
                        last = mm3(nc, out_, W[:, HI, L.p - 1, 0, g, :], W[:, LO, L.p - 1, 0, g, :], xh, xl, True, s == 0)
                        if s == 0:
                            last.then_inc(gate_prod, 1)
                    if s:
                        if L.before and isinstance(i, int) and k == 2:
                            pe.wait_ge(H_done, L.end0)
                        pe.wait_ge(h_done, L.kept * i + (L.kept0 + k - 1))
                        for g in L.gates[k]:
                            mm3(nc, ps[:, 4 * q + g, 0:L.n], W[:, HI, L.p - 1, 1, g, :], W[:, LO, L.p - 1, 1, g, :],
                                hs[:, q, HI, 0:L.n], hs[:, q, LO, 0:L.n], False, True).then_inc(gate_prod, 1)
                all_steps(pe, step)

            @block.scalar
            def _(act):
                def tanh_cell(L, i, k):
                    q = L.order[k][1]
                    act.wait_ge(cell_done, L.step(i, k) + 1)
                    nc.scalar.activation(tanc[:, q, 0:L.n], cell[:, q, 0:L.n], ACT.Tanh).then_inc(tanh_done, 1)

                def step(L, i, k):
                    q = L.order[k][1]
                    for j, g in enumerate(L.gates[k]):
                        if j == 2 and k and L.last(i, k):
                            tanh_cell(*L.last(i, k))
                        if g == 3 and (L.before or not (isinstance(i, int) and k < 2)):
                            act.wait_ge(h_raw, L.step(i, k - 1))
                        act.wait_ge(gate_prod, L.gate(i, k) + j + 1)
                        col = 4 * (L.p - 1) + g
                        nc.scalar.activation(gates[:, q, g, 0:L.n], ps[:, 4 * q + g, 0:L.n],
                                             ACT.Tanh if g == 2 else ACT.Sigmoid,
                                             bias=m.lbias[:, col:col + 1]).then_inc(gate_act, 1)
                    if k == 0 and L.last(i, k):
                        tanh_cell(*L.last(i, k))
                all_steps(act, step)
                L = loops[-1]
                tanh_cell(L, L.turns - 1, L.steps - 1)

            @block.vector
            def _(v):
                def state(L, i, k):
                    s, q = L.order[k]
                    v.wait_ge(tanh_done, L.step(i, k) + 1)
                    if k < 2:
                        wait(v, H_done, L.ends * i + (L.end0 + k - 1))
                    nc.vector.tensor_tensor(hf[:, q, 0:L.n], gates[:, q, 3, 0:L.n], tanc[:, q, 0:L.n],
                                            ALU.mult).then_inc(h_raw, 1)
                    if s == L.p - 1:
                        hi_, lo_ = [L.H[:, j, i, q, :, :, s] for j in (HI, LO)]
                        new = L.cols(hf[:, q, 0:L.n])
                    else:
                        hi_, lo_ = [hs[:, q, j, 0:L.n] for j in (HI, LO)]
                        new = hf[:, q, 0:L.n]
                    v.wait_ge(h_raw, L.step(i, k) + 1)
                    nc.vector.tensor_copy(hi_, new).then_inc(h_hi, 1)
                    if s < L.p - 1:
                        v.wait_ge(h_hi, L.step(i, k) + 1)
                        nc.vector.tensor_tensor(lo_, new, f32(hi_), ALU.subtract).then_inc(h_done, 1)

                def step(L, i, k):
                    s, q = L.order[k]
                    i_, f_, g_ = [gates[:, q, g, 0:L.n] for g in range(3)]
                    c_ = cell[:, q, 0:L.n]
                    v.wait_ge(gate_act, L.gate(i, k) + 2)
                    if s == 0:
                        nc.vector.tensor_tensor(c_, i_, g_, ALU.mult).then_inc(cell_done, 1)
                    else:
                        nc.vector.tensor_tensor(ig[:, q, 0:L.n], i_, g_, ALU.mult).then_inc(own, 1)
                    if L.last(i, k):
                        state(*L.last(i, k))
                    if s:
                        v.wait_ge(gate_act, L.gate(i, k) + 3)
                        nc.vector.tensor_tensor(fc[:, q, 0:L.n], f_, c_, ALU.mult).then_inc(own, 1)
                        v.wait_ge(own, L.own(i, k))
                        nc.vector.tensor_tensor(c_, ig[:, q, 0:L.n], fc[:, q, 0:L.n], ALU.add).then_inc(cell_done, 1)
                all_steps(v, step)
                L = loops[-1]
                state(L, L.turns - 1, L.steps - 1)


def finish_norm(nc, v, m, stats, ctx, tag, rec):
    chain = Chain(v, ctx.enter_context(nc.semaphore(f"{tag}_gather")))
    S = stats[:, :, :]
    t = ctx.enter_context(nc.sbuf_tensor(f"{tag}_t", [128, 2, B], F32))
    chain(nc.vector.tensor_tensor(t[:, 0, :], S[:, :, 1], S[:, :, 4], ALU.subtract))
    chain(nc.vector.tensor_tensor(t[:, 1, :], S[:, :, 2], S[:, :, 5], ALU.add))
    chain(nc.vector.tensor_tensor(m.mean[:, :], S[:, :, 1], S[:, :, 4], ALU.add))
    chain(nc.vector.tensor_scalar(m.mean[:, :], m.mean[:, :], 0.5, None, ALU.mult))
    chain(nc.vector.tensor_tensor(t[:, 0, :], t[:, 0, :], t[:, 0, :], ALU.mult))
    chain(nc.vector.scalar_tensor_tensor(out=t[:, 1, :], in0=t[:, 0, :], scalar=float(D // 4), in1=t[:, 1, :],
                                         op0=ALU.mult, op1=ALU.add))
    chain(nc.vector.tensor_scalar(m.rstd[:, :], t[:, 1, :], 1.0 / D, EPS_NORM, ALU.mult, ALU.add))
    nc.vector.reciprocal(m.rstd[:, :], m.rstd[:, :]).then_inc(rec, 1)


def root_norm(nc, act, m, rec, root):
    act.wait_ge(rec, 1)
    nc.scalar.activation(m.rstd[:, :], m.rstd[:, :], ACT.Sqrt).then_inc(root, 1)


def norm_group(nc, m, out, y, g):
    mean = m.mean[:, :].rearrange("p (g b) -> p g b", b=GB)
    rstd = m.rstd[:, :].rearrange("p (g b) -> p g b", b=GB)
    for b, (o, x) in enumerate(zip(group4(out), group4(y))):
        last = nc.vector.tensor_scalar(o, x, mean[:, g, b:b + 1], rstd[:, g, b:b + 1], ALU.subtract, ALU.mult)
    return last


def add_and_count(nc, v, X, ps, stats, g, added, counted):
    nc.vector.tensor_tensor(X[:, g, :], ps, X[:, g, :], ALU.add).then_inc(added, 1)
    v.wait_ge(added, g + 1)
    S = stats[:, :, :].rearrange("p (g b) s -> p g b s", b=GB)
    for b, x in enumerate(group4(X[:, g, :])):
        last = nc.vector.bn_stats(S[:, g, b, :], x)
    last.then_inc(counted, 1)


def group_stats(nc, pool, S, ln, g, steps, passed):
    mean_, diff, var = [ln[:, k, :] for k in range(3)]
    nc.gpsimd.tensor_tensor(mean_, S[:, g, :, 1], S[:, g, :, 4], ALU.add)
    nc.gpsimd.tensor_tensor(diff, S[:, g, :, 1], S[:, g, :, 4], ALU.subtract)
    nc.gpsimd.tensor_tensor(var, S[:, g, :, 2], S[:, g, :, 5], ALU.add).then_inc(steps[0], 1)
    hold(pool, steps[0], g + 1, passed)
    nc.gpsimd.tensor_scalar(mean_, mean_, 0.5, None, ALU.mult)
    nc.gpsimd.tensor_tensor(diff, diff, diff, ALU.mult).then_inc(steps[1], 1)
    hold(pool, steps[1], g + 1, passed)
    nc.gpsimd.tensor_scalar(diff, diff, float(D // 4), None, ALU.mult).then_inc(steps[2], 1)
    hold(pool, steps[2], g + 1, passed)
    nc.gpsimd.tensor_tensor(var, var, diff, ALU.add).then_inc(steps[3], 1)


def late(m, name, k, a=0, b=None):
    c0, c1 = LATE[name]
    return m.late[:, k, c0 + a:(c1 if b is None else c0 + b)]


def whole(m, name, tile=0, width=128):
    return m.whole[:, WHOLE[name][0] + tile * width:WHOLE[name][0] + (tile + 1) * width]


def batch_coef(nc, v, act_wait, chain, stats, gamma, beta, scale, shift, tmp, rec_sem, root_sem):
    chain(nc.vector.bn_aggr(tmp[:, 0:2], stats))
    chain(nc.vector.tensor_scalar(tmp[:, 2:3], tmp[:, 1:2], EPS_NORM, None, ALU.add))
    nc.vector.reciprocal(tmp[:, 3:4], tmp[:, 2:3]).then_inc(rec_sem, 1)
    v.wait_ge(root_sem, act_wait)
    chain(nc.vector.tensor_tensor(scale, gamma, tmp[:, 4:5], ALU.mult))
    chain(nc.vector.tensor_tensor(tmp[:, 5:6], tmp[:, 0:1], scale, ALU.mult))
    chain(nc.vector.tensor_tensor(shift, beta, tmp[:, 5:6], ALU.subtract))


def l1_first(nc, m):
    with ExitStack() as ctx:
        def sb(name, shape, dt=F32):
            return ctx.enter_context(nc.sbuf_tensor(name, shape, dt))

        def sem(name):
            return ctx.enter_context(nc.semaphore(name))

        hsum = sb("c_hsum", [128, 2, GN])
        xs = sb("c_xs", [128, 2, GN])
        agg = sb("c_agg", [128, 2, GN])
        stats = sb("c_stats", [128, B, 6])
        ln = sb("c_ln", [128, 2, 4, GB])
        eps = sb("c_eps", [128, 1])
        st1 = sb("c_st1", [128, 2, NG, 6])
        tmp = sb("c_tmp", [128, 2, 8])
        H = m.H[:, :, :, :].rearrange("p k (g b) t -> p k g (b t)", b=GB)
        X = m.X[:, :, :].rearrange("p (g b) d -> p g (b d)", b=GB)
        S = stats[:, :, :].rearrange("p (g b) s -> p g b s", b=GB)
        pre1 = m.pre1[:, :, :, :].rearrange("p k (g b) t -> p k g (b t)", b=GB)
        ps = m.ps
        halves = [sem(f"c1_ln{n}") for n in range(4)]
        summed, turned, added, counted, rooted, ready, normed, stored, agged, copied, wide, kept, judged = [
            sem(f"c1_{n}") for n in ("summed", "turned", "added", "counted", "rooted", "ready", "normed", "stored",
                                     "agged", "copied", "wide", "kept", "judged")]
        rec, root, chs, made, passed = [sem(f"c1_{n}") for n in ("rec", "root", "chain", "made", "passed")]
        DEPTH = 5
        with nc.Block() as block:
            @block.gpsimd
            def _(pool):
                nc.gpsimd.memset(eps[:, :], EPS_NORM).then_inc(made, 1)

                def slot(i, parity):
                    if live(i, 0):
                        hold(pool, turned, i - 1, passed)
                        nc.gpsimd.tensor_tensor(hsum[:, parity, :], f32(H[:, HI, i, :]), f32(H[:, LO, i, :]),
                                                ALU.add).then_inc(summed, 1)
                    if live(i, 2):
                        hold(pool, counted, i - 1, passed)
                        hold(pool, normed, i - 3, passed)
                        group_stats(nc, pool, S, ln[:, parity, :, :], i - 2, halves, passed)
                slots(pool, DEPTH, slot, 4)

            @block.vector
            def _(v):
                def slot(i, parity):
                    u = (parity + 1) % 2
                    if live(i, 2):
                        v.wait_ge(turned, i - 1)
                        add_and_count(nc, v, X, ps[:, 1, :], stats, i - 2, added, counted)
                    if live(i, 3):
                        v.wait_ge(rooted, i - 2)
                        nc.vector.reciprocal(ln[:, u, 3, :], ln[:, u, 3, :]).then_inc(ready, 1)
                        wait(v, agged, i - 4)
                        wait(v, stored, i - 4)
                        v.wait_ge(ready, i - 2)
                        for b, (o, x) in enumerate(zip(group4(xs[:, u, :]), group4(X[:, i - 3, :]))):
                            last = nc.vector.tensor_scalar(o, x, ln[:, u, 0, b:b + 1], ln[:, u, 3, b:b + 1],
                                                           ALU.subtract, ALU.mult)
                        last.then_inc(normed, 1)
                    if live(i, 5):
                        for t in range(2):
                            v.wait_ge(kept, 2 * (i - 5) + t + 1)
                            nc.vector.bn_stats(st1[:, t, i - 5, :], pre1[:, t, i - 5, :]).then_inc(judged, 1)
                slots(v, DEPTH, slot, 4)
                v.wait_ge(judged, 2 * NG)
                chain = Chain(v, chs)
                for t in range(2):
                    batch_coef(nc, v, t + 1, chain, st1[:, t, :, :].rearrange("p g s -> p (g s)"),
                               m.vec[:, V_G1 + t:V_G1 + t + 1], m.vec[:, V_BE1 + t:V_BE1 + t + 1],
                               m.bn1[:, 0, t:t + 1], m.bn1[:, 1, t:t + 1], tmp[:, t, :], rec, root)

            @block.scalar
            def _(act):
                act.wait_ge(made, 1)

                def slot(i, parity):
                    u = (parity + 1) % 2
                    if live(i, 4):
                        wait(act, wide, 2 * (i - 5))
                        act.wait_ge(agged, i - 3)
                        nc.scalar.activation(agg[:, parity, :], ps[:, 0, :], ACT.Copy).then_inc(copied, 1)
                    if live(i, 5):
                        for t in range(2):
                            act.wait_ge(wide, 2 * (i - 5) + t + 1)
                            nc.scalar.activation(pre1[:, t, i - 5, :], ps[:, 2 * u + 2 + t, :], ACT.Identity,
                                                 bias=m.vec[:, V_B1 + t:V_B1 + t + 1]).then_inc(kept, 1)
                    if live(i, 3):
                        act.wait_ge(normed, i - 2)
                        nc.scalar.activation(X[:, i - 3, :], xs[:, u, :], ACT.Copy).then_inc(stored, 1)
                    if live(i, 2):
                        act.wait_ge(halves[3], i - 1)
                        nc.scalar.activation(ln[:, parity, 3, :], ln[:, parity, 2, :], ACT.Sqrt, bias=eps[:, 0:1],
                                             scale=1.0 / D).then_inc(rooted, 1)
                slots(act, DEPTH, slot, 4)
                for t in range(2):
                    act.wait_ge(rec, t + 1)
                    nc.scalar.activation(tmp[:, t, 4:5], tmp[:, t, 3:4], ACT.Sqrt).then_inc(root, 1)

            @block.tensor
            def _(pe):
                def slot(i, parity):
                    u = (parity + 1) % 2
                    if live(i, 4):
                        pe.wait_ge(normed, i - 3)
                        wait(pe, copied, i - 4)
                        mm_each(nc, ps[:, 0, :], xs[:, parity, :], m.ahat[:, :]).then_inc(agged, 1)
                    if live(i, 5):
                        pe.wait_ge(copied, i - 4)
                        wait(pe, kept, 2 * (i - 6))
                        for t in range(2):
                            nc.tensor.matmul(ps[:, 2 * u + 2 + t, :], whole(m, "L1W1", t), agg[:, u, :],
                                             start=True, stop=True).then_inc(wide, 1)
                    if live(i, 1):
                        pe.wait_ge(summed, i)
                        wait(pe, added, i - 1)
                        for o, h in zip(group4(ps[:, 1, :]), group4(hsum[:, u, :])):
                            last = nc.tensor.transpose(o, h, m.ident[:, :])
                        last.then_inc(turned, 1)
                slots(pe, DEPTH, slot, 4)


def l1_second(nc, m):
    with ExitStack() as ctx:
        def sb(name, shape, dt=F32):
            return ctx.enter_context(nc.sbuf_tensor(name, shape, dt))

        def sem(name):
            return ctx.enter_context(nc.semaphore(name))

        st2 = sb("c_st2", [128, NG, 6])
        tmp = sb("c_tmp2", [128, 8])
        pre1 = m.pre1[:, :, :, :].rearrange("p k (g b) t -> p k g (b t)", b=GB)
        pre2 = m.pre2[:, :, :].rearrange("p (g b) t -> p g (b t)", b=GB)
        ps = m.ps
        hid = sb("c_hid", [128, 2, 2, GN])
        relu, prod, kept2, counted2, rec2, root2, chs2 = [sem(f"c2_{n}") for n in (
            "relu", "prod", "kept", "counted", "rec", "root", "chain")]
        with nc.Block() as block:
            @block.scalar
            def _(act):
                def slot(i, parity):
                    if live(i, 0):
                        wait(act, prod, i - 1)
                        for t in range(2):
                            nc.scalar.activation(hid[:, parity, t, :], pre1[:, t, i, :], ACT.Relu, bias=m.bn1[:, 1, t:t + 1],
                                                 scale=m.bn1[:, 0, t:t + 1]).then_inc(relu, 1)
                slots(act, 1, slot, 4)
                act.wait_ge(rec2, 1)
                nc.scalar.activation(tmp[:, 4:5], tmp[:, 3:4], ACT.Sqrt).then_inc(root2, 1)

            @block.vector
            def _(v):
                def slot(i, parity):
                    if live(i, 1):
                        v.wait_ge(prod, i)
                        nc.vector.tensor_scalar(pre2[:, i - 1, :], ps[:, (parity + 1) % 2, :], m.vec[:, V_B2:V_B2 + 1],
                                                None, ALU.add).then_inc(kept2, 1)
                        v.wait_ge(kept2, i)
                        nc.vector.bn_stats(st2[:, i - 1, :], pre2[:, i - 1, :]).then_inc(counted2, 1)
                slots(v, 1, slot, 4)
                v.wait_ge(counted2, NG)
                batch_coef(nc, v, 1, Chain(v, chs2), st2[:, :, :].rearrange("p g s -> p (g s)"),
                           m.vec[:, V_G2:V_G2 + 1], m.vec[:, V_BE2:V_BE2 + 1], m.bn2[:, 0:1], m.bn2[:, 1:2],
                           tmp[:, :], rec2, root2)

            @block.tensor
            def _(pe):
                def slot(i, parity):
                    if live(i, 1):
                        q = (parity + 1) % 2
                        pe.wait_ge(relu, 2 * i)
                        wait(pe, kept2, i - 2)
                        for t in range(2):
                            last = nc.tensor.matmul(ps[:, q, :], whole(m, "L1W2", t), hid[:, q, t, :], start=t == 0,
                                                    stop=t == 1)
                        last.then_inc(prod, 1)
                slots(pe, 1, slot, 4)


def l2(nc, m):
    with ExitStack() as ctx:
        def sb(name, shape, dt=F32, c=ctx):
            return c.enter_context(nc.sbuf_tensor(name, shape, dt))

        def sem(name):
            return ctx.enter_context(nc.semaphore(name))

        V = sb("V", [128, 2, NG, GB, D], F32R)
        se = sb("se", [128, 2, E])
        pack = sb("d_pack", [GB * HEADS, 2, E])
        attn = sb("attn", [128, ET, NG, GB * HEADS])
        stats = sb("d_stats", [128, B, 6])
        X = m.X[:, :, :].rearrange("p (g b) d -> p g (b d)", b=GB)
        pre2 = m.pre2[:, :, :].rearrange("p (g b) t -> p g (b t)", b=GB)
        S = stats[:, :, :].rearrange("p (g b) s -> p g b s", b=GB)
        ps = m.ps
        passed = sem("d_passed")

        run = sb("s_run", [128, E])
        top = sb("s_top", [128, E])
        BELOW, WEIGHTS = 4, 4

        def below_maximum(chain, k):
            e = se[:, k, :]
            chain(nc.vector.tensor_tensor(e, e, m.loga[:, :], ALU.add))
            chain(nc.vector.tensor_tensor_scan(run[:, :], m.pen[:, 0:E], e, NEG, ALU.add, ALU.max))
            chain(nc.vector.tensor_tensor_scan(top[:, ::-1], m.pen[:, E:0:-1], run[:, ::-1], NEG, ALU.add, ALU.max))
            chain(nc.vector.tensor_tensor(e, e, top[:, :], ALU.subtract))

        def weights(chain, k):
            e = se[:, k, :]
            chain(nc.vector.tensor_tensor_scan(run[:, :], m.same[:, 0:E], e, 0.0, ALU.mult, ALU.add))
            chain(nc.vector.tensor_tensor_scan(top[:, ::-1], m.same[:, E:0:-1], run[:, ::-1], 0.0, ALU.mult, ALU.max))
            chain(nc.vector.reciprocal(top[:, :], top[:, :]))
            chain(nc.vector.tensor_tensor(e, e, top[:, :], ALU.mult))

        DEPTH = 7
        SOFT_MAX, SOFT_EXP, SOFT_SUM = NG + 2, NG + 3, NG + 5
        soft, soft_exp = sem("d1_soft"), sem("d1_soft_exp")
        with ExitStack() as c1:
            z = sb("d_z", [128, 2, GN], F32, c1)
            ln = sb("d_ln", [128, 2, 4, GB], F32, c1)
            eps = sb("d_eps", [128, 1], F32, c1)
            xs = sb("d_xs", [128, 2, GN], F32, c1)
            xt = sb("d_xt", [128, 2, 2, GN], F32R, c1)
            q = sb("d_q", [128, 2, 2, GB, D], F32R, c1)
            z2 = sb("d_z2", [128, GB, E], F32, c1)
            lz = sb("d_lz", [128, 2, GB, E], F32, c1)
            halves = [sem(f"d1_ln{n}") for n in range(4)]
            scaled, back, added, counted, rooted, ready, made = [sem(f"d1_{n}") for n in (
                "scaled", "back", "added", "counted", "rooted", "ready", "made")]
            (centred, normed, copied, turned, thi, tlo, qv, qvhi, qvlo, summed, sloped, leaked, scored, saved, moved0,
             moved1) = [
                sem(f"d1_{n}") for n in ("centred", "normed", "copied", "turned", "thi", "tlo", "qv", "qvhi", "qvlo",
                                         "summed", "sloped", "leaked", "scored", "saved", "moved0", "moved1")]
            moved = (moved0, moved1)
            qvp = ps[:, 2:4, :].rearrange("p k (b w d) -> p (k b) w d", b=2, w=2)
            sums = ps[:, 4:6, :].rearrange("p k (b e) -> p (k b) e", b=2)
            Q_, V_ = 0, 1
            with nc.Block() as block:
                @block.sync
                def _(sp):
                    for g in range(NG):
                        p0 = g % (NG // 2) * GB * HEADS
                        sp.wait_ge(saved, g + 1)
                        sp.dma_start(se[p0:p0 + GB * HEADS, g // (NG // 2), :], pack[:, g % 2, :]).then_inc(moved[g % 2], 16)
                    for u in range(2):
                        sp.wait_ge(moved[u], 16 * NG // 2)

                @block.gpsimd
                def _(pool):
                    nc.gpsimd.memset(eps[:, :], EPS_NORM).then_inc(made, 1)

                    def slot(i, parity):
                        if live(i, 1):
                            g, u = i - 1, (parity + 1) % 2
                            hold(pool, counted, i, passed)
                            group_stats(nc, pool, S, ln[:, u, :, :], g, halves, passed)
                            hold(pool, turned, i - 2, passed)
                            hold(pool, copied, i - 2, passed)
                            x2 = xs[:, u, :].rearrange("p (b d) -> p b d", b=GB)
                            nc.gpsimd.tensor_tensor(x2, X[:, g, :].rearrange("p (b d) -> p b d", b=GB),
                                                    ln[:, u, 0, :].unsqueeze(2).broadcast_to([128, GB, D]),
                                                    ALU.subtract).then_inc(centred, 1)
                            hold(pool, centred, i, passed)
                            hold(pool, ready, i, passed)
                            nc.gpsimd.tensor_tensor(x2, x2, ln[:, u, 3, :].unsqueeze(2).broadcast_to([128, GB, D]),
                                                    ALU.mult).then_inc(normed, 1)
                    slots(pool, DEPTH, slot)

                @block.tensor
                def _(pe):
                    def slot(i, parity):
                        u = (parity + 1) % 2
                        if live(i, 6):
                            pe.wait_ge(qvlo, 2 * (i - 6) + 2)
                            wait(pe, leaked, i - 6)
                            for b in range(GB):
                                nc.tensor.matmul(sums[:, b, :], q[:, parity, HI, b, :], m.st[:, :], start=True, stop=False)
                                last = nc.tensor.matmul(sums[:, b, :], q[:, parity, LO, b, :], m.st[:, :], start=False,
                                                        stop=True)
                            last.then_inc(summed, 1)
                        if live(i, 3):
                            pe.wait_ge(normed, i - 2)
                            wait(pe, tlo, i - 3)
                            for o, c in zip(group4(ps[:, 0, :]), group4(xs[:, u, :])):
                                last = nc.tensor.transpose(o, c, m.ident[:, :])
                            last.then_inc(turned, 1)
                        if live(i, 4):
                            pe.wait_ge(tlo, i - 3)
                            wait(pe, qvlo, 2 * (i - 4))
                            for b, (h_, l_) in enumerate(zip(group4(xt[:, parity, HI, :]), group4(xt[:, parity, LO, :]))):
                                last = mm3(nc, ps[:, 2 + b // 2, (b % 2) * 256:(b % 2) * 256 + 256], h_, l_,
                                           late(m, "QV", HI), late(m, "QV", LO), True, True)
                            last.then_inc(qv, 1)
                        if live(i, 7):
                            pe.wait_ge(leaked, i - 6)
                            wait(pe, saved, i - 8)
                            for b in range(GB):
                                last = nc.tensor.matmul(ps[0:GB * HEADS, 6 + u, 0:E], m.score[:, b, :],
                                                        lz[:, u, b, :], start=b == 0, stop=b == GB - 1)
                            last.then_inc(scored, 1)
                        if live(i, 0):
                            pe.wait_ge(scaled, i + 1)
                            wait(pe, added, i)
                            for o, c in zip(group4(ps[:, 1, :]), group4(z[:, parity, :])):
                                last = nc.tensor.transpose(o, c, m.ident[:, :])
                            last.then_inc(back, 1)
                    slots(pe, DEPTH, slot)

                @block.scalar
                def _(act):
                    act.wait_ge(made, 1)

                    def slot(i, parity):
                        u = (parity + 1) % 2
                        if live(i, 0):
                            wait(act, back, i - 1)
                            nc.scalar.activation(z[:, parity, :], pre2[:, i, :], ACT.Identity, bias=m.bn2[:, 1:2],
                                                 scale=m.bn2[:, 0:1]).then_inc(scaled, 1)
                        if live(i, 6):
                            act.wait_ge(summed, i - 5)
                            nc.scalar.activation(z2[:, :, :], sums, ACT.Copy, scale=SLOPE).then_inc(sloped, 1)
                        if live(i, 3):
                            act.wait_ge(turned, i - 2)
                            take_hi(nc, xt[:, u, HI, :], ps[:, 0, :]).then_inc(thi, 1)
                        if live(i, 4):
                            act.wait_ge(qv, i - 3)
                            take_hi(nc, V[:, HI, i - 4, :, :], qvp[:, :, V_, :]).then_inc(qvhi, 1)
                            take_hi(nc, q[:, parity, HI, :, :], qvp[:, :, Q_, :]).then_inc(qvhi, 1)
                        if live(i, 1):
                            act.wait_ge(halves[3], i)
                            nc.scalar.activation(ln[:, u, 3, :], ln[:, u, 2, :], ACT.Sqrt, bias=eps[:, 0:1],
                                                 scale=1.0 / D).then_inc(rooted, 1)
                        if live(i, 3):
                            nc.scalar.activation(X[:, i - 3, :], xs[:, u, :], ACT.Copy).then_inc(copied, 1)
                        if isinstance(i, int) and i == SOFT_EXP:
                            act.wait_ge(soft, BELOW)
                            nc.scalar.activation(se[:, 0, :], se[:, 0, :], ACT.Exp).then_inc(soft_exp, 1)
                    slots(act, DEPTH, slot)

                @block.vector
                def _(v):
                    soft_chain = Chain(v, soft)

                    def slot(i, parity):
                        u = (parity + 1) % 2
                        if live(i, 1):
                            v.wait_ge(back, i)
                            add_and_count(nc, v, X, ps[:, 1, :], stats, i - 1, added, counted)
                        if live(i, 6):
                            v.wait_ge(sloped, i - 5)
                            wait(v, scored, i - 7)
                            nc.vector.tensor_tensor(lz[:, parity, :, :], sums, z2[:, :, :], ALU.max).then_inc(leaked, 1)
                        if live(i, 3):
                            v.wait_ge(thi, i - 2)
                            take_lo(nc, xt[:, u, LO, :], ps[:, 0, :], xt[:, u, HI, :]).then_inc(tlo, 1)
                        if live(i, 4):
                            v.wait_ge(qvhi, 2 * (i - 4) + 2)
                            take_lo(nc, V[:, LO, i - 4, :, :], qvp[:, :, V_, :], V[:, HI, i - 4, :, :]).then_inc(qvlo, 1)
                            take_lo(nc, q[:, parity, LO, :, :], qvp[:, :, Q_, :], q[:, parity, HI, :, :]).then_inc(qvlo, 1)
                        if live(i, 1):
                            v.wait_ge(rooted, i)
                            nc.vector.reciprocal(ln[:, u, 3, :], ln[:, u, 3, :]).then_inc(ready, 1)
                        if live(i, 7):
                            v.wait_ge(scored, i - 6)
                            wait(v, moved[u], 8 * (i - 7 - u))
                            nc.vector.tensor_copy(pack[:, u, :], ps[0:GB * HEADS, 6 + u, 0:E]).then_inc(saved, 1)
                        if isinstance(i, int) and i == SOFT_MAX:
                            for n in moved:
                                v.wait_ge(n, 16 * NG // 4)
                            below_maximum(soft_chain, 0)
                        if isinstance(i, int) and i == SOFT_SUM:
                            v.wait_ge(soft_exp, 1)
                            weights(soft_chain, 0)
                    slots(v, DEPTH, slot)

        dv, pe_s, ac = sem("d2_dv"), sem("d2_pe"), sem("d2_ac")
        at_ = attn[:, :, :, :].rearrange("p t g s -> p t (g s)")
        with nc.Block() as block:
            @block.vector
            def _(v):
                chain = Chain(v, dv)
                below_maximum(chain, 1)
                v.wait_ge(ac, 1)
                weights(chain, 1)
                v.wait_ge(pe_s, 1)
                chain(nc.vector.tensor_copy(at_[:, :, :], ps[:, 1, :].rearrange("p (t s) -> p t s", t=ET)))

            @block.tensor
            def _(pe):
                pe.wait_ge(dv, BELOW + WEIGHTS)
                for t in range(ET):
                    for k in range(2):
                        last = nc.tensor.transpose(ps[:, 1, (t * 2 + k) * 128:(t * 2 + k + 1) * 128],
                                                   se[:, k, t * 128:(t + 1) * 128], m.ident[:, :])
                last.then_inc(pe_s, 1)

            @block.scalar
            def _(act):
                act.wait_ge(dv, BELOW)
                nc.scalar.activation(se[:, 1, :], se[:, 1, :], ACT.Exp).then_inc(ac, 1)

        with ExitStack() as c3:
            av = sb("e_av", [128, 2, ET, GN], F32, c3)
            y = sb("e_y", [128, GN], F32, c3)
            taken, weighed, summed, copied, out_, added, counted, rec, root = [sem(f"d3_{n}") for n in (
                "taken", "weighed", "summed", "copied", "out", "added", "counted", "rec", "root")]
            with nc.Block() as block:
                @block.tensor
                def _(pe):
                    def slot(i, parity):
                        if live(i, 2):
                            pe.wait_ge(weighed, i - 1)
                            for b, o in enumerate(group4(ps[:, 4, :])):
                                for t in range(ET):
                                    last = nc.tensor.matmul(o, av[:, parity, t, b * 128:(b + 1) * 128], m.srce[:, t, :],
                                                            start=t == 0, stop=t == ET - 1)
                            last.then_inc(summed, 1)
                        if live(i, 0):
                            wait(pe, weighed, i - 1)
                            for t in range(ET):
                                w = m.dstn[:, t * 128:(t + 1) * 128]
                                o = ps[:, 2 * parity + t, :]
                                nc.tensor.matmul(o, w, V[:, HI, i, :, :].rearrange("p b d -> p (b d)"), start=True, stop=False)
                                last = nc.tensor.matmul(o, w, V[:, LO, i, :, :].rearrange("p b d -> p (b d)"),
                                                        start=False, stop=True)
                            last.then_inc(taken, 1)
                        if live(i, 2):
                            pe.wait_ge(copied, i - 1)
                            wait(pe, added, i - 2)
                            mm_each(nc, ps[:, 5, :], y, whole(m, "WOUT")).then_inc(out_, 1)
                    slots(pe, 2, slot, 4)

                @block.vector
                def _(v):
                    def slot(i, parity):
                        if live(i, 0):
                            v.wait_ge(taken, i + 1)
                            wait(v, summed, i - 1)
                            for t in range(ET):
                                last = nc.vector.tensor_tensor(
                                    av[:, parity, t, :].rearrange("p (s d) -> p s d", d=HD),
                                    ps[:, 2 * parity + t, :].rearrange("p (s d) -> p s d", d=HD),
                                    attn[:, t, i, :].unsqueeze(2).broadcast_to([128, GB * HEADS, HD]), ALU.mult)
                            last.then_inc(weighed, 1)
                        if live(i, 2):
                            v.wait_ge(out_, i - 1)
                            add_and_count(nc, v, X, ps[:, 5, :], stats, i - 2, added, counted)
                    slots(v, 2, slot, 4)
                    v.wait_ge(counted, NG)
                    finish_norm(nc, v, m, stats, c3, "e", rec)

                @block.scalar
                def _(act):
                    def slot(i, parity):
                        if live(i, 2):
                            act.wait_ge(summed, i - 1)
                            nc.scalar.activation(y[:, :], ps[:, 4, :], ACT.Copy).then_inc(copied, 1)
                    slots(act, 2, slot, 4)
                    root_norm(nc, act, m, rec, root)


def l3(nc, m, out):
    with ExitStack() as ctx:
        def sb(name, shape, dt=F32):
            return ctx.enter_context(nc.sbuf_tensor(name, shape, dt))

        def sem(name):
            return ctx.enter_context(nc.semaphore(name))

        xs = sb("f_xs", [128, GN])
        ax = sb("f_ax", [128, 2, GN], F32R)
        h1 = sb("f_h1", [128, 2, GN])
        a1 = sb("f_a1", [128, 2, 2, GN], F32R)
        h2 = sb("f_h2", [128, 4, GN])
        s3 = sb("f_s3", [128, 2, GN], F32R)
        stats = sb("f_stats", [128, B, 6])
        ln = sb("f_ln", [128, 2, 4, GB])
        power = sb("f_power", [128, GB])
        res = sb("f_res", [128, 2, GN])
        X = m.X[:, :, :].rearrange("p (g b) d -> p g (b d)", b=GB)
        S = stats[:, :, :].rearrange("p (g b) s -> p g b s", b=GB)
        outd = out.rearrange("(g b) n d -> n g b d", b=GB)
        ps = m.ps
        normed, copied, last_prod, added, counted, ready, written, passed = [sem(f"f_{n}") for n in (
            "normed", "copied", "last", "added", "counted", "ready", "written", "passed")]
        halves = [sem(f"f_ln{n}") for n in range(5)]
        prod, hi, lo = [[sem(f"f_{n}{s}") for s in range(5)] for n in ("prod", "hi", "lo")]
        stored = [sem(f"f_stored{u}") for u in range(2)]

        BEHIND = (1, 1, 1, 2, 2)
        PARTS = (1, 2, 2, 4, 1)
        RELU = (False, True, False, True, False)
        BANK = ((0,), (1, 2), (3, 1), (4, 5, 6, 7), (5,))
        LAST_BANK = 3
        LAST, NEXT = "last", "next"
        ORDER = [(0, 0), (3, 0), LAST, (3, 1), (1, 0), (1, 1), (3, 2), (3, 3), (2, 0), (2, 1), NEXT, (4, 0)]
        DEPTH = 4
        BUF = (ax, h1, a1, h2, s3)

        def pair(s, part):
            return [BUF[s][:, k, :] if PARTS[s] == 1 else BUF[s][:, k, part, :] for k in (HI, LO)]

        def count(s, k, g):
            return PARTS[s] * g + k + 1

        def product(s, k):
            o = ps[:, BANK[s][k], :]
            if s == 0:
                last = mm_each(nc, o, xs, m.adj2[:, :])
            elif s == 1:
                for b in range(2):
                    c = slice((2 * k + b) * 128, (2 * k + b + 1) * 128)
                    last = mm3(nc, o[:, b * 256:(b + 1) * 256], ax[:, HI, c], ax[:, LO, c], late(m, "L3W1", HI),
                               late(m, "L3W1", LO), True, True)
            elif s == 2:
                for b, ob in enumerate(group4(o)):
                    c = slice((b % 2) * 256 + k * 128, (b % 2) * 256 + (k + 1) * 128)
                    last = nc.tensor.matmul(ob, h1[:, b // 2, c], m.adj2[:, :], start=True, stop=True)
            elif s == 3:
                for t in range(2):
                    c = 512 * t + 128 * k
                    last = mm3(nc, o, late(m, "L3W2", HI, c, c + 128), late(m, "L3W2", LO, c, c + 128),
                               a1[:, HI, t, :], a1[:, LO, t, :], t == 0, t == 1)
            else:
                for b, ob in enumerate(group4(o)):
                    c = slice(b * 128, (b + 1) * 128)
                    for t in range(4):
                        last = nc.tensor.matmul(ob, h2[:, t, c], whole(m, "L3W3", t), start=t == 0, stop=t == 3)
            return last

        def stores(g, parity):
            return 8 * (g + 2 - parity)

        with nc.Block() as block:
            @block.tensor
            def _(pe):
                def slot(i, parity):
                    for what in ORDER:
                        if what == NEXT:
                            continue
                        if what == LAST:
                            if live(i, 3):
                                pe.wait_ge(lo[4], i - 2)
                                mm3(nc, ps[:, LAST_BANK, :], m.adj2s[:, HI, :], m.adj2s[:, LO, :], s3[:, HI, :], s3[:, LO, :],
                                    True, True).then_inc(last_prod, 1)
                            continue
                        s, k = what
                        g = i - BEHIND[s]
                        if not live(i, BEHIND[s]):
                            continue
                        if s == 0:
                            pe.wait_ge(normed, g + 1)
                        elif k == 0:
                            pe.wait_ge((hi if RELU[s - 1] else lo)[s - 1], count(s - 1, PARTS[s - 1] - 1, g))
                        if (s, k) == (2, 0):
                            wait(pe, added, i - 2)
                        product(s, k).then_inc(prod[s], 1)
                slots(pe, DEPTH, slot)

            @block.scalar
            def _(act):
                def slot(i, parity):
                    for what in ORDER:
                        if what == NEXT and live(i, 0):
                            act.wait_ge(normed, i + 1)
                            nc.scalar.activation(X[:, i, :], xs[:, :], ACT.Copy).then_inc(copied, 1)
                        if what in (NEXT, LAST) or not live(i, BEHIND[what[0]]):
                            continue
                        s, k = what
                        act.wait_ge(prod[s], count(s, k, i - BEHIND[s]))
                        if RELU[s]:
                            nc.scalar.activation(BUF[s][:, k, :], ps[:, BANK[s][k], :], ACT.Relu).then_inc(hi[s], 1)
                        else:
                            take_hi(nc, pair(s, k)[HI], ps[:, BANK[s][k], :]).then_inc(hi[s], 1)
                slots(act, DEPTH, slot)

            @block.vector
            def _(v):
                def slot(i, parity):
                    for what in ORDER:
                        if what == NEXT:
                            if live(i, 4):
                                v.wait_ge(ready, i - 3 + 1)
                                wait(v, stored[parity], stores(i - 6, parity))
                                for b, (o, y) in enumerate(zip(group4(res[:, parity, :]), group4(X[:, i - 4, :]))):
                                    last = nc.vector.tensor_scalar(o, y, ln[:, parity, 0, b:b + 1], ln[:, parity, 3, b:b + 1],
                                                                   ALU.subtract, ALU.mult)
                                last.then_inc(written, 1)
                            if live(i, 0):
                                wait(v, prod[0], i)
                                wait(v, copied, i)
                                norm_group(nc, m, xs[:, :], X[:, i, :], i).then_inc(normed, 1)
                        elif what == LAST:
                            if live(i, 3):
                                v.wait_ge(last_prod, i - 2)
                                add_and_count(nc, v, X, ps[:, LAST_BANK, :], stats, i - 3, added, counted)
                        elif live(i, BEHIND[what[0]]) and not RELU[what[0]]:
                            s, k = what
                            v.wait_ge(hi[s], count(s, k, i - BEHIND[s]))
                            h_, l_ = pair(s, k)
                            take_lo(nc, l_, ps[:, BANK[s][k], :], h_).then_inc(lo[s], 1)
                slots(v, DEPTH, slot)

            @block.gpsimd
            def _(pool):
                nc.gpsimd.memset(power[:, :], -0.5).then_inc(ready, 1)

                def slot(i, parity):
                    if live(i, 3):
                        g, q = i - 3, (parity + 1) % 2
                        hold(pool, counted, g + 1, passed)
                        hold(pool, written, g - 1, passed)
                        group_stats(nc, pool, S, ln[:, q, :, :], g, halves, passed)
                        var, rstd_ = ln[:, q, 2, :], ln[:, q, 3, :]
                        hold(pool, halves[3], g + 1, passed)
                        nc.gpsimd.tensor_scalar(var, var, 1.0 / D, EPS_NORM, ALU.mult, ALU.add).then_inc(halves[4], 1)
                        hold(pool, halves[4], g + 1, passed)
                        nc.gpsimd.tensor_tensor(rstd_, var, power[:, :], ALU.pow).then_inc(ready, 1)
                slots(pool, DEPTH, slot)

            @block.sync
            def _(sp):
                def slot(i, parity):
                    if live(i, 4):
                        sp.wait_ge(written, i - 3)
                        sp.dma_start(outd[:, i - 4, :, :], res[:, parity, :].rearrange("p (b d) -> p b d", b=GB)
                                     ).then_inc(stored[parity], 16)
                slots(sp, DEPTH, slot)
                for u in range(2):
                    sp.wait_ge(stored[u], 16 * NG // 2)


def kernel(**inputs):
    import numpy as np
    import concourse.bacc as bacc
    from concourse import mybir as mb
    from concourse.bass_utils import run_bass_kernel_spmd

    a = {k: np.asarray(v) for k, v in inputs.items()}

    def tiles(w):
        return w.reshape(-1, 128, w.shape[1]).transpose(1, 0, 2).reshape(128, -1)

    wih, whh = a["L0_gnn_Wih"].transpose(0, 2, 1), a["L0_gnn_Whh"].transpose(0, 2, 1)
    lstm = np.stack([wih, whh], 1).transpose(2, 0, 1, 3).reshape(128, -1)
    cols = lambda v: v.reshape(-1, 128).T
    arrays = dict(
        x=a["x"], xt=a["x"].transpose(2, 0, 1).reshape(128, -1), adj=a["adj"],
        gnn_w=np.concatenate([a["L0_gnn_Wg0"], a["adj"].T, a["L0_gnn_Wg1"]], 1),
        lstm_w=lstm,
        whole_w=np.concatenate([a["L1_gnn_W1"].T, tiles(a["L1_gnn_W2"].T), a["L2_gnn_W_out"].T, tiles(a["L3_gnn_W3"])], 1),
        late_w=np.concatenate([a["L2_gnn_W_lin"].T, a["L2_gnn_W_val"].T, a["L3_gnn_W1"], tiles(a["L3_gnn_W2"])], 1),
        vecs=np.concatenate([cols(a[k]) for k in ("L0_gnn_bih", "L0_gnn_bhh", "L1_gnn_b1", "L1_gnn_g1", "L1_gnn_be1",
                                                  "L1_gnn_b2", "L1_gnn_g2", "L1_gnn_be2", "L2_gnn_a")], 1),
        bg0=a["L0_gnn_bg0"], bg1=a["L0_gnn_bg1"], src=a["L2_gnn_src"], dst=a["L2_gnn_dst"])
    nc = bacc.Bacc("TRN2", target_bir_lowering=False, num_devices=1)
    args, feed = [], {}
    for name, arr in arrays.items():
        arr = np.ascontiguousarray(arr)
        feed[f"in_{name}"] = arr
        args.append(nc.dram_tensor(f"in_{name}", arr.shape, mb.dt.from_np(arr.dtype), kind="ExternalInput").ap())
    args.append(nc.dram_tensor("out", (64, 128, 128), mb.dt.float32, kind="ExternalOutput").ap())
    build(nc, *args)
    r = run_bass_kernel_spmd(nc, [feed], core_ids=[0])
    return r.results[0]["out"]
```
